# Optimizing a Trainium2 kernel written in Bass

```python
import numpy as np
import jax
import jax.numpy as jnp

def _softmax(x, axis=-1):
    return jax.nn.softmax(x, axis=axis)

def _gelu(x):
    return jax.nn.gelu(x, approximate=True)

def _silu(x):
    return jax.nn.silu(x)

def _sigmoid(x):
    return jax.nn.sigmoid(x)

def _layernorm(x, axis=-1, eps=1e-05):
    m = jnp.mean(x, axis=axis, keepdims=True)
    v = jnp.var(x, axis=axis, keepdims=True)
    return (x - m) / jnp.sqrt(v + eps)

def _scatter_add(tgt, idx, src, axis=0):
    return tgt.at[idx].add(src)

def _segment_sum(src, seg, n):
    return jax.ops.segment_sum(src, seg, n)
kernel_name = 'mk_gnn_resnorm_d2_gnn_r8_b90cff'

def setup_inputs(seed: int=0):
    np.random.seed(seed)
    _w = jnp.asarray

    def _rec_inputs():
        import jax
        import jax.numpy as jnp
        _gk = jax.random.key(seed)
        x = -0.000202 + 1 * jax.random.normal(jax.random.fold_in(_gk, 1), (6250, 128), jnp.float32)
        _s = jax.random.randint(jax.random.fold_in(_gk, 2), (100000,), 0, 6250, jnp.int32)
        _d = jax.random.randint(jax.random.fold_in(_gk, 3), (100000,), 0, 6250, jnp.int32)
        _loop = jnp.arange(6250, dtype=jnp.int32)
        src = jnp.concatenate([_s, _d, _loop])
        dst = jnp.concatenate([_d, _s, _loop])
        _o = jnp.argsort(dst, stable=True)
        src = src[_o]
        dst = dst[_o]
        edge_attr_128 = -5.16925e-05 + 1.00005 * jax.random.normal(jax.random.fold_in(_gk, 13), (206250, 128), jnp.float32)
        edge_attr_4 = -0.000149047 + 1.00006 * jax.random.normal(jax.random.fold_in(_gk, 14), (206250, 4), jnp.float32)
        edge_attr_8 = jax.random.uniform(jax.random.fold_in(_gk, 15), (206250, 8), jnp.float32, 0.0, 0.999999)
        return (x, src, dst, edge_attr_128, edge_attr_4, edge_attr_8)
    x, src, dst, edge_attr_128, edge_attr_4, edge_attr_8 = _rec_inputs()

    def _L0_gnn_setup():
        import jax, jax.numpy as jnp
        import numpy as np
        N, E, D, H = (6250, 100000, 128, 8)
        O = D // H
        NEG_SLOPE = 0.2
        LN_EPS = 1e-05

        def layer_norm(x, g, b):
            mu = jnp.mean(x, axis=-1, keepdims=True)
            var = jnp.mean((x - mu) ** 2, axis=-1, keepdims=True)
            return (x - mu) * jax.lax.rsqrt(var + LN_EPS) * g + b

        def gatv2(x, edge_index, edge_attr, W_l, b_l, W_r, b_r, W_e, att, b_att):
            src, dst = (edge_index[0], edge_index[1])
            xl = (x @ W_l + b_l).reshape(-1, H, O)
            xr = (x @ W_r + b_r).reshape(-1, H, O)
            ee = (edge_attr @ W_e).reshape(-1, H, O)
            m = jax.nn.leaky_relu(xl[src] + xr[dst] + ee, NEG_SLOPE)
            logits = jnp.einsum('eho,ho->eh', m, att)
            lmax = jax.ops.segment_max(logits, dst, num_segments=N)
            exl = jnp.exp(logits - lmax[dst])
            denom = jax.ops.segment_sum(exl, dst, num_segments=N)
            alpha = exl / (denom[dst] + 1e-16)
            msg = xl[src] * alpha[:, :, None]
            out = jax.ops.segment_sum(msg, dst, num_segments=N)
            return out.reshape(-1, H * O) + b_att
        key = jax.random.key(seed)
        ks = jax.random.split(key, 20)
        s = 1.0 / np.sqrt(D)
        sf = 1.0 / np.sqrt(4 * D)
        return {'x': jax.random.normal(ks[0], (N, D), jnp.float32), 'edge_index': jax.random.randint(ks[1], (2, E), 0, N, jnp.int32), 'edge_attr': jax.random.normal(ks[2], (E, D), jnp.float32), 'batch': jnp.zeros((N,), jnp.int32), 'W_l': jax.random.normal(ks[3], (D, H * O), jnp.float32) * s, 'b_l': jnp.zeros((H * O,), jnp.float32), 'W_r': jax.random.normal(ks[4], (D, H * O), jnp.float32) * s, 'b_r': jnp.zeros((H * O,), jnp.float32), 'W_e': jax.random.normal(ks[5], (D, H * O), jnp.float32) * s, 'att': jax.random.normal(ks[6], (H, O), jnp.float32) * (1.0 / np.sqrt(O)), 'b_att': jnp.zeros((H * O,), jnp.float32), 'W1': jax.random.normal(ks[7], (D, 4 * D), jnp.float32) * s, 'b1': jnp.zeros((4 * D,), jnp.float32), 'W2': jax.random.normal(ks[8], (4 * D, D), jnp.float32) * sf, 'b2': jnp.zeros((D,), jnp.float32), 'g1': jnp.ones((D,), jnp.float32), 'be1': jnp.zeros((D,), jnp.float32), 'g2': jnp.ones((D,), jnp.float32), 'be2': jnp.zeros((D,), jnp.float32)}
    _L0_gnn_all = _L0_gnn_setup()
    _L0_gnn_in = {k: v for k, v in _L0_gnn_all.items() if k in ('W_l', 'b_l', 'W_r', 'b_r', 'W_e', 'att', 'b_att', 'W1', 'b1', 'W2', 'b2', 'g1', 'be1', 'g2', 'be2')}
    del _L0_gnn_all

    def _L1_gnn_setup():
        import jax, jax.numpy as jnp
        import numpy as np
        N_NODES = 1250
        N_EDGES = 40000
        MUL = 32
        RADIAL = 8
        HID = 64
        NUM_NEIGHBORS = 32.0
        MIX = np.pi / 8.0
        INV_SQRT2 = 1.0 / np.sqrt(2.0)
        INV_SQRT3 = 1.0 / np.sqrt(3.0)

        def _forward(node_input, edge_attr, edge_scalar_attr, W1_0e, W1_1o, W_mlp1, W_mlp2, Wp_00, Wp_01, Wp_10, Wp_11, W2_0e, W2_1o, edge_src, edge_dst):
            N = node_input.shape[0]
            x0 = node_input[:, :MUL]
            x1 = node_input[:, MUL:].reshape(N, MUL, 3)
            f0 = x0 @ W1_0e / np.sqrt(MUL)
            f1 = jnp.einsum('nui,uw->nwi', x1, W1_1o) / np.sqrt(MUL)
            feat0, self0 = (f0[:, :MUL], f0[:, MUL:])
            feat1, self1 = (f1[:, :MUL], f1[:, MUL:])
            e0 = feat0[edge_src]
            e1 = feat1[edge_src]
            ea0 = edge_attr[:, :1]
            ea1 = edge_attr[:, 1:4]
            h = jax.nn.gelu(edge_scalar_attr @ W_mlp1 / np.sqrt(RADIAL))
            h = jax.nn.gelu(h @ W_mlp2 / np.sqrt(HID))
            w00 = h @ Wp_00
            w01 = h @ Wp_01
            w10 = h @ Wp_10
            w11 = h @ Wp_11
            out0_a = w00 * e0 * ea0
            out0_b = w11 * jnp.sum(e1 * ea1[:, None, :], -1) * INV_SQRT3
            out1_a = (w01 * e0)[:, :, None] * ea1[:, None, :]
            out1_b = w10[:, :, None] * e1 * ea0[:, :, None]
            mid0 = jnp.concatenate([out0_a, out0_b], axis=1) * INV_SQRT2
            mid1 = jnp.concatenate([out1_a, out1_b], axis=1) * INV_SQRT2
            n0 = jax.ops.segment_sum(mid0, edge_dst, num_segments=N) / np.sqrt(NUM_NEIGHBORS)
            n1 = jax.ops.segment_sum(mid1, edge_dst, num_segments=N) / np.sqrt(NUM_NEIGHBORS)
            conv0 = n0 @ W2_0e / np.sqrt(2 * MUL)
            conv1 = jnp.einsum('nui,uw->nwi', n1, W2_1o) / np.sqrt(2 * MUL)
            c, s = (np.cos(MIX), np.sin(MIX))
            y0 = c * self0 + s * conv0
            y1 = c * self1 + s * conv1
            return jnp.concatenate([y0, y1.reshape(N, MUL * 3)], axis=1)
        key = jax.random.key(seed)
        ks = jax.random.split(key, 16)
        inp = {'node_input': jax.random.normal(ks[0], (N_NODES, 4 * MUL), jnp.float32), 'edge_attr': jax.random.normal(ks[1], (N_EDGES, 4), jnp.float32), 'edge_scalar_attr': jax.random.uniform(ks[2], (N_EDGES, RADIAL), jnp.float32), 'W1_0e': jax.random.normal(ks[3], (MUL, 2 * MUL), jnp.float32), 'W1_1o': jax.random.normal(ks[4], (MUL, 2 * MUL), jnp.float32), 'W_mlp1': jax.random.normal(ks[5], (RADIAL, HID), jnp.float32), 'W_mlp2': jax.random.normal(ks[6], (HID, HID), jnp.float32), 'Wp_00': jax.random.normal(ks[7], (HID, MUL), jnp.float32), 'Wp_01': jax.random.normal(ks[8], (HID, MUL), jnp.float32), 'Wp_10': jax.random.normal(ks[9], (HID, MUL), jnp.float32), 'Wp_11': jax.random.normal(ks[10], (HID, MUL), jnp.float32), 'W2_0e': jax.random.normal(ks[11], (2 * MUL, MUL), jnp.float32), 'W2_1o': jax.random.normal(ks[12], (2 * MUL, MUL), jnp.float32), 'edge_src': jax.random.randint(ks[13], (N_EDGES,), 0, N_NODES, jnp.int32), 'edge_dst': jax.random.randint(ks[14], (N_EDGES,), 0, N_NODES, jnp.int32)}
        return inp
    _L1_gnn_all = _L1_gnn_setup()
    _L1_gnn_in = {k: v for k, v in _L1_gnn_all.items() if k in ('W1_0e', 'W1_1o', 'W_mlp1', 'W_mlp2', 'Wp_00', 'Wp_01', 'Wp_10', 'Wp_11', 'W2_0e', 'W2_1o')}
    del _L1_gnn_all
    return {'x': x, 'src': src, 'dst': dst, 'edge_attr_128': edge_attr_128, 'edge_attr_4': edge_attr_4, 'edge_attr_8': edge_attr_8, 'L0_gnn_W_l': _L0_gnn_in['W_l'], 'L0_gnn_b_l': _L0_gnn_in['b_l'], 'L0_gnn_W_r': _L0_gnn_in['W_r'], 'L0_gnn_b_r': _L0_gnn_in['b_r'], 'L0_gnn_W_e': _L0_gnn_in['W_e'], 'L0_gnn_att': _L0_gnn_in['att'], 'L0_gnn_b_att': _L0_gnn_in['b_att'], 'L0_gnn_W1': _L0_gnn_in['W1'], 'L0_gnn_b1': _L0_gnn_in['b1'], 'L0_gnn_W2': _L0_gnn_in['W2'], 'L0_gnn_b2': _L0_gnn_in['b2'], 'L0_gnn_g1': _L0_gnn_in['g1'], 'L0_gnn_be1': _L0_gnn_in['be1'], 'L0_gnn_g2': _L0_gnn_in['g2'], 'L0_gnn_be2': _L0_gnn_in['be2'], 'L1_gnn_W1_0e': _L1_gnn_in['W1_0e'], 'L1_gnn_W1_1o': _L1_gnn_in['W1_1o'], 'L1_gnn_W_mlp1': _L1_gnn_in['W_mlp1'], 'L1_gnn_W_mlp2': _L1_gnn_in['W_mlp2'], 'L1_gnn_Wp_00': _L1_gnn_in['Wp_00'], 'L1_gnn_Wp_01': _L1_gnn_in['Wp_01'], 'L1_gnn_Wp_10': _L1_gnn_in['Wp_10'], 'L1_gnn_Wp_11': _L1_gnn_in['Wp_11'], 'L1_gnn_W2_0e': _L1_gnn_in['W2_0e'], 'L1_gnn_W2_1o': _L1_gnn_in['W2_1o']}

def reference(x, src, dst, edge_attr_128, edge_attr_4, edge_attr_8, L0_gnn_W_l, L0_gnn_b_l, L0_gnn_W_r, L0_gnn_b_r, L0_gnn_W_e, L0_gnn_att, L0_gnn_b_att, L0_gnn_W1, L0_gnn_b1, L0_gnn_W2, L0_gnn_b2, L0_gnn_g1, L0_gnn_be1, L0_gnn_g2, L0_gnn_be2, L1_gnn_W1_0e, L1_gnn_W1_1o, L1_gnn_W_mlp1, L1_gnn_W_mlp2, L1_gnn_Wp_00, L1_gnn_Wp_01, L1_gnn_Wp_10, L1_gnn_Wp_11, L1_gnn_W2_0e, L1_gnn_W2_1o):
    import jax
    import jax.numpy as jnp

    def _L0_gnn_ref(x, edge_index, edge_attr, batch, W_l, b_l, W_r, b_r, W_e, att, b_att, W1, b1, W2, b2, g1, be1, g2, be2):
        import jax, jax.numpy as jnp
        import numpy as np
        N, E, D, H = (6250, 100000, 128, 8)
        O = D // H
        NEG_SLOPE = 0.2
        LN_EPS = 1e-05

        def layer_norm(x, g, b):
            mu = jnp.mean(x, axis=-1, keepdims=True)
            var = jnp.mean((x - mu) ** 2, axis=-1, keepdims=True)
            return (x - mu) * jax.lax.rsqrt(var + LN_EPS) * g + b

        def gatv2(x, edge_index, edge_attr, W_l, b_l, W_r, b_r, W_e, att, b_att):
            src, dst = (edge_index[0], edge_index[1])
            xl = (x @ W_l + b_l).reshape(-1, H, O)
            xr = (x @ W_r + b_r).reshape(-1, H, O)
            ee = (edge_attr @ W_e).reshape(-1, H, O)
            m = jax.nn.leaky_relu(xl[src] + xr[dst] + ee, NEG_SLOPE)
            logits = jnp.einsum('eho,ho->eh', m, att)
            lmax = jax.ops.segment_max(logits, dst, num_segments=N)
            exl = jnp.exp(logits - lmax[dst])
            denom = jax.ops.segment_sum(exl, dst, num_segments=N)
            alpha = exl / (denom[dst] + 1e-16)
            msg = xl[src] * alpha[:, :, None]
            out = jax.ops.segment_sum(msg, dst, num_segments=N)
            return out.reshape(-1, H * O) + b_att
        attn_out = gatv2(x, edge_index, edge_attr, W_l, b_l, W_r, b_r, W_e, att, b_att)
        h = layer_norm(x + attn_out, g1, be1)
        ffn = jax.nn.gelu(h @ W1 + b1, approximate=False) @ W2 + b2
        return layer_norm(h + ffn, g2, be2)

    def _L1_gnn_ref(node_input, edge_attr, edge_scalar_attr, W1_0e, W1_1o, W_mlp1, W_mlp2, Wp_00, Wp_01, Wp_10, Wp_11, W2_0e, W2_1o, edge_src, edge_dst):
        import jax, jax.numpy as jnp
        import numpy as np
        N_NODES = 1250
        N_EDGES = 40000
        MUL = 32
        RADIAL = 8
        HID = 64
        NUM_NEIGHBORS = 32.0
        MIX = np.pi / 8.0
        INV_SQRT2 = 1.0 / np.sqrt(2.0)
        INV_SQRT3 = 1.0 / np.sqrt(3.0)

        def _forward(node_input, edge_attr, edge_scalar_attr, W1_0e, W1_1o, W_mlp1, W_mlp2, Wp_00, Wp_01, Wp_10, Wp_11, W2_0e, W2_1o, edge_src, edge_dst):
            N = node_input.shape[0]
            x0 = node_input[:, :MUL]
            x1 = node_input[:, MUL:].reshape(N, MUL, 3)
            f0 = x0 @ W1_0e / np.sqrt(MUL)
            f1 = jnp.einsum('nui,uw->nwi', x1, W1_1o) / np.sqrt(MUL)
            feat0, self0 = (f0[:, :MUL], f0[:, MUL:])
            feat1, self1 = (f1[:, :MUL], f1[:, MUL:])
            e0 = feat0[edge_src]
            e1 = feat1[edge_src]
            ea0 = edge_attr[:, :1]
            ea1 = edge_attr[:, 1:4]
            h = jax.nn.gelu(edge_scalar_attr @ W_mlp1 / np.sqrt(RADIAL))
            h = jax.nn.gelu(h @ W_mlp2 / np.sqrt(HID))
            w00 = h @ Wp_00
            w01 = h @ Wp_01
            w10 = h @ Wp_10
            w11 = h @ Wp_11
            out0_a = w00 * e0 * ea0
            out0_b = w11 * jnp.sum(e1 * ea1[:, None, :], -1) * INV_SQRT3
            out1_a = (w01 * e0)[:, :, None] * ea1[:, None, :]
            out1_b = w10[:, :, None] * e1 * ea0[:, :, None]
            mid0 = jnp.concatenate([out0_a, out0_b], axis=1) * INV_SQRT2
            mid1 = jnp.concatenate([out1_a, out1_b], axis=1) * INV_SQRT2
            n0 = jax.ops.segment_sum(mid0, edge_dst, num_segments=N) / np.sqrt(NUM_NEIGHBORS)
            n1 = jax.ops.segment_sum(mid1, edge_dst, num_segments=N) / np.sqrt(NUM_NEIGHBORS)
            conv0 = n0 @ W2_0e / np.sqrt(2 * MUL)
            conv1 = jnp.einsum('nui,uw->nwi', n1, W2_1o) / np.sqrt(2 * MUL)
            c, s = (np.cos(MIX), np.sin(MIX))
            y0 = c * self0 + s * conv0
            y1 = c * self1 + s * conv1
            return jnp.concatenate([y0, y1.reshape(N, MUL * 3)], axis=1)
        return _forward(node_input, edge_attr, edge_scalar_attr, W1_0e, W1_1o, W_mlp1, W_mlp2, Wp_00, Wp_01, Wp_10, Wp_11, W2_0e, W2_1o, edge_src, edge_dst)
    edge_index = jnp.stack([src, dst])
    batch0 = jnp.zeros((6250,), jnp.int32)
    x = _layernorm(x + _L0_gnn_ref(x, edge_index, edge_attr_128, batch0, L0_gnn_W_l, L0_gnn_b_l, L0_gnn_W_r, L0_gnn_b_r, L0_gnn_W_e, L0_gnn_att, L0_gnn_b_att, L0_gnn_W1, L0_gnn_b1, L0_gnn_W2, L0_gnn_b2, L0_gnn_g1, L0_gnn_be1, L0_gnn_g2, L0_gnn_be2), axis=-1)
    x = _layernorm(x + _L1_gnn_ref(x, edge_attr_4, edge_attr_8, L1_gnn_W1_0e, L1_gnn_W1_1o, L1_gnn_W_mlp1, L1_gnn_W_mlp2, L1_gnn_Wp_00, L1_gnn_Wp_01, L1_gnn_Wp_10, L1_gnn_Wp_11, L1_gnn_W2_0e, L1_gnn_W2_1o, src, dst), axis=-1)
    return x

_drawn_inputs = setup_inputs


def setup_inputs(seed=0):
    import zlib

    import numpy as np

    out = dict(_drawn_inputs(seed))
    spreads = {'L0_gnn_b_l': (0.0, 0.1),
     'L0_gnn_b_r': (0.0, 0.8),
     'L0_gnn_b_att': (0.0, 0.1),
     'L0_gnn_b1': (0.0, 0.281),
     'L0_gnn_b2': (0.0, 0.1),
     'L0_gnn_g1': (1.0, 0.2),
     'L0_gnn_be1': (0.0, 0.1),
     'L0_gnn_g2': (1.0, 0.2),
     'L0_gnn_be2': (0.0, 0.1)}
    factors = {}
    for name, (base, spread) in spreads.items():
        noise = np.random.default_rng([zlib.crc32(name.encode()), seed]).standard_normal(out[name].shape)
        drawn = base * np.exp(spread * noise) if base else spread * noise
        out[name] = jnp.asarray(drawn.astype(out[name].dtype))
    for name, factor in factors.items():
        out[name] = (out[name] * factor).astype(out[name].dtype)
    return out
```

```python
import numpy as np
import concourse.bass as bass
from concourse import mybir

F32 = mybir.dt.float32
I32 = mybir.dt.int32
ALU = mybir.AluOpType
ACT = mybir.ActivationFunctionType

P = 128
N, E, D, H = 6250, 206250, 128, 8
O = D // H
FF = 4 * D
FC = FF // P
MUL, RADIAL, HID = 32, 8, 64
TG = 4
GE = TG * P
G = -(-E // GE)
T = G * TG
E_PAD = G * GE
NB = 4
BATCHES = -(-(N + P) // (NB * P))
N_PAD = BATCHES * NB * P
W = P
U = 8
PEEL = G % U + U
BIG = 1e30
LN_EPS = 1e-5
MIX_C, MIX_S = float(np.cos(np.pi / 8)), float(np.sin(np.pi / 8))
SELF_SCALE = MIX_C / float(np.sqrt(MUL))
FEAT_SCALE = 1.0 / float(np.sqrt(MUL))
CONV_SCALE = MIX_S / float(np.sqrt(2 * MUL) * np.sqrt(32.0) * np.sqrt(2.0))
CONV_SCALE_B = CONV_SCALE / float(np.sqrt(3.0))


class Step:

    def __init__(self, at, i=0, stride=U):
        self.at, self.i, self.stride = at, i, stride

    def back(self, n):
        return Step(self.at - n, self.i, self.stride)

    def index(self, scale=1, plus=0):
        base = self.at * scale + plus
        return base if isinstance(self.i, int) else self.i * (self.stride * scale) + base

    def uses(self, n=1, by=1):
        base = (self.at // n + 1) * by
        return base if isinstance(self.i, int) else self.i * (self.stride // n * by) + base

    def slot(self, n):
        return self.at % n


def at_least(eng, sem, value):
    if not isinstance(value, int) or value > 0:
        eng.wait_ge(sem, value)


def steps(eng, total, peel, unroll, tail, body):
    for k in range(peel):
        body(Step(k, 0, unroll), lambda lag, k=k: 0 <= k - lag < total)
    with eng.Fori(0, (total - peel) // unroll) as i:
        for u in range(unroll):
            body(Step(peel + u, i, unroll), lambda lag: True)
    for k in range(total, total + tail):
        body(Step(k, 0, unroll), lambda lag, k=k: 0 <= k - lag < total)


def bc(ap, axis, n):
    ap = ap.unsqueeze(axis)
    shape = list(ap.shape)
    shape[axis] = n
    return ap.broadcast_to(shape)


def constants(nc, sb, q, out):
    with (nc.semaphore("consts_loaded") as consts_loaded, nc.semaphore("zeroed") as zeroed,
          nc.semaphore("blocks_loaded") as blocks_loaded, nc.semaphore("masks") as masks,
          nc.semaphore("limits_loaded") as limits_loaded, nc.semaphore("limits_ready") as limits_ready,
          nc.semaphore("limits_stored") as limits_stored, nc.semaphore("chain") as chain,
          nc.sbuf_tensor("dst_here", [P, T], I32) as dst_here, nc.sbuf_tensor("dst_before", [P, T], I32) as dst_before,
          nc.sbuf_tensor("dst_tiles", [P, T], I32) as dst_tiles, nc.sbuf_tensor("base_all", [P, T], I32) as base_all,
          nc.sbuf_tensor("limit_sb", [P, T], F32) as limit_sb, nc.sbuf_tensor("last_limit", [1, 1], F32) as last_limit,
          nc.sbuf_tensor("iota_i", [P, W], I32) as iota_i, nc.sbuf_tensor("att_col", [P, 1], F32) as att_col,
          nc.Block() as block):
        loads = []

        def row(t, name, n):
            loads.append((t, q[name].rearrange("(a n) -> a n", a=1).partition_broadcast(P).rearrange("p a n -> p (a n)")))

        loads.append((dst_here[:, :], q["dst_line"][1:1 + E_PAD].rearrange("(p t) -> p t", p=P)))
        loads.append((dst_before[:, :], q["dst_line"][0:E_PAD].rearrange("(p t) -> p t", p=P)))
        loads.append((dst_tiles[:, :], q["dst_tiles"]))
        loads.append((base_all[:, :], q["dst_tiles"][0:1, :].partition_broadcast(P).rearrange("p a n -> p (a n)")))
        loads.append((sb["tile_base"][:, :], q["dst_tiles"][0:1, :]))
        loads.append((att_col[:, :], q["L0_gnn_att"].rearrange("h o -> (h o)").rearrange("(p a) -> p a", a=1)))
        loads.append((sb["b_att"][:, :], q["L0_gnn_b_att"].rearrange("(p a) -> p a", a=1)))
        loads.append((sb["W_lr"][:, 0:D], q["L0_gnn_W_l"]))
        loads.append((sb["W_lr"][:, D:2 * D], q["L0_gnn_W_r"]))
        loads.append((sb["W_e"][:, :], q["L0_gnn_W_e"]))
        loads.append((sb["W1"][:, :], q["L0_gnn_W1"]))
        loads.append((sb["W2"][:, :, :], q["L0_gnn_W2"].rearrange("(c p) n -> p c n", p=P)))
        loads.append((sb["b1"][:, :], q["b1_columns"]))
        loads.append((sb["xT"][:, :], q["xT"]))
        row(sb["b_lr"][:, 0:D], "L0_gnn_b_l", D)
        row(sb["b_lr"][:, D:2 * D], "L0_gnn_b_r", D)
        for name in ("b2", "g1", "be1", "g2", "be2"):
            row(sb[name][:, :], "L0_gnn_" + name, D)
        blocks = []
        for half in range(2):
            blocks.append((sb["mlp1"][half * RADIAL:(half + 1) * RADIAL, half * HID:(half + 1) * HID], q["L1_gnn_W_mlp1"]))
            blocks.append((sb["mlp2"][half * HID:(half + 1) * HID, half * HID:(half + 1) * HID], q["L1_gnn_W_mlp2"]))
            for c, name in enumerate(("Wp_00", "Wp_10", "Wp_01", "Wp_11")):
                blocks.append((sb["Wp"][half * HID:(half + 1) * HID, half, c * MUL:(c + 1) * MUL], q["L1_gnn_" + name]))
        blocks.append((sb["W_feat"][0:MUL, 0:MUL], q["L1_gnn_W1_0e"][:, 0:MUL]))
        blocks.append((sb["W_feat"][0:MUL, D:D + MUL], q["L1_gnn_W1_0e"][:, MUL:2 * MUL]))
        blocks.append((sb["W_convA"][0:MUL, 0:MUL], q["L1_gnn_W2_0e"][0:MUL, :]))
        blocks.append((sb["W_convB"][3 * MUL:4 * MUL, 0:MUL], q["L1_gnn_W2_0e"][MUL:2 * MUL, :]))
        for c in range(3):
            lo = MUL * (c + 1)
            blocks.append((sb["W_feat"][MUL + c:D:3, lo:lo + MUL], q["L1_gnn_W1_1o"][:, 0:MUL]))
            blocks.append((sb["W_feat"][MUL + c:D:3, D + MUL + c:2 * D:3], q["L1_gnn_W1_1o"][:, MUL:2 * MUL]))
            blocks.append((sb["W_convA"][lo:lo + MUL, MUL + c:D:3], q["L1_gnn_W2_1o"][MUL:2 * MUL, :]))
            blocks.append((sb["W_convB"][MUL * c:MUL * (c + 1), MUL + c:D:3], q["L1_gnn_W2_1o"][0:MUL, :]))

        @block.sync
        def _(sp):
            for to, of in loads:
                sp.dma_start(to, of).then_inc(consts_loaded, 16)
            sp.wait_ge(limits_ready, 2)
            sp.dma_start(q["limit"][0:E_PAD].rearrange("(p t) -> p t", p=P), limit_sb[:, :]).then_inc(limits_stored, 16)
            sp.dma_start(q["limit"][E_PAD:E_PAD + 1].rearrange("(a n) -> a n", a=1), last_limit[:, :]).then_inc(limits_stored, 16)
            sp.wait_ge(limits_stored, 32)

        @block.scalar
        def _(act):
            act.wait_ge(zeroed, 6)
            with nc.allow_non_contiguous_dma(reason="small weights, once"):
                for to, of in blocks:
                    act.dma_start(to, of).then_inc(blocks_loaded, 16)

        @block.gpsimd
        def _(pool):
            pool.memset(sb["ident"][:, :], 0.0).then_inc(masks, 1)
            pool.memset(sb["att_block"][:, :], 1.0).then_inc(masks, 1)
            pool.memset(sb["head_rows"][:, :], 1.0).then_inc(masks, 1)
            pool.iota(iota_i[:, :], pattern=[[1, W]], base=0, channel_multiplier=0).then_inc(masks, 1)
            pool.wait_ge(masks, 4)
            pool.affine_select(out=sb["ident"][:, :], in_=sb["ident"][:, :], compare_op=ALU.not_equal, fill=1.0,
                               base=0, pattern=[[-1, P]], channel_multiplier=1).then_inc(masks, 1)
            pool.affine_select(out=sb["att_block"][:, :], in_=sb["att_block"][:, :], compare_op=ALU.is_ge, fill=0.0,
                               base=0, pattern=[[-O, H]], channel_multiplier=1).then_inc(masks, 1)
            pool.affine_select(out=sb["head_rows"][:, :], in_=sb["head_rows"][:, :], compare_op=ALU.is_ge, fill=0.0,
                               base=0, pattern=[[1, D]], channel_multiplier=-O).then_inc(masks, 1)
            pool.wait_ge(masks, 7)
            pool.affine_select(out=sb["att_block"][:, :], in_=sb["att_block"][:, :], compare_op=ALU.is_ge, fill=0.0,
                               base=O - 1, pattern=[[O, H]], channel_multiplier=-1).then_inc(masks, 1)
            pool.affine_select(out=sb["head_rows"][:, :], in_=sb["head_rows"][:, :], compare_op=ALU.is_ge, fill=0.0,
                               base=O - 1, pattern=[[-1, D]], channel_multiplier=O).then_inc(masks, 1)

        @block.vector
        def _(dve):
            for name in ("mlp1", "mlp2", "W_feat", "W_convA", "W_convB"):
                dve.memset(sb[name][:, :], 0.0).then_inc(zeroed, 1)
            dve.memset(sb["Wp"][:, :, :], 0.0).then_inc(zeroed, 1)
            dve.memset(last_limit[:, :], -BIG).then_inc(limits_ready, 1)
            dve.memset(sb["minus_half"][:, :], -0.5)
            dve.memset(sb["acc"][:, :, :], 0.0)
            dve.wait_ge(masks, 9)
            dve.tensor_copy(sb["iota"][:, :], iota_i[:, :])
            dve.tensor_scalar(sb["minus_ident8"][:, :], sb["ident"][0:H, 0:H], -1.0, None, ALU.mult)
            dve.wait_ge(consts_loaded, 16 * len(loads))
            dve.tensor_scalar(sb["att_block"][:, :], sb["att_block"][:, :], att_col[:, :], None, ALU.mult)
            dve.tensor_tensor(limit_sb[:, :], dst_here[:, :], dst_before[:, :], ALU.is_equal).then_inc(chain, 1)
            dve.wait_ge(chain, 1)
            dve.tensor_scalar(limit_sb[:, :], limit_sb[:, :], 2 * BIG, -BIG, ALU.mult, ALU.add).then_inc(limits_ready, 1)
            dve.tensor_tensor(sb["dst_rel"][:, :], dst_tiles[:, :], base_all[:, :], ALU.subtract)
            dve.wait_ge(blocks_loaded, 16 * len(blocks))
            dve.tensor_scalar(sb["W_convA"][:, :], sb["W_convA"][:, :], CONV_SCALE, None, ALU.mult)
            dve.tensor_scalar(sb["W_convB"][0:3 * MUL, :], sb["W_convB"][0:3 * MUL, :], CONV_SCALE, None, ALU.mult)
            dve.tensor_scalar(sb["W_convB"][3 * MUL:P, :], sb["W_convB"][3 * MUL:P, :], CONV_SCALE_B, None, ALU.mult)


def project_nodes(nc, sb, q, out):
    with (nc.sbuf_tensor("rows", [P, 2, NB, 2 * D], F32) as rows, nc.psum_tensor("proj", [P, 2, NB, 2 * D], F32) as proj,
          nc.semaphore("projected") as projected, nc.semaphore("rows_ready") as rows_ready,
          nc.semaphore("rows_stored0") as st0, nc.semaphore("rows_stored1") as st1, nc.Block() as block):
        rows_stored = [st0, st1]
        PL = BATCHES % 2 + 2

        def nodes(table, k):
            return q[table][bass.ds(k.index(NB * P), NB * P), :].rearrange("(t p) f -> p t f", p=P)

        @block.tensor
        def _(pe):
            def body(k, live):
                if not live(0):
                    return
                at_least(pe, rows_ready, k.back(2).uses())
                for t in range(NB):
                    last = nc.tensor.matmul(proj[:, k.slot(2), t, :], sb["xT"][:, (k.at * NB + t) * P:(k.at * NB + t + 1) * P], sb["W_lr"][:, :], start=True, stop=True)
                last.then_inc(projected, 1)
            for n in range(BATCHES):
                body(Step(n), lambda lag: True)

        @block.vector
        def _(dve):
            def body(k, live):
                if not live(0):
                    return
                dve.wait_ge(projected, k.uses())
                at_least(dve, rows_stored[k.slot(2)], k.back(2).uses(2, 32))
                dve.tensor_tensor(rows[:, k.slot(2), :, :], proj[:, k.slot(2), :, :], bc(sb["b_lr"][:, :], 1, NB), ALU.add).then_inc(rows_ready, 1)
            steps(dve, BATCHES, PL, 2, 0, body)

        @block.sync
        def _(sp):
            def body(k, live):
                if not live(0):
                    return
                sp.wait_ge(rows_ready, k.uses())
                sp.dma_start(nodes("xl", k), rows[:, k.slot(2), :, 0:D]).then_inc(rows_stored[k.slot(2)], 16)
                sp.dma_start(nodes("xr", k), rows[:, k.slot(2), :, D:2 * D]).then_inc(rows_stored[k.slot(2)], 16)
            steps(sp, BATCHES, PL, 2, 0, body)
            for b in range(2):
                sp.wait_ge(rows_stored[b], Step(BATCHES - 2 + (BATCHES - b) % 2).uses(2, 32))


def attention(nc, sb, q, out):
    from contextlib import ExitStack
    with ExitStack() as ctx:
        def tile(name, shape, dt=F32):
            return ctx.enter_context(nc.sbuf_tensor("attn_" + name, shape, dt))

        def bank(name, shape):
            return ctx.enter_context(nc.psum_tensor("attn_" + name, shape, F32))

        def sem(name):
            return ctx.enter_context(nc.semaphore("attn_" + name))

        NX, NI, NS = 8, 4, 8
        idx = [tile(f"idx{b}", [P, TG], I32) for b in range(NI)]
        xl_rows = tile("xl_rows", [P, NX, TG, D])
        attrT = tile("attrT", [P, 4, GE])
        xr_win = tile("xr_win", [W, 4, TG, D])
        limit = tile("limit_rows", [H, 4, GE + 1])
        onehot = tile("onehot", [P, NS, TG, W])
        onehotT = tile("onehotT", [W, 2, GE])
        fifth = tile("fifth", [P, 2, GE])
        leaky = tile("leaky", [P, 2, GE])
        logitT = tile("logitT", [H, 2, GE])
        prefix = tile("prefix", [H, 2, GE])
        peak = tile("peak", [H, 2, GE])
        drop = tile("drop", [H, 2, 1])
        expd = tile("expd", [P, 2, TG, D])
        factor = tile("factor", [P, 2, 1])
        msg = tile("msg", [P, 2, TG, D])
        onehotT_ps = bank("onehotT_ps", [W, GE])
        pre_ps = bank("pre_ps", [P, 2, GE])
        logit_ps = bank("logit_ps", [H, GE])
        shift_ps = bank("shift_ps", [P, GE])
        sums_ps = bank("sums_ps", [P, 2, GE])

        idx_loaded = [sem(f"idx_loaded{b}") for b in range(NI)]
        attr_loaded = [sem(f"attr_loaded{b}") for b in range(4)]
        xr_loaded = [sem(f"xr_loaded{b}") for b in range(4)]
        limit_loaded = [sem(f"limit_loaded{b}") for b in range(4)]
        rows_gathered = [sem(f"rows_gathered{b}") for b in range(NX)]
        pool_turn = sem("pool_turn")
        onehot_ready, onehotT_ready, onehotT_copied = sem("onehot_ready"), sem("onehotT_ready"), sem("onehotT_copied")
        pre_ready, fifth_ready, leaky_ready = sem("pre_ready"), sem("fifth_ready"), sem("leaky_ready")
        logit_ready, logit_copied = sem("logit_ready"), sem("logit_copied")
        prefix_ready, peak_ready, drop_ready = sem("prefix_ready"), sem("peak_ready"), sem("drop_ready")
        shift_ready, exp_ready, msg_ready = sem("shift_ready"), sem("exp_ready"), sem("msg_ready")
        sums_ready, acc_steps = sem("sums_ready"), sem("acc_steps")
        ACC_STEPS = 1 + TG
        TAIL = 5
        block = ctx.enter_context(nc.Block())
        tile_base, dst_rel, acc = sb["tile_base"], sb["dst_rel"], sb["acc"]

        @block.sync
        def _(sp):
            def body(k, live):
                if not live(0):
                    return
                b = k.slot(4)
                at_least(sp, rows_gathered[k.back(NI).slot(NX)], k.back(NI).uses(NX, 16 * TG))
                sp.dma_start(idx[k.slot(NI)][:, :], q["src_tiles"][:, bass.ds(k.index(TG), TG)]).then_inc(idx_loaded[k.slot(NI)], 16)
                at_least(sp, pre_ready, k.back(4).uses())
                sp.dma_start(attrT[:, b, :], q["attrT"][:, bass.ds(k.index(GE), GE)]).then_inc(attr_loaded[b], 16)
                for t in range(TG):
                    base = sp.value_load(tile_base[0:1, bass.ds(k.index(TG, t), 1)], min_val=0, max_val=N)
                    sp.dma_start(xr_win[:, b, t, :], q["xr"][bass.ds(base, W), :]).then_inc(xr_loaded[b], 16)
                at_least(sp, peak_ready, k.back(4).uses())
                sp.dma_start(limit[:, b, :], q["limit"][bass.ds(k.index(GE), GE + 1)].rearrange("(a n) -> a n", a=1)
                             .partition_broadcast(H).rearrange("p a n -> p (a n)")).then_inc(limit_loaded[b], 16)
            steps(sp, G, PEEL, U, 0, body)

        @block.gpsimd
        def _(pool):
            def body(k, live):
                if not live(0):
                    return
                pool.wait_ge(idx_loaded[k.slot(NI)], k.uses(NI, 16))
                pool.sem_inc(pool_turn, 1)
                if not isinstance(k.i, int) or k.at >= NX:
                    pool.wait_ge(msg_ready, k.back(NX).uses())
                    pool.sem_inc(pool_turn, 1)
                for t in range(TG):
                    pool.indirect_dma_start(xl_rows[:, k.slot(NX), t, :], None, q["xl"][:, :],
                                            bass.IndirectOffsetOnAxis(ap=idx[k.slot(NI)][:, t:t + 1], axis=0)
                                            ).then_inc(rows_gathered[k.slot(NX)], 16)
            steps(pool, G, PEEL, U, 0, body)

        @block.tensor
        def _(pe):
            ident = sb["ident"]

            def body(k, live):
                if live(5):
                    g = k.back(5)
                    pe.wait_ge(msg_ready, g.uses())
                    at_least(pe, acc_steps, g.back(1).uses(1, ACC_STEPS))
                    for t in range(TG):
                        cols = slice(t * W, (t + 1) * W)
                        nc.tensor.matmul(sums_ps[:, 0, cols], msg[:, g.slot(2), t, :], onehot[:, g.slot(NS), t, :], start=True, stop=True)
                        last = nc.tensor.matmul(sums_ps[:, 1, cols], expd[:, g.slot(2), t, :], onehot[:, g.slot(NS), t, :], start=True, stop=True)
                    last.then_inc(sums_ready, 1)
                if live(4):
                    g = k.back(4)
                    pe.wait_ge(drop_ready, g.uses())
                    pe.wait_ge(logit_copied, g.uses())
                    at_least(pe, exp_ready, g.back(1).uses(1, 2))
                    for t in range(TG):
                        cols = slice(t * P, (t + 1) * P)
                        nc.tensor.matmul(shift_ps[:, t * H:(t + 1) * H], logitT[:, g.slot(2), cols], ident[0:H, 0:H], start=True, stop=False)
                        nc.tensor.matmul(shift_ps[:, t * H:(t + 1) * H], peak[:, g.slot(2), cols], sb["minus_ident8"][:, :], start=False, stop=True)
                    nc.tensor.matmul(shift_ps[:, TG * H:TG * H + 1], sb["head_rows"][:, :], drop[:, g.slot(2), :],
                                     start=True, stop=True).then_inc(shift_ready, 1)
                if live(3):
                    g = k.back(3)
                    pe.wait_ge(leaky_ready, g.uses())
                    at_least(pe, logit_copied, g.back(1).uses())
                    nc.tensor.matmul(logit_ps[:, :], sb["att_block"][:, :], leaky[:, g.slot(2), :], start=True, stop=True).then_inc(logit_ready, 1)
                if live(2):
                    g = k.back(2)
                    b = g.slot(4)
                    pe.wait_ge(attr_loaded[b], g.uses(4, 16))
                    at_least(pe, leaky_ready, g.back(2).uses())
                    nc.tensor.matmul(pre_ps[:, g.slot(2), :], sb["W_e"][:, :], attrT[:, b, :], start=True, stop=False)
                    pe.wait_ge(xr_loaded[b], g.uses(4, 16 * TG))
                    pe.wait_ge(onehotT_copied, g.uses())
                    for t in range(TG):
                        cols = slice(t * P, (t + 1) * P)
                        nc.tensor.matmul(pre_ps[:, g.slot(2), cols], xr_win[:, b, t, :], onehotT[:, g.slot(2), cols], start=False, stop=False)
                    pe.wait_ge(rows_gathered[g.slot(NX)], g.uses(NX, 16 * TG))
                    for t in range(TG):
                        last = nc.tensor.matmul(pre_ps[:, g.slot(2), t * P:(t + 1) * P], xl_rows[:, g.slot(NX), t, :], ident[:, :],
                                                start=False, stop=t == TG - 1)
                    last.then_inc(pre_ready, 1)
                if live(1):
                    g = k.back(1)
                    pe.wait_ge(onehot_ready, g.uses())
                    at_least(pe, onehotT_copied, g.back(1).uses())
                    for t in range(TG):
                        last = nc.tensor.transpose(onehotT_ps[:, t * P:(t + 1) * P], onehot[:, g.slot(NS), t, :], ident[:, :])
                    last.then_inc(onehotT_ready, 1)
            steps(pe, G, PEEL, U, TAIL, body)

        @block.scalar
        def _(act):
            def body(k, live):
                if live(4):
                    g = k.back(4)
                    act.wait_ge(shift_ready, g.uses())
                    at_least(act, acc_steps, g.back(2).uses(1, ACC_STEPS))
                    nc.scalar.activation(factor[:, g.slot(2), :], shift_ps[:, TG * H:TG * H + 1], ACT.Exp).then_inc(exp_ready, 1)
                    nc.scalar.activation(expd[:, g.slot(2), :, :].rearrange("p t (h o) -> p (t h) o", o=O), bc(shift_ps[:, 0:TG * H], 2, O),
                                         ACT.Exp).then_inc(exp_ready, 1)
                if live(3):
                    g = k.back(3)
                    act.wait_ge(logit_ready, g.uses())
                    at_least(act, shift_ready, g.back(2).uses())
                    nc.scalar.activation(logitT[:, g.slot(2), :], logit_ps[:, :], ACT.Copy).then_inc(logit_copied, 1)
                if live(2):
                    g = k.back(2)
                    act.wait_ge(pre_ready, g.uses())
                    at_least(act, leaky_ready, g.back(2).uses())
                    nc.scalar.activation(fifth[:, g.slot(2), :], pre_ps[:, g.slot(2), :], ACT.Copy, scale=0.2).then_inc(fifth_ready, 1)
                if live(1):
                    g = k.back(1)
                    act.wait_ge(onehotT_ready, g.uses())
                    at_least(act, pre_ready, g.back(2).uses())
                    nc.scalar.activation(onehotT[:, g.slot(2), :], onehotT_ps[:, :], ACT.Copy).then_inc(onehotT_copied, 1)
            steps(act, G, PEEL, U, TAIL, body)

        @block.vector
        def _(dve):
            dve.memset(prefix[:, 1, :], -BIG).then_inc(prefix_ready, 1)
            dve.wait_ge(prefix_ready, 1)
            dve.sem_clear(prefix_ready)

            def body(k, live):
                if live(0):
                    at_least(dve, sums_ready, k.back(NS).uses())
                    nc.vector.tensor_tensor(onehot[:, k.slot(NS), :, :], bc(sb["iota"][:, :], 1, TG),
                                            bc(dst_rel[:, bass.ds(k.index(TG), TG)], 2, W), ALU.is_equal).then_inc(onehot_ready, 1)
                if live(5):
                    g = k.back(5)
                    first = g.index(ACC_STEPS)
                    for t in range(TG):
                        base = dve.value_load(tile_base[0:1, bass.ds(g.index(TG, t), 1)], min_val=0, max_val=N)
                        if t == 0:
                            dve.wait_ge(sums_ready, g.uses())
                            at_least(dve, acc_steps, first)
                            nc.vector.tensor_scalar(acc[:, :, bass.ds(base, 1)], acc[:, :, bass.ds(base, 1)],
                                                    factor[:, g.slot(2), :], None, ALU.mult).then_inc(acc_steps, 1)
                        dve.wait_ge(acc_steps, first + (t + 1))
                        nc.vector.tensor_tensor(acc[:, :, bass.ds(base, W)], acc[:, :, bass.ds(base, W)],
                                                sums_ps[:, :, t * W:(t + 1) * W], ALU.add).then_inc(acc_steps, 1)
                if live(4):
                    g = k.back(4)
                    dve.wait_ge(exp_ready, g.uses(1, 2))
                    at_least(dve, sums_ready, g.back(2).uses())
                    nc.vector.tensor_tensor(msg[:, g.slot(2), :, :], xl_rows[:, g.slot(NX), :, :], expd[:, g.slot(2), :, :], ALU.mult).then_inc(msg_ready, 1)
                if live(3):
                    g = k.back(3)
                    b, s, before = g.slot(4), g.slot(2), g.back(1).slot(2)
                    dve.wait_ge(limit_loaded[b], g.uses(4, 16))
                    dve.wait_ge(logit_copied, g.uses())
                    at_least(dve, drop_ready, g.back(1).uses())
                    nc.vector.tensor_tensor_scan(prefix[:, s, :], limit[:, b, 0:GE], logitT[:, s, :],
                                                 prefix[:, before, GE - 1:GE], ALU.min, ALU.max).then_inc(prefix_ready, 1)
                    dve.wait_ge(prefix_ready, g.uses())
                    at_least(dve, shift_ready, g.back(2).uses())
                    nc.vector.tensor_tensor_scan(peak[:, s, ::-1], limit[:, b, GE:0:-1], prefix[:, s, ::-1],
                                                 -BIG, ALU.min, ALU.max).then_inc(peak_ready, 1)
                    dve.wait_ge(peak_ready, g.uses())
                    nc.vector.tensor_scalar(drop[:, s, :], prefix[:, before, GE - 1:GE], peak[:, s, 0:1], 0.0,
                                            ALU.subtract, ALU.min).then_inc(drop_ready, 1)
                if live(2):
                    g = k.back(2)
                    dve.wait_ge(fifth_ready, g.uses())
                    at_least(dve, logit_ready, g.back(2).uses())
                    nc.vector.tensor_tensor(leaky[:, g.slot(2), :], pre_ps[:, g.slot(2), :], fifth[:, g.slot(2), :], ALU.max).then_inc(leaky_ready, 1)
            steps(dve, G, PEEL, U, TAIL, body)


def update_nodes(nc, sb, q, out):
    from contextlib import ExitStack
    with ExitStack() as ctx:
        def tile(name, shape, dt=F32):
            return ctx.enter_context(nc.sbuf_tensor("upd_" + name, shape, dt))

        def bank(name, shape):
            return ctx.enter_context(nc.psum_tensor("upd_" + name, shape, F32))

        def sem(name):
            return ctx.enter_context(nc.semaphore("upd_" + name))

        BN = NB * P
        x_rows = tile("x_rows", [P, 3, NB, D])
        sumT = tile("sumT", [P, 2, BN])
        h = tile("h", [P, 2, NB, D])
        hT = tile("hT", [P, BN])
        hidden = tile("hidden", [P, FC, BN])
        v = tile("v", [P, NB, D])
        x2 = tile("x2", [P, 2, NB, D])
        x2T = tile("x2T", [P, BN])
        feat = tile("feat", [P, 2, NB, D])
        stats = tile("stats", [P, NB, 6])
        moments = tile("moments", [P, NB, 2])
        spread = tile("spread", [P, NB])
        rstd = tile("rstd", [P, NB])
        rden = tile("rden", [P, 2, BN])
        sum_ps = bank("sum_ps", [P, NB, D])
        turn_ps = bank("turn_ps", [P, BN])
        hidden_ps = bank("hidden_ps", [P, 2, BN])
        ffn_ps = bank("ffn_ps", [P, NB, D])
        table_ps = bank("table_ps", [P, NB, 2 * D])
        x_loaded = [sem(f"x_loaded{b}") for b in range(3)]
        feat_stored = [sem(f"feat_stored{b}") for b in range(2)]
        sumT_ready, sum_ready, h_ready, turned, turn_copied = sem("sumT_ready"), sem("sum_ready"), sem("h_ready"), sem("turned"), sem("turn_copied")
        hidden_ready, gelu_ready, ffn_ready, x2_ready = sem("hidden_ready"), sem("gelu_ready"), sem("ffn_ready"), sem("x2_ready")
        table_ready, feat_ready, self_ready = sem("table_ready"), sem("feat_ready"), sem("self_ready")
        spread_ready, rstd_ready, chain1, chain2 = sem("spread_ready"), sem("rstd_ready"), sem("chain1"), sem("chain2")
        acc, resid = sb["acc"], sb["xT"][:, :].rearrange("p (t f) -> p t f", f=D)
        aggregate_turn = sem("aggregate_turn")
        LAGS = 2
        UN = 6
        PN = BATCHES % UN + UN
        block = ctx.enter_context(nc.Block())

        def nodes(table, k):
            return q[table][bass.ds(k.index(BN), BN), :].rearrange("(t p) f -> p t f", p=P)

        def norm_count(k, lag, nth):
            if lag == 0:
                return 1 if isinstance(k.i, int) and k.at == 0 else k.index(3, -1)
            if isinstance(k.i, int) and k.at == BATCHES:
                return 3 * BATCHES - 1 + nth
            return k.index(3, nth)

        def turns_before(g, kind):
            return g.index(2, kind)

        @block.sync
        def _(sp):
            def body(k, live):
                if live(0):
                    at_least(sp, x2_ready, k.back(3).uses())
                    sp.dma_start(x_rows[:, k.slot(3), :, :], nodes("x_pad", k)).then_inc(x_loaded[k.slot(3)], 16)
                if live(2):
                    g = k.back(2)
                    sp.wait_ge(feat_ready, g.uses())
                    sp.dma_start(nodes("feat", g), feat[:, g.slot(2), :, :]).then_inc(feat_stored[g.slot(2)], 16)
            steps(sp, BATCHES, PN, UN, LAGS, body)
            for b in range(2):
                sp.wait_ge(feat_stored[b], Step(BATCHES - 2 + (BATCHES - b) % 2).uses(2, 16))

        @block.gpsimd
        def _(pool):
            def body(k, live):
                for lag, norms in ((0, 1), (1, 2)):
                    if live(lag):
                        for nth in range(norms):
                            pool.wait_ge(spread_ready, norm_count(k, lag, nth))
                            nc.gpsimd.tensor_tensor(rstd[:, :], spread[:, :], sb["minus_half"][:, :], ALU.pow).then_inc(rstd_ready, 1)
            steps(pool, BATCHES, PN, UN, LAGS, body)

        @block.tensor
        def _(pe):
            ident = sb["ident"]

            def body(k, live):
                if live(2):
                    g = k.back(2)
                    pe.wait_ge(x2_ready, g.uses())
                    at_least(pe, turn_copied, turns_before(g, 1))
                    for t in range(NB):
                        last = nc.tensor.transpose(turn_ps[:, t * P:(t + 1) * P], x2[:, g.slot(2), t, :], ident[:, :])
                    last.then_inc(turned, 1)
                    pe.wait_ge(turn_copied, turns_before(g, 1) + 1)
                    at_least(pe, feat_ready, g.back(1).uses())
                    at_least(pe, self_ready, g.back(1).uses())
                    for t in range(NB):
                        last = nc.tensor.matmul(table_ps[:, t, :], x2T[:, t * P:(t + 1) * P], sb["W_feat"][:, :], start=True, stop=True)
                    last.then_inc(table_ready, 1)
                if live(1):
                    g = k.back(1)
                    pe.wait_ge(h_ready, g.uses())
                    at_least(pe, turn_copied, turns_before(g, 0))
                    for t in range(NB):
                        last = nc.tensor.transpose(turn_ps[:, t * P:(t + 1) * P], h[:, g.slot(2), t, :], ident[:, :])
                    last.then_inc(turned, 1)
                    pe.wait_ge(turn_copied, turns_before(g, 0) + 1)
                    for c in range(FC):
                        at_least(pe, gelu_ready, g.index(FC, c - 1))
                        nc.tensor.matmul(hidden_ps[:, c % 2, :], sb["W1"][:, c * P:(c + 1) * P], hT[:, :], start=True, stop=True).then_inc(hidden_ready, 1)
                    pe.wait_ge(gelu_ready, g.uses(1, FC))
                    at_least(pe, x2_ready, g.back(1).uses())
                    for t in range(NB):
                        for c in range(FC):
                            last = nc.tensor.matmul(ffn_ps[:, t, :], hidden[:, c, t * P:(t + 1) * P], sb["W2"][:, c, :], start=c == 0, stop=c == FC - 1)
                    last.then_inc(ffn_ready, 1)
                if live(0):
                    pe.wait_ge(sumT_ready, k.uses())
                    at_least(pe, h_ready, k.back(1).uses())
                    for t in range(NB):
                        last = nc.tensor.transpose(sum_ps[:, t, :], sumT[:, k.slot(2), t * P:(t + 1) * P], ident[:, :])
                    last.then_inc(sum_ready, 1)
            steps(pe, BATCHES, PN, UN, LAGS, body)

        @block.scalar
        def _(act):
            def body(k, live):
                if live(2):
                    g = k.back(2)
                    act.wait_ge(turned, turns_before(g, 1) + 1)
                    at_least(act, table_ready, g.back(1).uses())
                    nc.scalar.activation(x2T[:, :], turn_ps[:, :], ACT.Copy).then_inc(turn_copied, 1)
                    act.wait_ge(table_ready, g.uses())
                    at_least(act, feat_stored[g.slot(2)], g.back(2).uses(2, 16))
                    nc.scalar.activation(feat[:, g.slot(2), :, :], table_ps[:, :, 0:D], ACT.Copy, scale=FEAT_SCALE).then_inc(feat_ready, 1)
                if live(1):
                    g = k.back(1)
                    act.wait_ge(turned, turns_before(g, 0) + 1)
                    at_least(act, hidden_ready, g.index(FC))
                    nc.scalar.activation(hT[:, :], turn_ps[:, :], ACT.Copy).then_inc(turn_copied, 1)
                    at_least(act, ffn_ready, g.back(1).uses())
                    for c in range(FC):
                        act.wait_ge(hidden_ready, g.index(FC, c + 1))
                        nc.scalar.activation(hidden[:, c, :], hidden_ps[:, c % 2, :], ACT.Gelu, bias=sb["b1"][:, c:c + 1]).then_inc(gelu_ready, 1)
            steps(act, BATCHES, PN, UN, LAGS, body)

        @block.vector
        def _(dve):
            def linked(chain, start):
                made = [0]

                def link(ins):
                    made[0] += 1
                    ins.then_inc(chain, 1)
                    dve.wait_ge(chain, start + made[0])
                return link

            def normalise(link, to, of, k, lag, nth):
                for t in range(NB):
                    last = nc.vector.bn_stats(stats[:, t, :], of[:, t, :])
                link(last)
                dve.sem_inc(aggregate_turn, 1)
                for t in range(NB):
                    last = nc.vector.bn_aggr(moments[:, t, :], stats[:, t, :])
                link(last)
                nc.vector.tensor_scalar(spread[:, :], moments[:, :, 1], LN_EPS, None, ALU.add).then_inc(spread_ready, 1)
                link(nc.vector.tensor_tensor(to, of, bc(moments[:, :, 0], 2, D), ALU.subtract))
                dve.wait_ge(rstd_ready, norm_count(k, lag, nth))
                return nc.vector.tensor_tensor(to, to, bc(rstd[:, :], 2, D), ALU.mult)

            def body(k, live):
                if live(0):
                    link = linked(chain1, k.index(8))
                    cols = bass.ds(k.index(BN), BN)
                    s = k.slot(2)
                    link(nc.vector.tensor_scalar(rden[:, 0, :], acc[:, 1, cols], 1e-16, None, ALU.add))
                    link(nc.vector.reciprocal(rden[:, 1, :], rden[:, 0, :]))
                    link(nc.vector.tensor_tensor(rden[:, 0, :], acc[:, 0, cols], rden[:, 1, :], ALU.mult))
                    nc.vector.scalar_tensor_tensor(out=sumT[:, s, :], in0=rden[:, 0, :], scalar=sb["b_att"][:, :], in1=sb["xT"][:, cols],
                                                   op0=ALU.add, op1=ALU.add).then_inc(sumT_ready, 1)
                    dve.wait_ge(sum_ready, k.uses())
                    at_least(dve, x2_ready, k.back(2).uses())
                    to = h[:, s, :, :]
                    link(normalise(link, to, sum_ps[:, :, :], k, 0, 0))
                    link(nc.vector.tensor_tensor(to, to, bc(sb["g1"][:, :], 1, NB), ALU.mult))
                    nc.vector.tensor_tensor(to, to, bc(sb["be1"][:, :], 1, NB), ALU.add).then_inc(h_ready, 1)
                if live(1):
                    g = k.back(1)
                    s = g.slot(2)
                    link = linked(chain2, g.index(12))
                    dve.wait_ge(ffn_ready, g.uses())
                    dve.wait_ge(x_loaded[g.slot(3)], g.uses(3, 16))
                    to = v[:, :, :]
                    link(nc.vector.tensor_tensor(to, ffn_ps[:, :, :], h[:, s, :, :], ALU.add))
                    link(nc.vector.tensor_tensor(to, to, bc(sb["b2"][:, :], 1, NB), ALU.add))
                    link(normalise(link, to, to, k, 1, 0))
                    link(nc.vector.tensor_tensor(to, to, bc(sb["g2"][:, :], 1, NB), ALU.mult))
                    link(nc.vector.tensor_tensor(to, to, bc(sb["be2"][:, :], 1, NB), ALU.add))
                    link(nc.vector.tensor_tensor(to, to, x_rows[:, g.slot(3), :, :], ALU.add))
                    at_least(dve, self_ready, g.back(2).uses())
                    normalise(link, x2[:, s, :, :], to, k, 1, 1).then_inc(x2_ready, 1)
                if live(2):
                    g = k.back(2)
                    dve.wait_ge(feat_ready, g.uses())
                    nc.vector.scalar_tensor_tensor(out=resid[:, bass.ds(g.index(NB), NB), :], in0=table_ps[:, :, D:2 * D], scalar=SELF_SCALE,
                                                   in1=x2[:, g.slot(2), :, :], op0=ALU.mult, op1=ALU.add).then_inc(self_ready, 1)
            steps(dve, BATCHES, PN, UN, LAGS, body)
            dve.memset(acc[:, :, :], 0.0)


def convolution(nc, sb, q, out):
    from contextlib import ExitStack
    with ExitStack() as ctx:
        def tile(name, shape, dt=F32):
            return ctx.enter_context(nc.sbuf_tensor("conv_" + name, shape, dt))

        def bank(name, shape):
            return ctx.enter_context(nc.psum_tensor("conv_" + name, shape, F32))

        def sem(name):
            return ctx.enter_context(nc.semaphore("conv_" + name))

        NX, NI, NS = 8, 4, 8
        HE = GE // 2
        V3 = 3 * MUL
        idx = [tile(f"idx{b}", [P, TG], I32) for b in range(NI)]
        rows = tile("feat_rows", [P, NX, TG, D])
        radial = tile("radial", [2 * RADIAL, 4, HE])
        onehot = tile("onehot", [P, NS, TG, W])
        hid1 = tile("hid1", [2 * HID, 2, HE])
        hid2 = tile("hid2", [2 * HID, 2, HE])
        by0 = tile("by0", [P, TG, D])
        scal = tile("scal", [P, TG, 3, MUL])
        dots = tile("dots", [P, TG, 3, MUL])
        edge4 = tile("edge4", [P, T, 4])
        edge4_loaded = sem("edge4_loaded")
        dot = tile("dot", [P, 2, TG, MUL])
        vals = tile("vals", [P, 2, TG, 2 * D])
        hid1_ps = bank("hid1_ps", [2 * HID, GE])
        hid2_ps = bank("hid2_ps", [2 * HID, GE])
        w_ps = bank("w_ps", [P, 2, TG, D])
        sums_ps = bank("sums_ps", [P, 2, GE])
        idx_loaded = [sem(f"idx_loaded{b}") for b in range(NI)]
        radial_loaded = [sem(f"radial_loaded{b}") for b in range(4)]
        rows_gathered = [sem(f"rows_gathered{b}") for b in range(NX)]
        pool_turn = sem("pool_turn")
        onehot_ready, hid1_ready, gelu1_ready, hid2_ready, gelu2_ready = sem("onehot_ready"), sem("hid1_ready"), sem("gelu1_ready"), sem("hid2_ready"), sem("gelu2_ready")
        w_ready, vals_ready, sums_ready, acc_steps, chain = sem("w_ready"), sem("vals_ready"), sem("sums_ready"), sem("acc_steps"), sem("product_steps")
        TAIL = 5
        PRODUCTS = 6
        block = ctx.enter_context(nc.Block())
        tile_base, dst_rel, acc = sb["tile_base"], sb["dst_rel"], sb["acc"]

        @block.sync
        def _(sp):
            sp.dma_start(edge4[:, :, :], q["edge4_tiles"].rearrange("p (t c) -> p t c", c=4)).then_inc(edge4_loaded, 16)

            def body(k, live):
                if not live(0):
                    return
                at_least(sp, rows_gathered[k.back(NI).slot(NX)], k.back(NI).uses(NX, 16 * TG))
                sp.dma_start(idx[k.slot(NI)][:, :], q["src_tiles"][:, bass.ds(k.index(TG), TG)]).then_inc(idx_loaded[k.slot(NI)], 16)
                at_least(sp, hid1_ready, k.back(4).uses())
                for half in range(2):
                    sp.dma_start(radial[half * RADIAL:(half + 1) * RADIAL, k.slot(4), :],
                                 q["radialT"][:, bass.ds(k.index(GE, half * HE), HE)]).then_inc(radial_loaded[k.slot(4)], 16)
            steps(sp, G, PEEL, U, 0, body)

        @block.gpsimd
        def _(pool):
            def body(k, live):
                if not live(0):
                    return
                pool.wait_ge(idx_loaded[k.slot(NI)], k.uses(NI, 16))
                pool.sem_inc(pool_turn, 1)
                if not isinstance(k.i, int) or k.at >= NX:
                    pool.wait_ge(vals_ready, k.back(NX).uses())
                    pool.sem_inc(pool_turn, 1)
                for t in range(TG):
                    pool.indirect_dma_start(rows[:, k.slot(NX), t, :], None, q["feat"][:, :],
                                            bass.IndirectOffsetOnAxis(ap=idx[k.slot(NI)][:, t:t + 1], axis=0)
                                            ).then_inc(rows_gathered[k.slot(NX)], 16)
            steps(pool, G, PEEL, U, 0, body)

        @block.tensor
        def _(pe):
            def body(k, live):
                if live(5):
                    g = k.back(5)
                    pe.wait_ge(vals_ready, g.uses())
                    at_least(pe, acc_steps, g.back(1).uses(1, TG))
                    for t in range(TG):
                        for part in range(2):
                            last = nc.tensor.matmul(sums_ps[:, part, t * W:(t + 1) * W], vals[:, g.slot(2), t, part * D:(part + 1) * D],
                                                    onehot[:, g.slot(NS), t, :], start=True, stop=True)
                    last.then_inc(sums_ready, 1)
                if live(3):
                    g = k.back(3)
                    pe.wait_ge(gelu2_ready, g.uses())
                    at_least(pe, vals_ready, g.back(2).uses())
                    for c in range(2):
                        last = nc.tensor.matmul(w_ps[:, g.slot(2), c:TG:2, :], hid2[:, g.slot(2), c * P:(c + 1) * P], sb["Wp"][:, :, :], start=True, stop=True)
                    last.then_inc(w_ready, 1)
                if live(2):
                    g = k.back(2)
                    pe.wait_ge(gelu1_ready, g.uses())
                    at_least(pe, gelu2_ready, g.back(1).uses())
                    nc.tensor.matmul(hid2_ps[:, 0:HE], sb["mlp2"][:, :], hid1[:, g.slot(2), :], start=True, stop=True).then_inc(hid2_ready, 1)
                if live(1):
                    g = k.back(1)
                    pe.wait_ge(radial_loaded[g.slot(4)], g.uses(4, 32))
                    at_least(pe, gelu1_ready, g.back(1).uses())
                    nc.tensor.matmul(hid1_ps[:, 0:HE], sb["mlp1"][:, :], radial[:, g.slot(4), :], start=True, stop=True).then_inc(hid1_ready, 1)
            steps(pe, G, PEEL, U, TAIL, body)

        @block.scalar
        def _(act):
            def body(k, live):
                if live(2):
                    g = k.back(2)
                    act.wait_ge(hid2_ready, g.uses())
                    at_least(act, w_ready, g.back(2).uses())
                    nc.scalar.activation(hid2[:, g.slot(2), :], hid2_ps[:, 0:HE], ACT.Gelu_apprx_tanh, scale=1.0 / float(np.sqrt(HID))).then_inc(gelu2_ready, 1)
                if live(1):
                    g = k.back(1)
                    act.wait_ge(hid1_ready, g.uses())
                    at_least(act, hid2_ready, g.back(2).uses())
                    nc.scalar.activation(hid1[:, g.slot(2), :], hid1_ps[:, 0:HE], ACT.Gelu_apprx_tanh, scale=1.0 / float(np.sqrt(RADIAL))).then_inc(gelu1_ready, 1)
            steps(act, G, PEEL, U, TAIL, body)

        @block.vector
        def _(dve):
            dve.wait_ge(edge4_loaded, 16)

            def body(k, live):
                if live(0):
                    at_least(dve, sums_ready, k.back(NS).uses())
                    nc.vector.tensor_tensor(onehot[:, k.slot(NS), :, :], bc(sb["iota"][:, :], 1, TG),
                                            bc(dst_rel[:, bass.ds(k.index(TG), TG)], 2, W), ALU.is_equal).then_inc(onehot_ready, 1)
                if live(5):
                    g = k.back(5)
                    for t in range(TG):
                        base = dve.value_load(tile_base[0:1, bass.ds(g.index(TG, t), 1)], min_val=0, max_val=N)
                        if t == 0:
                            dve.wait_ge(sums_ready, g.uses())
                        at_least(dve, acc_steps, g.index(TG, t))
                        nc.vector.tensor_tensor(acc[:, :, bass.ds(base, W)], acc[:, :, bass.ds(base, W)],
                                                sums_ps[:, :, t * W:(t + 1) * W], ALU.add).then_inc(acc_steps, 1)
                if live(4):
                    g = k.back(4)
                    r = rows[:, g.slot(NX), :, :]
                    e1 = r[:, :, MUL:D].rearrange("p t (c w) -> p t c w", c=3)
                    ea = edge4[:, bass.ds(g.index(TG), TG), :]
                    at_least(dve, chain, g.index(PRODUCTS))
                    dve.wait_ge(rows_gathered[g.slot(NX)], g.uses(NX, 16 * TG))
                    nc.vector.tensor_tensor(dots[:, :, :, :], e1, bc(ea[:, :, 1:4], 3, MUL), ALU.mult).then_inc(chain, 1)
                    nc.vector.tensor_tensor(by0[:, :, :], r, ea[:, :, 0:1].broadcast_to([P, TG, D]), ALU.mult).then_inc(chain, 1)
                    dve.wait_ge(chain, g.index(PRODUCTS, 2))
                    nc.vector.tensor_tensor(dot[:, 0, :, :], dots[:, :, 0, :], dots[:, :, 1, :], ALU.add).then_inc(chain, 1)
                    nc.vector.tensor_tensor(scal[:, :, :, :], bc(r[:, :, 0:MUL], 2, 3), bc(ea[:, :, 1:4], 3, MUL), ALU.mult).then_inc(chain, 1)
                    dve.wait_ge(chain, g.index(PRODUCTS, 4))
                    nc.vector.tensor_tensor(dot[:, 1, :, :], dot[:, 0, :, :], dots[:, :, 2, :], ALU.add).then_inc(chain, 1)
                    dve.wait_ge(w_ready, g.uses())
                    at_least(dve, sums_ready, g.back(2).uses())
                    to, w = vals[:, g.slot(2), :, :], w_ps[:, g.slot(2), :, :]
                    nc.vector.tensor_tensor(to[:, :, 0:MUL], by0[:, :, 0:MUL], w[:, :, 0:MUL], ALU.mult)
                    nc.vector.tensor_tensor(to[:, :, MUL:D].rearrange("p t (c w) -> p t c w", c=3), by0[:, :, MUL:D].rearrange("p t (c w) -> p t c w", c=3),
                                            bc(w[:, :, MUL:2 * MUL], 2, 3), ALU.mult)
                    nc.vector.tensor_tensor(to[:, :, D:D + V3].rearrange("p t (c w) -> p t c w", c=3), scal[:, :, :, :],
                                            bc(w[:, :, 2 * MUL:3 * MUL], 2, 3), ALU.mult).then_inc(chain, 1)
                    dve.wait_ge(chain, g.index(PRODUCTS, 6))
                    nc.vector.tensor_tensor(to[:, :, D + V3:2 * D], dot[:, 1, :, :], w[:, :, 3 * MUL:4 * MUL], ALU.mult).then_inc(vals_ready, 1)
            steps(dve, G, PEEL, U, TAIL, body)


def finish_nodes(nc, sb, q, out):
    from contextlib import ExitStack
    with ExitStack() as ctx:
        def tile(name, shape, dt=F32):
            return ctx.enter_context(nc.sbuf_tensor("fin_" + name, shape, dt))

        def sem(name):
            return ctx.enter_context(nc.semaphore("fin_" + name))

        conv_ps = ctx.enter_context(nc.psum_tensor("conv_ps", [P, 2, NB, D], F32))
        v = tile("v", [P, 2, NB, D])
        done = tile("done", [P, 2, NB, D])
        stats = tile("stats", [P, NB, 6])
        moments = tile("moments", [P, NB, 2])
        spread = tile("spread", [P, NB])
        rstd = tile("rstd", [P, NB])
        conv_ready, v_ready, spread_ready, rstd_ready = sem("conv_ready"), sem("v_ready"), sem("spread_ready"), sem("rstd_ready")
        done_ready, chain = sem("done_ready"), sem("chain")
        stored = [sem(f"stored{b}") for b in range(2)]
        acc, resid = sb["acc"], sb["xT"][:, :].rearrange("p (t f) -> p t f", f=D)
        FULL = N // (NB * P)
        REST = N - FULL * NB * P
        USED = FULL + 1
        UN = 2
        PN = USED % UN + UN
        aggregate_turn = sem("aggregate_turn")
        block = ctx.enter_context(nc.Block())

        @block.tensor
        def _(pe):
            for n in range(USED):
                at_least(pe, v_ready, n - 1)
                for t in range(NB):
                    cols = slice((n * NB + t) * P, (n * NB + t + 1) * P)
                    nc.tensor.matmul(conv_ps[:, n % 2, t, :], acc[:, 0, cols], sb["W_convA"][:, :], start=True, stop=False)
                    last = nc.tensor.matmul(conv_ps[:, n % 2, t, :], acc[:, 1, cols], sb["W_convB"][:, :], start=False, stop=True)
                last.then_inc(conv_ready, 1)

        @block.gpsimd
        def _(pool):
            def body(k, live):
                if not live(0):
                    return
                pool.wait_ge(spread_ready, k.uses())
                nc.gpsimd.tensor_tensor(rstd[:, :], spread[:, :], sb["minus_half"][:, :], ALU.pow).then_inc(rstd_ready, 1)
            steps(pool, USED, PN, UN, 0, body)

        @block.vector
        def _(dve):
            def body(k, live):
                if not live(0):
                    return
                s = k.slot(2)
                dve.wait_ge(conv_ready, k.uses())
                at_least(dve, done_ready, k.back(1).uses())
                nc.vector.tensor_tensor(v[:, s, :, :], conv_ps[:, s, :, :], resid[:, bass.ds(k.index(NB), NB), :], ALU.add).then_inc(v_ready, 1)
                dve.wait_ge(v_ready, k.uses())
                for t in range(NB):
                    last = nc.vector.bn_stats(stats[:, t, :], v[:, s, t, :])
                last.then_inc(chain, 1)
                dve.wait_ge(chain, k.index(3, 1))
                dve.sem_inc(aggregate_turn, 1)
                for t in range(NB):
                    last = nc.vector.bn_aggr(moments[:, t, :], stats[:, t, :])
                last.then_inc(chain, 1)
                dve.wait_ge(chain, k.index(3, 2))
                nc.vector.tensor_scalar(spread[:, :], moments[:, :, 1], LN_EPS, None, ALU.add).then_inc(spread_ready, 1)
                nc.vector.tensor_tensor(v[:, s, :, :], v[:, s, :, :], bc(moments[:, :, 0], 2, D), ALU.subtract).then_inc(chain, 1)
                dve.wait_ge(chain, k.index(3, 3))
                dve.wait_ge(rstd_ready, k.uses())
                at_least(dve, stored[s], k.back(2).uses(2, 16))
                nc.vector.tensor_tensor(done[:, s, :, :], v[:, s, :, :], bc(rstd[:, :], 2, D), ALU.mult).then_inc(done_ready, 1)
            steps(dve, USED, PN, UN, 0, body)

        @block.sync
        def _(sp):
            def body(k, live):
                if not live(0):
                    return
                sp.wait_ge(done_ready, k.uses())
                sp.dma_start(out[bass.ds(k.index(NB * P), NB * P), :].rearrange("(t p) f -> p t f", p=P), done[:, k.slot(2), :, :]).then_inc(stored[k.slot(2)], 16)
            for k in range(FULL % UN + UN):
                body(Step(k, 0, UN), lambda lag: True)
            with sp.Fori(0, (FULL - FULL % UN - UN) // UN) as i:
                for u in range(UN):
                    body(Step(FULL % UN + UN + u, i, UN), lambda lag: True)
            sp.wait_ge(done_ready, USED)
            pieces = 0
            for t in range(NB):
                n = min(P, REST - t * P)
                if n > 0:
                    lo = FULL * NB * P + t * P
                    sp.dma_start(out[lo:lo + n, :], done[0:n, FULL % 2, t, :]).then_inc(stored[FULL % 2], 16)
                    pieces += 1
            for b in range(2):
                whole = (FULL - b + 1) // 2 * 16
                sp.wait_ge(stored[b], whole + (pieces * 16 if b == FULL % 2 else 0))


def program(nc, q, out):
    from contextlib import ExitStack
    with ExitStack() as ctx:
        def tile(name, shape, dt=F32):
            return ctx.enter_context(nc.sbuf_tensor(name, shape, dt))

        sb = {}
        for name, shape in (("W_lr", [P, 2 * D]), ("W_e", [P, D]), ("W1", [P, FF]), ("W2", [P, FC, D]), ("b1", [P, FC]), ("b_att", [P, 1]),
                            ("b_lr", [P, 2 * D]), ("b2", [P, D]), ("g1", [P, D]), ("be1", [P, D]), ("g2", [P, D]), ("be2", [P, D]),
                            ("mlp1", [2 * RADIAL, 2 * HID]), ("mlp2", [2 * HID, 2 * HID]), ("Wp", [2 * HID, 2, D]), ("W_feat", [P, 2 * D]),
                            ("W_convA", [P, D]), ("W_convB", [P, D]), ("ident", [P, P]), ("minus_ident8", [H, H]), ("att_block", [P, H]),
                            ("head_rows", [H, D]), ("iota", [P, W]), ("minus_half", [P, NB]), ("dst_rel", [P, T]), ("acc", [P, 2, N_PAD]),
                            ("xT", [P, N_PAD])):
            sb[name] = tile("c_" + name, shape)
        sb["tile_base"] = tile("c_tile_base", [1, T], I32)
        constants(nc, sb, q, out)
        project_nodes(nc, sb, q, out)
        attention(nc, sb, q, out)
        update_nodes(nc, sb, q, out)
        convolution(nc, sb, q, out)
        finish_nodes(nc, sb, q, out)


def kernel(**inputs):
    import concourse.bacc as bacc
    from concourse.bass_utils import run_bass_kernel_spmd as run

    a = {k: np.asarray(v) for k, v in inputs.items()}

    def padded(x, n, value=0):
        return np.concatenate([x, np.full((n - x.shape[0],) + x.shape[1:], value, x.dtype)])

    dst = padded(a["dst"], E_PAD, N)
    x_pad = padded(a["x"], N_PAD)
    arrays = {k: np.ascontiguousarray(v) for k, v in a.items()
              if k.startswith("L") and k != "L0_gnn_b1"}
    arrays |= {
        "x_pad": x_pad,
        "xT": np.ascontiguousarray(x_pad.T),
        "b1_columns": np.ascontiguousarray(a["L0_gnn_b1"].reshape(FC, P).T),
        "src_tiles": np.ascontiguousarray(padded(a["src"], E_PAD).reshape(T, P).T),
        "dst_tiles": np.ascontiguousarray(dst.reshape(T, P).T),
        "dst_line": np.concatenate([np.full((1,), -1, dst.dtype), dst]),
        "attrT": np.ascontiguousarray(padded(a["edge_attr_128"], E_PAD).T),
        "radialT": np.ascontiguousarray(padded(a["edge_attr_8"], E_PAD).T),
        "edge4_tiles": np.ascontiguousarray(padded(a["edge_attr_4"], E_PAD).reshape(T, P, 4).transpose(1, 0, 2)).reshape(P, T * 4),
    }
    nc = bacc.Bacc("TRN2", target_bir_lowering=False, num_devices=1)
    q = {k: nc.dram_tensor("in_" + k, v.shape, mybir.dt.from_np(v.dtype), kind="ExternalInput").ap() for k, v in arrays.items()}
    for name, shape in (("xl", (N_PAD, D)), ("xr", (N_PAD, D)), ("feat", (N_PAD, D)), ("limit", (E_PAD + 1,))):
        q[name] = nc.dram_tensor(name, shape, F32).ap()
    out = nc.dram_tensor("out", (N, D), F32, kind="ExternalOutput").ap()
    program(nc, q, out)
    return run(nc, [{"in_" + k: v for k, v in arrays.items()}], core_ids=[0]).results[0]["out"]
```

```python
import numpy as np
from contextlib import ExitStack
import concourse.bass as bass
from concourse import mybir

F32 = mybir.dt.float32
I32 = mybir.dt.int32
ALU = mybir.AluOpType
ACT = mybir.ActivationFunctionType

P = 128
N, E, D, H = 6250, 206250, 128, 8
O = D // H
OX = O + 1
FF = 4 * D
FC = FF // P
MUL, RADIAL, HID = 32, 8, 64
V3 = 3 * MUL
TG = 4
GE = TG * P
G = -(-E // GE)
T = G * TG
E_PAD = G * GE
LINES = max(n for n in range(1, P + 1) if G % n == 0)
NB = 4
BATCHES = -(-(N + P) // (NB * P))
N_PAD = BATCHES * NB * P
BLOCKS = BATCHES * NB + 1
NARROW = 64
U = 8
PEEL = G % U + U
BIG = 1e30
LN_EPS = 1e-5
MIX_C, MIX_S = float(np.cos(np.pi / 8)), float(np.sin(np.pi / 8))
SELF_SCALE = MIX_C / float(np.sqrt(MUL))
FEAT_SCALE = 1.0 / float(np.sqrt(MUL))
CONV_SCALE = MIX_S / float(np.sqrt(2 * MUL) * np.sqrt(32.0) * np.sqrt(2.0))
CONV_SCALE_B = CONV_SCALE / float(np.sqrt(3.0))


class Step:

    def __init__(self, at, i=0, stride=U):
        self.at, self.i, self.stride = at, i, stride

    def back(self, n):
        return Step(self.at - n, self.i, self.stride)

    def index(self, scale=1, plus=0):
        base = self.at * scale + plus
        return base if isinstance(self.i, int) else self.i * (self.stride * scale) + base

    def uses(self, n=1, by=1):
        base = (self.at // n + 1) * by
        return base if isinstance(self.i, int) else self.i * (self.stride // n * by) + base

    def slot(self, n):
        return self.at % n


def at_least(eng, sem, value):
    if not isinstance(value, int) or value > 0:
        eng.wait_ge(sem, value)


def steps(eng, total, peel, unroll, tail, body):
    for k in range(peel):
        body(Step(k, 0, unroll), lambda lag, k=k: 0 <= k - lag < total)
    with eng.Fori(0, (total - peel) // unroll) as i:
        for u in range(unroll):
            body(Step(peel + u, i, unroll), lambda lag: True)
    for k in range(total, total + tail):
        body(Step(k, 0, unroll), lambda lag, k=k: 0 <= k - lag < total)


def by_width(eng, narrow, run):
    flag = eng.value_load(narrow[0:1, 0:1], min_val=0, max_val=1)
    with eng.If(flag > 0):
        run(1)
    with eng.Else():
        run(TG)


def bc(ap, axis, n):
    ap = ap.unsqueeze(axis)
    shape = list(ap.shape)
    shape[axis] = n
    return ap.broadcast_to(shape)


def constants(nc, sb, q, out):
    with ExitStack() as ctx:
        def tile(name, shape, dt=F32):
            return ctx.enter_context(nc.sbuf_tensor("set_" + name, shape, dt))

        def sem(name):
            return ctx.enter_context(nc.semaphore("set_" + name))

        consts_loaded, zeroed, blocks_loaded, masks, chain = sem("consts_loaded"), sem("zeroed"), sem("blocks_loaded"), sem("masks"), sem("chain")
        limits_ready, limits_stored, rel_ready, rel_stored = sem("limits_ready"), sem("limits_stored"), sem("rel_ready"), sem("rel_stored")
        ident_ready, ident_stored = sem("ident_ready"), sem("ident_stored")
        dst_here, dst_before = tile("dst_here", [P, T], I32), tile("dst_before", [P, T], I32)
        dst_tiles, base_all = tile("dst_tiles", [P, T], I32), tile("base_all", [P, T], I32)
        pos_i, base_pos = tile("pos_i", [P, T], I32), tile("base_pos", [P, T], I32)
        limit_sb, last_limit = tile("limit_sb", [P, T]), tile("last_limit", [1, 1])
        lines, rel_lines = tile("lines", [LINES, E_PAD // LINES], I32), tile("rel_lines", [LINES, E_PAD // LINES])
        tile_last, span, widest = tile("tile_last", [1, T], I32), tile("span", [1, G]), tile("widest", [1, 1])
        iota_i, p_i, p_col = tile("iota_i", [P, P], I32), tile("p_i", [P, 1], I32), tile("p_col", [P, 1])
        att_col = tile("att_col", [P, 1])
        block = ctx.enter_context(nc.Block())
        loads = []

        def row(t, name, n):
            loads.append((t, q[name].rearrange("(a n) -> a n", a=1).partition_broadcast(P).rearrange("p a n -> p (a n)")))

        loads.append((dst_here[:, :], q["dst_line"][1:1 + E_PAD].rearrange("(p t) -> p t", p=P)))
        loads.append((dst_before[:, :], q["dst_line"][0:E_PAD].rearrange("(p t) -> p t", p=P)))
        loads.append((dst_tiles[:, :], q["dst_tiles"]))
        loads.append((base_all[:, :], q["dst_tiles"][0:1, :].partition_broadcast(P).rearrange("p a n -> p (a n)")))
        loads.append((sb["tile_base"][:, :], q["dst_tiles"][0:1, :]))
        loads.append((tile_last[:, :], q["dst_tiles"][P - 1:P, :]))
        loads.append((lines[:, :], q["dst_line"][1:1 + E_PAD].rearrange("(p n) -> p n", p=LINES)))
        loads.append((att_col[:, :], q["L0_gnn_att"].rearrange("h o -> (h o)").rearrange("(p a) -> p a", a=1)))
        loads.append((sb["W_lr"][:, 0:D], q["L0_gnn_W_l"]))
        loads.append((sb["W_lr"][:, D:2 * D], q["L0_gnn_W_r"]))
        loads.append((sb["W_e"][:, :], q["L0_gnn_W_e"]))
        loads.append((sb["W1"][:, :], q["L0_gnn_W1"]))
        loads.append((sb["W2"][:, :, :], q["L0_gnn_W2"].rearrange("(c p) n -> p c n", p=P)))
        loads.append((sb["b1"][:, :], q["b1_columns"]))
        loads.append((sb["xT"][:, :], q["xT"]))
        row(sb["b_lr"][:, 0:D], "L0_gnn_b_l", D)
        row(sb["b_lr"][:, D:2 * D], "L0_gnn_b_r", D)
        for name in ("b_att", "b2", "g1", "be1", "g2", "be2"):
            row(sb[name][:, :], "L0_gnn_" + name, D)
        blocks = []
        for half in range(2):
            blocks.append((sb["mlp1"][half * RADIAL:(half + 1) * RADIAL, half * HID:(half + 1) * HID], q["L1_gnn_W_mlp1"]))
            blocks.append((sb["mlp2"][half * HID:(half + 1) * HID, half * HID:(half + 1) * HID], q["L1_gnn_W_mlp2"]))
            for c, name in enumerate(("Wp_00", "Wp_10", "Wp_01", "Wp_11")):
                blocks.append((sb["Wp"][half * HID:(half + 1) * HID, half, c * MUL:(c + 1) * MUL], q["L1_gnn_" + name]))
        blocks.append((sb["W_feat"][0:MUL, 0:MUL], q["L1_gnn_W1_0e"][:, 0:MUL]))
        blocks.append((sb["W_feat"][0:MUL, D:D + MUL], q["L1_gnn_W1_0e"][:, MUL:2 * MUL]))
        blocks.append((sb["W_convA"][0:MUL, 0:MUL], q["L1_gnn_W2_0e"][0:MUL, :]))
        blocks.append((sb["W_convB"][3 * MUL:4 * MUL, 0:MUL], q["L1_gnn_W2_0e"][MUL:2 * MUL, :]))
        for c in range(3):
            lo = MUL * (c + 1)
            blocks.append((sb["W_feat"][MUL + c:D:3, lo:lo + MUL], q["L1_gnn_W1_1o"][:, 0:MUL]))
            blocks.append((sb["W_feat"][MUL + c:D:3, D + MUL + c:2 * D:3], q["L1_gnn_W1_1o"][:, MUL:2 * MUL]))
            blocks.append((sb["W_convA"][lo:lo + MUL, MUL + c:D:3], q["L1_gnn_W2_1o"][MUL:2 * MUL, :]))
            blocks.append((sb["W_convB"][MUL * c:MUL * (c + 1), MUL + c:D:3], q["L1_gnn_W2_1o"][0:MUL, :]))

        @block.sync
        def _(sp):
            for to, of in loads:
                sp.dma_start(to, of).then_inc(consts_loaded, 16)
            sp.wait_ge(limits_ready, 2)
            sp.dma_start(q["limit"][0:E_PAD].rearrange("(p t) -> p t", p=P), limit_sb[:, :]).then_inc(limits_stored, 16)
            sp.dma_start(q["limit"][E_PAD:E_PAD + 1].rearrange("(a n) -> a n", a=1), last_limit[:, :]).then_inc(limits_stored, 16)
            for nth, table in enumerate(("rel_group", "rel_tile")):
                sp.wait_ge(rel_ready, nth + 1)
                sp.dma_start(q[table].rearrange("(p n) -> p n", p=LINES), rel_lines[:, :]).then_inc(rel_stored, 16)
            sp.wait_ge(ident_ready, 1)
            sp.dma_start(q["ident_rows"], sb["ident"][:, :]).then_inc(ident_stored, 16)
            sp.wait_ge(limits_stored, 32)
            sp.wait_ge(rel_stored, 32)
            sp.wait_ge(ident_stored, 16)

        @block.scalar
        def _(act):
            act.wait_ge(zeroed, 6)
            with nc.allow_non_contiguous_dma(reason="small weights, once"):
                for to, of in blocks:
                    act.dma_start(to, of).then_inc(blocks_loaded, 16)

        @block.gpsimd
        def _(pool):
            pool.memset(sb["ident"][:, :], 0.0).then_inc(masks, 1)
            pool.memset(sb["att_block"][:, :], 1.0).then_inc(masks, 1)
            pool.iota(p_i[:, :], pattern=[[0, 1]], base=0, channel_multiplier=1).then_inc(masks, 1)
            pool.iota(iota_i[:, :], pattern=[[1, P]], base=0, channel_multiplier=0).then_inc(masks, 1)
            pool.wait_ge(masks, 4)
            pool.affine_select(out=sb["ident"][:, :], in_=sb["ident"][:, :], compare_op=ALU.not_equal, fill=1.0,
                               base=0, pattern=[[-1, P]], channel_multiplier=1).then_inc(masks, 1)
            pool.affine_select(out=sb["att_block"][:, :], in_=sb["att_block"][:, :], compare_op=ALU.is_ge, fill=0.0,
                               base=0, pattern=[[-O, H]], channel_multiplier=1).then_inc(masks, 1)
            pool.wait_ge(masks, 6)
            pool.affine_select(out=sb["att_block"][:, :], in_=sb["att_block"][:, :], compare_op=ALU.is_ge, fill=0.0,
                               base=O - 1, pattern=[[O, H]], channel_multiplier=-1).then_inc(masks, 1)

        @block.vector
        def _(dve):
            for name in ("mlp1", "mlp2", "W_feat", "W_convA", "W_convB"):
                dve.memset(sb[name][:, :], 0.0).then_inc(zeroed, 1)
            dve.memset(sb["Wp"][:, :, :], 0.0).then_inc(zeroed, 1)
            dve.memset(last_limit[:, :], -BIG).then_inc(limits_ready, 1)
            dve.memset(sb["minus_half"][:, :], -0.5)
            dve.memset(sb["one"][:, :], 1.0)
            dve.memset(sb["less"][:, :], 0.0).then_inc(chain, 1)
            dve.wait_ge(masks, 7)
            dve.tensor_copy(sb["iota"][:, :], iota_i[:, :])
            dve.tensor_copy(p_col[:, :], p_i[:, :]).then_inc(chain, 1)
            dve.wait_ge(chain, 2)
            dve.tensor_scalar(sb["minus_p"][:, :], p_col[:, :], -1.0, None, ALU.mult)
            dve.tensor_scalar(sb["less"][0:H, :], sb["ident"][0:H, 0:H], -1.0, None, ALU.mult)
            dve.tensor_copy(sb["less"][32:32 + H, :], sb["ident"][32:32 + H, 32:32 + H]).then_inc(ident_ready, 1)
            dve.wait_ge(consts_loaded, 16 * len(loads))
            dve.tensor_scalar(sb["att_block"][:, :], sb["att_block"][:, :], att_col[:, :], None, ALU.mult)
            dve.tensor_tensor(limit_sb[:, :], dst_here[:, :], dst_before[:, :], ALU.is_equal).then_inc(chain, 1)
            dve.wait_ge(chain, 3)
            dve.tensor_scalar(limit_sb[:, :], limit_sb[:, :], 2 * BIG, -BIG, ALU.mult, ALU.add).then_inc(limits_ready, 1)
            for nth, n in enumerate((GE, P)):
                view = lines[:, :].rearrange("p (w e) -> p w e", e=n)
                if nth:
                    dve.wait_ge(rel_stored, 16)
                dve.tensor_tensor(rel_lines[:, :].rearrange("p (w e) -> p w e", e=n), view,
                                  view[:, :, 0:1].broadcast_to([LINES, E_PAD // LINES // n, n]), ALU.subtract).then_inc(rel_ready, 1)
            dve.tensor_scalar(pos_i[:, :], dst_tiles[:, :], P - 1, None, ALU.bitwise_and).then_inc(chain, 1)
            dve.tensor_scalar(base_pos[:, :], base_all[:, :], P - 1, None, ALU.bitwise_and).then_inc(chain, 1)
            dve.tensor_scalar(sb["tile_pos"][:, :], sb["tile_base"][:, :], P - 1, None, ALU.bitwise_and)
            dve.tensor_scalar(sb["tile_block"][:, :], sb["tile_base"][:, :], P.bit_length() - 1, None, ALU.arith_shift_right)
            dve.wait_ge(chain, 5)
            dve.tensor_copy(sb["dst_pos"][:, :], pos_i[:, :])
            dve.tensor_scalar(sb["keep"][:, :], base_pos[:, :], p_col[:, :], None, ALU.is_le).then_inc(chain, 1)
            dve.wait_ge(chain, 6)
            dve.tensor_scalar(sb["pass_on"][:, :], sb["keep"][:, :], -1.0, 1.0, ALU.mult, ALU.add)
            firsts = sb["tile_base"][:, :].rearrange("a (g t) -> a g t", t=TG)[:, :, 0]
            lasts = tile_last[:, :].rearrange("a (g t) -> a g t", t=TG)[:, :, TG - 1]
            dve.tensor_tensor(span[:, :], lasts, firsts, ALU.subtract).then_inc(chain, 1)
            dve.wait_ge(chain, 7)
            dve.reduce_max(widest[:, :], span[:, :], mybir.AxisListType.X).then_inc(chain, 1)
            dve.wait_ge(chain, 8)
            dve.tensor_scalar(sb["narrow"][:, :], widest[:, :], float(NARROW), None, ALU.is_lt)
            dve.wait_ge(blocks_loaded, 16 * len(blocks))
            dve.tensor_scalar(sb["W_convA"][:, :], sb["W_convA"][:, :], CONV_SCALE, None, ALU.mult)
            dve.tensor_scalar(sb["W_convB"][0:3 * MUL, :], sb["W_convB"][0:3 * MUL, :], CONV_SCALE, None, ALU.mult)
            dve.tensor_scalar(sb["W_convB"][3 * MUL:P, :], sb["W_convB"][3 * MUL:P, :], CONV_SCALE_B, None, ALU.mult)


def project_nodes(nc, sb, q, out):
    with (nc.sbuf_tensor("rows", [P, 2, NB, 2 * D], F32) as rows, nc.psum_tensor("proj", [P, 2, NB, 2 * D], F32) as proj,
          nc.semaphore("projected") as projected, nc.semaphore("rows_ready") as rows_ready,
          nc.semaphore("rows_stored0") as st0, nc.semaphore("rows_stored1") as st1, nc.Block() as block):
        rows_stored = [st0, st1]
        PL = BATCHES % 2 + 2

        def nodes(table, k):
            return q[table][bass.ds(k.index(NB * P), NB * P), :].rearrange("(t p) f -> p t f", p=P)

        @block.tensor
        def _(pe):
            def body(k, live):
                if not live(0):
                    return
                at_least(pe, rows_ready, k.back(2).uses())
                for t in range(NB):
                    last = nc.tensor.matmul(proj[:, k.slot(2), t, :], sb["xT"][:, (k.at * NB + t) * P:(k.at * NB + t + 1) * P], sb["W_lr"][:, :], start=True, stop=True)
                last.then_inc(projected, 1)
            for n in range(BATCHES):
                body(Step(n), lambda lag: True)

        @block.vector
        def _(dve):
            def body(k, live):
                if not live(0):
                    return
                dve.wait_ge(projected, k.uses())
                at_least(dve, rows_stored[k.slot(2)], k.back(2).uses(2, 32))
                dve.tensor_tensor(rows[:, k.slot(2), :, :], proj[:, k.slot(2), :, :], bc(sb["b_lr"][:, :], 1, NB), ALU.add).then_inc(rows_ready, 1)
            steps(dve, BATCHES, PL, 2, 0, body)

        @block.sync
        def _(sp):
            def body(k, live):
                if not live(0):
                    return
                sp.wait_ge(rows_ready, k.uses())
                sp.dma_start(nodes("xl", k), rows[:, k.slot(2), :, 0:D]).then_inc(rows_stored[k.slot(2)], 16)
                sp.dma_start(nodes("xr", k), rows[:, k.slot(2), :, D:2 * D]).then_inc(rows_stored[k.slot(2)], 16)
            steps(sp, BATCHES, PL, 2, 0, body)
            for b in range(2):
                sp.wait_ge(rows_stored[b], Step(BATCHES - 2 + (BATCHES - b) % 2).uses(2, 32))


def attention(nc, sb, q, out, acc):
    with ExitStack() as ctx:
        def tile(name, shape, dt=F32):
            return ctx.enter_context(nc.sbuf_tensor("attn_" + name, shape, dt))

        def bank(name, shape):
            return ctx.enter_context(nc.psum_tensor("attn_" + name, shape, F32))

        def sem(name):
            return ctx.enter_context(nc.semaphore("attn_" + name))

        NX = 8
        ND = 4
        HX = H * OX
        LOGITS = 32
        idx = [tile(f"idx{b}", [P, TG], I32) for b in range(ND)]
        xl_rows = tile("xl_rows", [P, NX, TG, D])
        attrT = tile("attrT", [P, ND, GE])
        xr_win = tile("xr_win", [P, ND, TG, D])
        rel = tile("rel", [P, ND, GE])
        limit = tile("limit", [H, ND, GE + 1])
        first_pos = tile("first_pos", [H, ND, P])
        onehot = tile("onehot", [P, 2, TG, P])
        distance = tile("distance", [P, 2, GE])
        onehotT = tile("onehotT", [P, 2, GE])
        fifth = tile("fifth", [P, 2, GE])
        leaky = tile("leaky", [P, 2, GE])
        stack = tile("stack", [LOGITS + H, 2, GE])
        prefix = tile("prefix", [H, 2, GE])
        drop = tile("drop", [H, 2, 1])
        drop_diag = tile("drop_diag", [H, 2, H])
        factor = tile("factor", [P, 2, H])
        msg = tile("msg", [P, 2, TG, H, OX])
        pre_ps = bank("pre_ps", [P, 2, GE])
        logit_ps = bank("logit_ps", [H, GE])
        shift_ps = bank("shift_ps", [P, GE])
        sums_ps = bank("sums_ps", [P, 2, GE])

        idx_loaded = [sem(f"idx_loaded{b}") for b in range(ND)]
        attr_loaded = [sem(f"attr_loaded{b}") for b in range(ND)]
        xr_loaded = [sem(f"xr_loaded{b}") for b in range(ND)]
        rel_loaded = [sem(f"rel_loaded{b}") for b in range(ND)]
        limit_loaded = [sem(f"limit_loaded{b}") for b in range(ND)]
        first_loaded = [sem(f"first_loaded{b}") for b in range(ND)]
        rows_gathered = [sem(f"rows_gathered{b}") for b in range(NX)]
        pool_turn, zeroed = sem("pool_turn"), sem("zeroed")
        onehot_ready, distance_ready, onehotT_ready = sem("onehot_ready"), sem("distance_ready"), sem("onehotT_ready")
        pre_ready, fifth_ready, leaky_ready = sem("pre_ready"), sem("fifth_ready"), sem("leaky_ready")
        logit_ready, logit_copied = sem("logit_ready"), sem("logit_copied")
        prefix_ready, peak_ready, drop_made, drop_ready = sem("prefix_ready"), sem("peak_ready"), sem("drop_made"), sem("drop_ready")
        shift_ready, exp_ready, msg_ready = sem("shift_ready"), sem("exp_ready"), sem("msg_ready")
        sums_ready, acc_steps = sem("sums_ready"), sem("acc_steps")
        TAIL = 4
        block = ctx.enter_context(nc.Block())

        @block.sync
        def _(sp):
            def run(wins):
                rows = NARROW if wins == 1 else P
                rel_line = q["rel_group"] if wins == 1 else q["rel_tile"]

                def body(k, live):
                    if not live(0):
                        return
                    b = k.slot(ND)
                    at_least(sp, rows_gathered[k.back(ND).slot(NX)], k.back(ND).uses(NX, 16 * TG))
                    sp.dma_start(idx[b][:, :], q["src_tiles"][:, bass.ds(k.index(TG), TG)]).then_inc(idx_loaded[b], 16)
                    at_least(sp, onehotT_ready, k.back(ND).uses())
                    sp.dma_start(rel[0:rows, b, :], rel_line[bass.ds(k.index(GE), GE)].rearrange("(a n) -> a n", a=1)
                                 .partition_broadcast(rows).rearrange("p a n -> p (a n)")).then_inc(rel_loaded[b], 16)
                    at_least(sp, pre_ready, k.back(ND).uses())
                    sp.dma_start(attrT[:, b, :], q["attrT"][:, bass.ds(k.index(GE), GE)]).then_inc(attr_loaded[b], 16)
                    for w in range(wins):
                        base = sp.value_load(sb["tile_base"][0:1, bass.ds(k.index(TG, w), 1)], min_val=0, max_val=N)
                        sp.dma_start(xr_win[0:rows, b, w, :], q["xr"][bass.ds(base, rows), :]).then_inc(xr_loaded[b], 16)
                    at_least(sp, shift_ready, k.back(ND).uses())
                    sp.dma_start(limit[:, b, :], q["limit"][bass.ds(k.index(GE), GE + 1)].rearrange("(a n) -> a n", a=1)
                                 .partition_broadcast(H).rearrange("p a n -> p (a n)")).then_inc(limit_loaded[b], 16)
                    pos = sp.value_load(sb["tile_pos"][0:1, bass.ds(k.index(TG), 1)], min_val=0, max_val=P - 1)
                    sp.dma_start(first_pos[:, b, :], q["ident_rows"][bass.ds(pos, 1), :]
                                 .partition_broadcast(H).rearrange("p a n -> p (a n)")).then_inc(first_loaded[b], 16)
                steps(sp, G, PEEL, U, 0, body)
            by_width(sp, sb["narrow"], run)

        @block.gpsimd
        def _(pool):
            def body(k, live):
                if not live(0):
                    return
                b = k.slot(ND)
                pool.wait_ge(idx_loaded[b], k.uses(ND, 16))
                pool.sem_inc(pool_turn, 1)
                if not isinstance(k.i, int) or k.at >= NX:
                    pool.wait_ge(msg_ready, k.back(NX).uses())
                    pool.sem_inc(pool_turn, 1)
                for t in range(TG):
                    pool.indirect_dma_start(xl_rows[:, k.slot(NX), t, :], None, q["xl"][:, :],
                                            bass.IndirectOffsetOnAxis(ap=idx[b][:, t:t + 1], axis=0)
                                            ).then_inc(rows_gathered[k.slot(NX)], 16)
            steps(pool, G, PEEL, U, 0, body)

        @block.tensor
        def _(pe):
            ident = sb["ident"]

            def run(wins):
                def body(k, live):
                    if live(4):
                        g = k.back(4)
                        pe.wait_ge(msg_ready, g.uses())
                        pe.wait_ge(onehot_ready, g.uses())
                        at_least(pe, acc_steps, g.back(2 if wins == 1 else 1).uses(1, 1 + 2 * wins))
                        for t in range(TG):
                            to = sums_ps[:, g.slot(2), 0:HX] if wins == 1 else sums_ps[:, t // 2, t % 2 * 256:t % 2 * 256 + HX]
                            last = nc.tensor.matmul(to, onehot[:, g.slot(2), t, :], msg[:, g.slot(2), t, :, :].rearrange("p h o -> p (h o)"),
                                                    start=wins > 1 or t == 0, stop=wins > 1 or t == TG - 1)
                        last.then_inc(sums_ready, 1)
                    if live(3):
                        g = k.back(3)
                        pe.wait_ge(drop_ready, g.uses())
                        at_least(pe, exp_ready, g.back(1).uses(1, 2))
                        for t in range(TG):
                            nc.tensor.matmul(shift_ps[:, t * H:(t + 1) * H], stack[:, g.slot(2), t * P:(t + 1) * P], sb["less"][:, :], start=True, stop=True)
                        pe.wait_ge(first_loaded[g.slot(ND)], g.uses(ND, 16))
                        nc.tensor.matmul(shift_ps[:, TG * H:(TG + 1) * H], first_pos[:, g.slot(ND), :], drop_diag[:, g.slot(2), :],
                                         start=True, stop=True).then_inc(shift_ready, 1)
                    if live(2):
                        g = k.back(2)
                        pe.wait_ge(leaky_ready, g.uses())
                        at_least(pe, prefix_ready, g.back(1).uses())
                        nc.tensor.matmul(logit_ps[:, :], sb["att_block"][:, :], leaky[:, g.slot(2), :], start=True, stop=True).then_inc(logit_ready, 1)
                    if live(1):
                        g = k.back(1)
                        b = g.slot(ND)
                        pe.wait_ge(attr_loaded[b], g.uses(ND, 16))
                        at_least(pe, leaky_ready, g.back(2).uses())
                        nc.tensor.matmul(pre_ps[:, g.slot(2), :], sb["W_e"][:, :], attrT[:, b, :], start=True, stop=False)
                        pe.wait_ge(xr_loaded[b], g.uses(ND, 16 * wins))
                        pe.wait_ge(onehotT_ready, g.uses())
                        if wins == 1:
                            nc.tensor.matmul(pre_ps[:, g.slot(2), :], xr_win[0:NARROW, b, 0, :], onehotT[0:NARROW, g.slot(2), :], start=False, stop=False)
                        else:
                            for t in range(TG):
                                cols = slice(t * P, (t + 1) * P)
                                nc.tensor.matmul(pre_ps[:, g.slot(2), cols], xr_win[:, b, t, :], onehotT[:, g.slot(2), cols], start=False, stop=False)
                        pe.wait_ge(rows_gathered[g.slot(NX)], g.uses(NX, 16 * TG))
                        for t in range(TG):
                            last = nc.tensor.matmul(pre_ps[:, g.slot(2), t * P:(t + 1) * P], xl_rows[:, g.slot(NX), t, :], ident[:, :],
                                                    is_transpose=True, start=False, stop=t == TG - 1)
                        last.then_inc(pre_ready, 1)
                steps(pe, G, PEEL, U, TAIL, body)
            by_width(pe, sb["narrow"], run)

        @block.scalar
        def _(act):
            def run(wins):
                rows = NARROW if wins == 1 else P

                def body(k, live):
                    if live(3):
                        g = k.back(3)
                        act.wait_ge(shift_ready, g.uses())
                        at_least(act, sums_ready, g.back(2).uses())
                        nc.scalar.activation(msg[:, g.slot(2), :, :, O].rearrange("p t h -> p (t h)"), shift_ps[:, 0:TG * H], ACT.Exp).then_inc(exp_ready, 1)
                        at_least(act, acc_steps, g.back(2).uses(1, 1 + 2 * wins))
                        nc.scalar.activation(factor[:, g.slot(2), :], shift_ps[:, TG * H:(TG + 1) * H], ACT.Exp).then_inc(exp_ready, 1)
                    if live(2):
                        g = k.back(2)
                        act.wait_ge(logit_ready, g.uses())
                        at_least(act, shift_ready, g.back(2).uses())
                        nc.scalar.activation(stack[LOGITS:LOGITS + H, g.slot(2), :], logit_ps[:, :], ACT.Copy).then_inc(logit_copied, 1)
                    if live(1):
                        g = k.back(1)
                        act.wait_ge(pre_ready, g.uses())
                        at_least(act, leaky_ready, g.back(2).uses())
                        nc.scalar.activation(fifth[:, g.slot(2), :], pre_ps[:, g.slot(2), :], ACT.Copy, scale=0.2).then_inc(fifth_ready, 1)
                    if live(0):
                        s = k.slot(2)
                        act.wait_ge(rel_loaded[k.slot(ND)], k.uses(ND, 16))
                        at_least(act, onehotT_ready, k.back(2).uses())
                        nc.scalar.activation(distance[0:rows, s, :], rel[0:rows, k.slot(ND), :], ACT.Abs, bias=sb["minus_p"][0:rows, :]).then_inc(distance_ready, 1)
                        act.wait_ge(distance_ready, k.uses())
                        at_least(act, pre_ready, k.back(2).uses())
                        nc.scalar.activation(onehotT[0:rows, s, :], distance[0:rows, s, :], ACT.Relu, bias=sb["one"][0:rows, :], scale=-1.0).then_inc(onehotT_ready, 1)
                steps(act, G, PEEL, U, TAIL, body)
            by_width(act, sb["narrow"], run)

        @block.vector
        def _(dve):
            dve.memset(acc[:, :, :, :], 0.0).then_inc(zeroed, 1)
            dve.memset(stack[:, :, :], 0.0).then_inc(zeroed, 1)
            dve.memset(prefix[:, 1, :], -BIG).then_inc(zeroed, 1)
            dve.wait_ge(zeroed, 3)

            def run(wins):
                step_count = 1 + 2 * wins

                def body(k, live):
                    if live(3):
                        g = k.back(3)
                        at_least(dve, sums_ready, g.back(2).uses())
                        nc.vector.tensor_tensor(onehot[:, g.slot(2), :, :], bc(sb["iota"][:, :], 1, TG),
                                                bc(sb["dst_pos"][:, bass.ds(g.index(TG), TG)], 2, P), ALU.is_equal).then_inc(onehot_ready, 1)
                    if live(4):
                        g = k.back(4)
                        first = g.index(step_count)
                        for w in range(wins):
                            at = dve.value_load(sb["tile_block"][0:1, bass.ds(g.index(TG, w), 1)], min_val=0, max_val=BLOCKS - 2)
                            here, beyond = acc[:, bass.ds(at, 1), :, :].rearrange("p b h o -> p (b h o)"), acc[:, bass.ds(at + 1, 1), :, :].rearrange("p b h o -> p (b h o)")
                            sums = sums_ps[:, g.slot(2), 0:HX] if wins == 1 else sums_ps[:, w // 2, w % 2 * 256:w % 2 * 256 + HX]
                            if w == 0:
                                dve.wait_ge(exp_ready, g.uses(1, 2))
                                at_least(dve, acc_steps, first)
                                old = acc[:, bass.ds(at, 1), :, :].rearrange("p b h o -> p (b h) o")
                                nc.vector.tensor_tensor(old, old, bc(factor[:, g.slot(2), :], 2, OX), ALU.mult).then_inc(acc_steps, 1)
                                dve.wait_ge(sums_ready, g.uses())
                            tile_at = bass.ds(g.index(TG, w), 1)
                            dve.wait_ge(acc_steps, first + (1 + 2 * w))
                            nc.vector.scalar_tensor_tensor(out=here, in0=sums, scalar=sb["keep"][:, tile_at], in1=here,
                                                           op0=ALU.mult, op1=ALU.add).then_inc(acc_steps, 1)
                            nc.vector.scalar_tensor_tensor(out=beyond, in0=sums, scalar=sb["pass_on"][:, tile_at], in1=beyond,
                                                           op0=ALU.mult, op1=ALU.add).then_inc(acc_steps, 1)
                    if live(3):
                        g = k.back(3)
                        dve.wait_ge(exp_ready, g.uses(1, 2))
                        m = msg[:, g.slot(2), :, :, :].rearrange("p t h o -> p (t h) o")
                        nc.vector.tensor_tensor(m[:, :, 0:O], xl_rows[:, g.slot(NX), :, :].rearrange("p t (h o) -> p (t h) o", o=O),
                                                m[:, :, O:OX].broadcast_to([P, TG * H, O]), ALU.mult).then_inc(msg_ready, 1)
                    if live(2):
                        g = k.back(2)
                        b, s, before = g.slot(ND), g.slot(2), g.back(1).slot(2)
                        dve.wait_ge(limit_loaded[b], g.uses(ND, 16))
                        dve.wait_ge(logit_copied, g.uses())
                        at_least(dve, drop_made, g.back(1).uses())
                        nc.vector.tensor_tensor_scan(prefix[:, s, :], limit[:, b, 0:GE], logit_ps[:, :],
                                                     prefix[:, before, GE - 1:GE], ALU.min, ALU.max).then_inc(prefix_ready, 1)
                        dve.wait_ge(prefix_ready, g.uses())
                        at_least(dve, shift_ready, g.back(2).uses())
                        nc.vector.tensor_tensor_scan(stack[0:H, s, ::-1], limit[:, b, GE:0:-1], prefix[:, s, ::-1],
                                                     -BIG, ALU.min, ALU.max).then_inc(peak_ready, 1)
                        dve.wait_ge(peak_ready, g.uses())
                        nc.vector.tensor_scalar(drop[:, s, :], prefix[:, before, GE - 1:GE], stack[0:H, s, 0:1], 0.0,
                                                ALU.subtract, ALU.min).then_inc(drop_made, 1)
                        dve.wait_ge(drop_made, g.uses())
                        nc.vector.tensor_scalar(drop_diag[:, s, :], sb["ident"][0:H, 0:H], drop[:, s, :], None, ALU.mult).then_inc(drop_ready, 1)
                    if live(1):
                        g = k.back(1)
                        dve.wait_ge(fifth_ready, g.uses())
                        at_least(dve, logit_ready, g.back(2).uses())
                        nc.vector.tensor_tensor(leaky[:, g.slot(2), :], pre_ps[:, g.slot(2), :], fifth[:, g.slot(2), :], ALU.max).then_inc(leaky_ready, 1)
                steps(dve, G, PEEL, U, TAIL, body)
            by_width(dve, sb["narrow"], run)


def update_nodes(nc, sb, q, out, acc):
    with ExitStack() as ctx:
        def tile(name, shape, dt=F32):
            return ctx.enter_context(nc.sbuf_tensor("upd_" + name, shape, dt))

        def bank(name, shape):
            return ctx.enter_context(nc.psum_tensor("upd_" + name, shape, F32))

        def sem(name):
            return ctx.enter_context(nc.semaphore("upd_" + name))

        BN = NB * P
        x_rows = tile("x_rows", [P, 3, NB, D])
        x_bias = tile("x_bias", [P, 2, NB, D])
        h_bias = tile("h_bias", [P, 2, NB, D])
        y = tile("y", [P, NB, D])
        h = tile("h", [P, 2, NB, D])
        hT = tile("hT", [P, BN])
        hidden = tile("hidden", [P, FC, BN])
        v = tile("v", [P, NB, D])
        x2 = tile("x2", [P, 2, NB, D])
        x2T = tile("x2T", [P, BN])
        feat = tile("feat", [P, 2, NB, D])
        stats = tile("stats", [P, NB, 6])
        moments = tile("moments", [P, NB, 2])
        spread = tile("spread", [P, NB])
        rstd = tile("rstd", [P, NB])
        den = tile("den", [P, 2, NB, H])
        turn_ps = bank("turn_ps", [P, BN])
        hidden_ps = bank("hidden_ps", [P, 2, BN])
        ffn_ps = bank("ffn_ps", [P, NB, D])
        table_ps = bank("table_ps", [P, NB, 2 * D])
        x_loaded = [sem(f"x_loaded{b}") for b in range(3)]
        feat_stored = [sem(f"feat_stored{b}") for b in range(2)]
        x_bias_ready, h_bias_ready, h_ready, turned, turn_copied = sem("x_bias_ready"), sem("h_bias_ready"), sem("h_ready"), sem("turned"), sem("turn_copied")
        hidden_ready, gelu_ready, ffn_ready, x2_ready = sem("hidden_ready"), sem("gelu_ready"), sem("ffn_ready"), sem("x2_ready")
        table_ready, feat_ready, self_ready = sem("table_ready"), sem("feat_ready"), sem("self_ready")
        spread_ready, rstd_ready, chain1, chain2 = sem("spread_ready"), sem("rstd_ready"), sem("chain1"), sem("chain2")
        resid = sb["xT"][:, :].rearrange("p (t f) -> p t f", f=D)
        aggregate_turn = sem("aggregate_turn")
        LAGS = 2
        UN = 6
        PN = BATCHES % UN + UN
        block = ctx.enter_context(nc.Block())

        def nodes(table, k):
            return q[table][bass.ds(k.index(BN), BN), :].rearrange("(t p) f -> p t f", p=P)

        def norm_count(k, lag, nth):
            if lag == 0:
                return 1 if isinstance(k.i, int) and k.at == 0 else k.index(3, -1)
            if isinstance(k.i, int) and k.at == BATCHES:
                return 3 * BATCHES - 1 + nth
            return k.index(3, nth)

        def turns_before(g, kind):
            return g.index(2, kind)

        @block.sync
        def _(sp):
            def body(k, live):
                if live(0):
                    at_least(sp, x2_ready, k.back(3).uses())
                    sp.dma_start(x_rows[:, k.slot(3), :, :], nodes("x_pad", k)).then_inc(x_loaded[k.slot(3)], 16)
                if live(2):
                    g = k.back(2)
                    sp.wait_ge(feat_ready, g.uses())
                    sp.dma_start(nodes("feat", g), feat[:, g.slot(2), :, :]).then_inc(feat_stored[g.slot(2)], 16)
            steps(sp, BATCHES, PN, UN, LAGS, body)
            for b in range(2):
                sp.wait_ge(feat_stored[b], Step(BATCHES - 2 + (BATCHES - b) % 2).uses(2, 16))

        @block.gpsimd
        def _(pool):
            def body(k, live):
                if live(0):
                    s = k.slot(2)
                    pool.wait_ge(x_loaded[k.slot(3)], k.uses(3, 16))
                    at_least(pool, h_ready, k.back(2).uses())
                    nc.gpsimd.tensor_tensor(x_bias[:, s, :, :], x_rows[:, k.slot(3), :, :], bc(sb["b_att"][:, :], 1, NB), ALU.add).then_inc(x_bias_ready, 1)
                    pool.wait_ge(spread_ready, norm_count(k, 0, 0))
                    nc.gpsimd.tensor_tensor(rstd[:, :], spread[:, :], sb["minus_half"][:, :], ALU.pow).then_inc(rstd_ready, 1)
                    pool.wait_ge(h_ready, k.uses())
                    at_least(pool, x2_ready, k.back(2).uses())
                    nc.gpsimd.tensor_tensor(h_bias[:, s, :, :], h[:, s, :, :], bc(sb["b2"][:, :], 1, NB), ALU.add).then_inc(h_bias_ready, 1)
                if live(1):
                    for nth in range(2):
                        pool.wait_ge(spread_ready, norm_count(k, 1, nth))
                        nc.gpsimd.tensor_tensor(rstd[:, :], spread[:, :], sb["minus_half"][:, :], ALU.pow).then_inc(rstd_ready, 1)
            steps(pool, BATCHES, PN, UN, LAGS, body)

        @block.tensor
        def _(pe):
            ident = sb["ident"]

            def body(k, live):
                if live(2):
                    g = k.back(2)
                    pe.wait_ge(x2_ready, g.uses())
                    at_least(pe, turn_copied, turns_before(g, 1))
                    for t in range(NB):
                        last = nc.tensor.transpose(turn_ps[:, t * P:(t + 1) * P], x2[:, g.slot(2), t, :], ident[:, :])
                    last.then_inc(turned, 1)
                    pe.wait_ge(turn_copied, turns_before(g, 1) + 1)
                    at_least(pe, feat_ready, g.back(1).uses())
                    at_least(pe, self_ready, g.back(1).uses())
                    for t in range(NB):
                        last = nc.tensor.matmul(table_ps[:, t, :], x2T[:, t * P:(t + 1) * P], sb["W_feat"][:, :], start=True, stop=True)
                    last.then_inc(table_ready, 1)
                if live(1):
                    g = k.back(1)
                    pe.wait_ge(h_ready, g.uses())
                    at_least(pe, turn_copied, turns_before(g, 0))
                    for t in range(NB):
                        last = nc.tensor.transpose(turn_ps[:, t * P:(t + 1) * P], h[:, g.slot(2), t, :], ident[:, :])
                    last.then_inc(turned, 1)
                    pe.wait_ge(turn_copied, turns_before(g, 0) + 1)
                    for c in range(FC):
                        at_least(pe, gelu_ready, g.index(FC, c - 1))
                        nc.tensor.matmul(hidden_ps[:, c % 2, :], sb["W1"][:, c * P:(c + 1) * P], hT[:, :], start=True, stop=True).then_inc(hidden_ready, 1)
                    pe.wait_ge(gelu_ready, g.uses(1, FC))
                    at_least(pe, x2_ready, g.back(1).uses())
                    for t in range(NB):
                        for c in range(FC):
                            last = nc.tensor.matmul(ffn_ps[:, t, :], hidden[:, c, t * P:(t + 1) * P], sb["W2"][:, c, :], start=c == 0, stop=c == FC - 1)
                    last.then_inc(ffn_ready, 1)
            steps(pe, BATCHES, PN, UN, LAGS, body)

        @block.scalar
        def _(act):
            def body(k, live):
                if live(2):
                    g = k.back(2)
                    act.wait_ge(turned, turns_before(g, 1) + 1)
                    at_least(act, table_ready, g.back(1).uses())
                    nc.scalar.activation(x2T[:, :], turn_ps[:, :], ACT.Copy).then_inc(turn_copied, 1)
                    act.wait_ge(table_ready, g.uses())
                    at_least(act, feat_stored[g.slot(2)], g.back(2).uses(2, 16))
                    nc.scalar.activation(feat[:, g.slot(2), :, :], table_ps[:, :, 0:D], ACT.Copy, scale=FEAT_SCALE).then_inc(feat_ready, 1)
                if live(1):
                    g = k.back(1)
                    act.wait_ge(turned, turns_before(g, 0) + 1)
                    at_least(act, hidden_ready, g.index(FC))
                    nc.scalar.activation(hT[:, :], turn_ps[:, :], ACT.Copy).then_inc(turn_copied, 1)
                    at_least(act, ffn_ready, g.back(1).uses())
                    for c in range(FC):
                        act.wait_ge(hidden_ready, g.index(FC, c + 1))
                        nc.scalar.activation(hidden[:, c, :], hidden_ps[:, c % 2, :], ACT.Gelu, bias=sb["b1"][:, c:c + 1]).then_inc(gelu_ready, 1)
            steps(act, BATCHES, PN, UN, LAGS, body)

        @block.vector
        def _(dve):
            def linked(chain, start):
                made = [0]

                def link(ins):
                    made[0] += 1
                    ins.then_inc(chain, 1)
                    dve.wait_ge(chain, start + made[0])
                return link

            def normalise(link, to, of, k, lag, nth):
                for t in range(NB):
                    last = nc.vector.bn_stats(stats[:, t, :], of[:, t, :])
                link(last)
                dve.sem_inc(aggregate_turn, 1)
                for t in range(NB):
                    last = nc.vector.bn_aggr(moments[:, t, :], stats[:, t, :])
                link(last)
                nc.vector.tensor_scalar(spread[:, :], moments[:, :, 1], LN_EPS, None, ALU.add).then_inc(spread_ready, 1)
                dve.wait_ge(rstd_ready, norm_count(k, lag, nth))
                for t in range(NB):
                    last = nc.vector.tensor_scalar(to[:, t, :], of[:, t, :], moments[:, t, 0:1], rstd[:, t:t + 1], ALU.subtract, ALU.mult)
                return last

            def body(k, live):
                if live(0):
                    link = linked(chain1, k.index(8))
                    s = k.slot(2)
                    here = acc[:, bass.ds(k.index(NB), NB), :, :]
                    link(nc.vector.tensor_scalar(den[:, 0, :, :], here[:, :, :, O], 1e-16, None, ALU.add))
                    link(nc.vector.reciprocal(den[:, 1, :, :], den[:, 0, :, :]))
                    flat = here.rearrange("p t h o -> p (t h) o")[:, :, 0:O]
                    link(nc.vector.tensor_tensor(y[:, :, :].rearrange("p t (h o) -> p (t h) o", o=O), flat,
                                                 bc(den[:, 1, :, :].rearrange("p t h -> p (t h)"), 2, O), ALU.mult))
                    dve.wait_ge(x_bias_ready, k.uses())
                    link(nc.vector.tensor_tensor(y[:, :, :], y[:, :, :], x_bias[:, s, :, :], ALU.add))
                    at_least(dve, x2_ready, k.back(2).uses())
                    to = h[:, s, :, :]
                    link(normalise(link, to, y[:, :, :], k, 0, 0))
                    link(nc.vector.tensor_tensor(to, to, bc(sb["g1"][:, :], 1, NB), ALU.mult))
                    at_least(dve, h_bias_ready, k.back(2).uses())
                    nc.vector.tensor_tensor(to, to, bc(sb["be1"][:, :], 1, NB), ALU.add).then_inc(h_ready, 1)
                if live(1):
                    g = k.back(1)
                    s = g.slot(2)
                    link = linked(chain2, g.index(9))
                    dve.wait_ge(ffn_ready, g.uses())
                    dve.wait_ge(x_loaded[g.slot(3)], g.uses(3, 16))
                    to = v[:, :, :]
                    dve.wait_ge(h_bias_ready, g.uses())
                    link(nc.vector.tensor_tensor(to, ffn_ps[:, :, :], h_bias[:, s, :, :], ALU.add))
                    link(normalise(link, to, to, k, 1, 0))
                    link(nc.vector.tensor_tensor(to, to, bc(sb["g2"][:, :], 1, NB), ALU.mult))
                    link(nc.vector.tensor_tensor(to, to, bc(sb["be2"][:, :], 1, NB), ALU.add))
                    link(nc.vector.tensor_tensor(to, to, x_rows[:, g.slot(3), :, :], ALU.add))
                    at_least(dve, self_ready, g.back(2).uses())
                    normalise(link, x2[:, s, :, :], to, k, 1, 1).then_inc(x2_ready, 1)
                if live(2):
                    g = k.back(2)
                    dve.wait_ge(feat_ready, g.uses())
                    nc.vector.scalar_tensor_tensor(out=resid[:, bass.ds(g.index(NB), NB), :], in0=table_ps[:, :, D:2 * D], scalar=SELF_SCALE,
                                                   in1=x2[:, g.slot(2), :, :], op0=ALU.mult, op1=ALU.add).then_inc(self_ready, 1)
            steps(dve, BATCHES, PN, UN, LAGS, body)


def convolution(nc, sb, q, out, acc):
    with ExitStack() as ctx:
        def tile(name, shape, dt=F32):
            return ctx.enter_context(nc.sbuf_tensor("conv_" + name, shape, dt))

        def bank(name, shape):
            return ctx.enter_context(nc.psum_tensor("conv_" + name, shape, F32))

        def sem(name):
            return ctx.enter_context(nc.semaphore("conv_" + name))

        NX = 8
        ND = 4
        HE = GE // 2
        DX = 2 * D
        idx = [tile(f"idx{b}", [P, TG], I32) for b in range(ND)]
        rows = tile("rows", [P, NX, TG, D])
        radial = tile("radial", [2 * RADIAL, ND, HE])
        edge4 = tile("edge4", [P, T, 4])
        onehot = tile("onehot", [P, 2, TG, P])
        hid1 = tile("hid1", [2 * HID, 2, HE])
        hid2 = tile("hid2", [2 * HID, 2, HE])
        scaled = tile("scaled", [P, 2, TG, 2 * MUL])
        dots = tile("dots", [P, TG, 3, MUL])
        dot = tile("dot", [P, 2, TG, MUL])
        scal = tile("scal", [P, TG, MUL])
        vals = tile("vals", [P, 2, TG, DX])
        hid1_ps = bank("hid1_ps", [2 * HID, GE])
        hid2_ps = bank("hid2_ps", [2 * HID, GE])
        w_ps = bank("w_ps", [P, 2, TG, D])
        sums_ps = bank("sums_ps", [P, 2, GE])
        idx_loaded = [sem(f"idx_loaded{b}") for b in range(ND)]
        radial_loaded = [sem(f"radial_loaded{b}") for b in range(ND)]
        rows_gathered = [sem(f"rows_gathered{b}") for b in range(NX)]
        pool_turn, edge4_loaded, zeroed = sem("pool_turn"), sem("edge4_loaded"), sem("zeroed")
        onehot_ready, hid1_ready, gelu1_ready, hid2_ready, gelu2_ready = sem("onehot_ready"), sem("hid1_ready"), sem("gelu1_ready"), sem("hid2_ready"), sem("gelu2_ready")
        w_ready, scaled_ready, products, vals_ready = sem("w_ready"), sem("scaled_ready"), sem("products"), sem("vals_ready")
        sums_ready, acc_steps = sem("sums_ready"), sem("acc_steps")
        TAIL = 5
        PRODUCTS = 5
        block = ctx.enter_context(nc.Block())

        @block.sync
        def _(sp):
            sp.dma_start(edge4[:, :, :], q["edge4_tiles"].rearrange("p (t c) -> p t c", c=4)).then_inc(edge4_loaded, 16)

            def body(k, live):
                if not live(0):
                    return
                b = k.slot(ND)
                at_least(sp, rows_gathered[k.back(ND).slot(NX)], k.back(ND).uses(NX, 16 * TG))
                sp.dma_start(idx[b][:, :], q["src_tiles"][:, bass.ds(k.index(TG), TG)]).then_inc(idx_loaded[b], 16)
                at_least(sp, hid1_ready, k.back(ND).uses())
                for half in range(2):
                    sp.dma_start(radial[half * RADIAL:(half + 1) * RADIAL, b, :],
                                 q["radialT"][:, bass.ds(k.index(GE, half * HE), HE)]).then_inc(radial_loaded[b], 16)
            steps(sp, G, PEEL, U, 0, body)

        @block.gpsimd
        def _(pool):
            def body(k, live):
                if not live(0):
                    return
                b = k.slot(ND)
                pool.wait_ge(idx_loaded[b], k.uses(ND, 16))
                pool.sem_inc(pool_turn, 1)
                if not isinstance(k.i, int) or k.at >= NX:
                    pool.wait_ge(vals_ready, k.back(NX).uses())
                    pool.sem_inc(pool_turn, 1)
                for t in range(TG):
                    pool.indirect_dma_start(rows[:, k.slot(NX), t, :], None, q["feat"][:, :],
                                            bass.IndirectOffsetOnAxis(ap=idx[b][:, t:t + 1], axis=0)
                                            ).then_inc(rows_gathered[k.slot(NX)], 16)
            steps(pool, G, PEEL, U, 0, body)

        @block.tensor
        def _(pe):
            def run(wins):
                def body(k, live):
                    if live(4):
                        g = k.back(4)
                        pe.wait_ge(vals_ready, g.uses())
                        pe.wait_ge(onehot_ready, g.uses())
                        at_least(pe, acc_steps, g.back(2 if wins == 1 else 1).uses(1, 2 * wins))
                        for t in range(TG):
                            to = sums_ps[:, g.slot(2), 0:DX] if wins == 1 else sums_ps[:, t // 2, t % 2 * DX:(t % 2 + 1) * DX]
                            last = nc.tensor.matmul(to, onehot[:, g.slot(2), t, :], vals[:, g.slot(2), t, :], start=wins > 1 or t == 0, stop=wins > 1 or t == TG - 1)
                        last.then_inc(sums_ready, 1)
                    if live(2):
                        g = k.back(2)
                        pe.wait_ge(gelu2_ready, g.uses())
                        at_least(pe, vals_ready, g.back(2).uses())
                        for c in range(2):
                            last = nc.tensor.matmul(w_ps[:, g.slot(2), c:TG:2, :], hid2[:, g.slot(2), c * P:(c + 1) * P], sb["Wp"][:, :, :], start=True, stop=True)
                        last.then_inc(w_ready, 1)
                    if live(1):
                        g = k.back(1)
                        pe.wait_ge(gelu1_ready, g.uses())
                        at_least(pe, gelu2_ready, g.back(1).uses())
                        nc.tensor.matmul(hid2_ps[:, 0:HE], sb["mlp2"][:, :], hid1[:, g.slot(2), :], start=True, stop=True).then_inc(hid2_ready, 1)
                    if live(0):
                        pe.wait_ge(radial_loaded[k.slot(ND)], k.uses(ND, 32))
                        at_least(pe, gelu1_ready, k.back(1).uses())
                        nc.tensor.matmul(hid1_ps[:, 0:HE], sb["mlp1"][:, :], radial[:, k.slot(ND), :], start=True, stop=True).then_inc(hid1_ready, 1)
                steps(pe, G, PEEL, U, TAIL, body)
            by_width(pe, sb["narrow"], run)

        @block.scalar
        def _(act):
            act.wait_ge(edge4_loaded, 16)

            def body(k, live):
                if live(2):
                    g = k.back(2)
                    act.wait_ge(w_ready, g.uses())
                    at_least(act, vals_ready, g.back(2).uses())
                    for t in range(TG):
                        nc.scalar.activation(scaled[:, g.slot(2), t, :], w_ps[:, g.slot(2), t, 0:2 * MUL], ACT.Copy,
                                             scale=edge4[:, bass.ds(g.index(TG, t), 1), 0:1].rearrange("p t c -> p (t c)")).then_inc(scaled_ready, 1)
                if live(1):
                    g = k.back(1)
                    act.wait_ge(hid2_ready, g.uses())
                    at_least(act, w_ready, g.back(2).uses())
                    nc.scalar.activation(hid2[:, g.slot(2), :], hid2_ps[:, 0:HE], ACT.Gelu_apprx_tanh, scale=1.0 / float(np.sqrt(HID))).then_inc(gelu2_ready, 1)
                if live(0):
                    act.wait_ge(hid1_ready, k.uses())
                    at_least(act, hid2_ready, k.back(2).uses())
                    nc.scalar.activation(hid1[:, k.slot(2), :], hid1_ps[:, 0:HE], ACT.Gelu_apprx_tanh, scale=1.0 / float(np.sqrt(RADIAL))).then_inc(gelu1_ready, 1)
            steps(act, G, PEEL, U, TAIL, body)

        @block.vector
        def _(dve):
            dve.memset(acc[:, :, :], 0.0).then_inc(zeroed, 1)
            dve.wait_ge(zeroed, 1)
            dve.wait_ge(edge4_loaded, 16)

            def run(wins):
                def body(k, live):
                    if live(3):
                        g = k.back(3)
                        at_least(dve, sums_ready, g.back(2).uses())
                        nc.vector.tensor_tensor(onehot[:, g.slot(2), :, :], bc(sb["iota"][:, :], 1, TG),
                                                bc(sb["dst_pos"][:, bass.ds(g.index(TG), TG)], 2, P), ALU.is_equal).then_inc(onehot_ready, 1)
                    if live(5):
                        g = k.back(5)
                        first = g.index(2 * wins)
                        for w in range(wins):
                            at = dve.value_load(sb["tile_block"][0:1, bass.ds(g.index(TG, w), 1)], min_val=0, max_val=BLOCKS - 2)
                            here, beyond = acc[:, bass.ds(at, 1), :].rearrange("p b f -> p (b f)"), acc[:, bass.ds(at + 1, 1), :].rearrange("p b f -> p (b f)")
                            sums = sums_ps[:, g.slot(2), 0:DX] if wins == 1 else sums_ps[:, w // 2, w % 2 * DX:(w % 2 + 1) * DX]
                            tile_at = bass.ds(g.index(TG, w), 1)
                            if w == 0:
                                dve.wait_ge(sums_ready, g.uses())
                            at_least(dve, acc_steps, first + 2 * w if w else first)
                            nc.vector.scalar_tensor_tensor(out=here, in0=sums, scalar=sb["keep"][:, tile_at], in1=here,
                                                           op0=ALU.mult, op1=ALU.add).then_inc(acc_steps, 1)
                            nc.vector.scalar_tensor_tensor(out=beyond, in0=sums, scalar=sb["pass_on"][:, tile_at], in1=beyond,
                                                           op0=ALU.mult, op1=ALU.add).then_inc(acc_steps, 1)
                    if live(3):
                        g = k.back(3)
                        s = g.slot(2)
                        r = rows[:, g.slot(NX), :, :]
                        e0 = r[:, :, 0:MUL]
                        e1 = r[:, :, MUL:D].rearrange("p t (c w) -> p t c w", c=3)
                        a1 = bc(edge4[:, bass.ds(g.index(TG), TG), 1:4], 3, MUL)
                        to, w = vals[:, s, :, :], w_ps[:, s, :, :]
                        at_least(dve, vals_ready, g.back(1).uses())
                        dve.wait_ge(rows_gathered[g.slot(NX)], g.uses(NX, 16 * TG))
                        nc.vector.tensor_tensor(dots[:, :, :, :], e1, a1, ALU.mult).then_inc(products, 1)
                        dve.wait_ge(scaled_ready, g.uses(1, TG))
                        nc.vector.tensor_tensor(scal[:, :, :], w[:, :, 2 * MUL:3 * MUL], e0, ALU.mult).then_inc(products, 1)
                        dve.wait_ge(products, g.index(PRODUCTS, 1))
                        nc.vector.tensor_tensor(dot[:, 0, :, :], dots[:, :, 0, :], dots[:, :, 1, :], ALU.add).then_inc(products, 1)
                        nc.vector.tensor_tensor(to[:, :, 0:MUL], scaled[:, s, :, 0:MUL], e0, ALU.mult)
                        dve.wait_ge(products, g.index(PRODUCTS, 3))
                        nc.vector.tensor_tensor(dot[:, 1, :, :], dot[:, 0, :, :], dots[:, :, 2, :], ALU.add).then_inc(products, 1)
                        nc.vector.tensor_tensor(to[:, :, MUL:D].rearrange("p t (c w) -> p t c w", c=3), e1, bc(scaled[:, s, :, MUL:2 * MUL], 2, 3), ALU.mult)
                        nc.vector.tensor_tensor(to[:, :, D:D + V3].rearrange("p t (c w) -> p t c w", c=3), bc(scal[:, :, :], 2, 3), a1, ALU.mult).then_inc(products, 1)
                        dve.wait_ge(products, g.index(PRODUCTS, 4))
                        nc.vector.tensor_tensor(to[:, :, D + V3:DX], dot[:, 1, :, :], w[:, :, 3 * MUL:4 * MUL], ALU.mult).then_inc(vals_ready, 1)
                steps(dve, G, PEEL, U, TAIL, body)
            by_width(dve, sb["narrow"], run)


def finish_nodes(nc, sb, q, out, acc):
    with ExitStack() as ctx:
        def tile(name, shape, dt=F32):
            return ctx.enter_context(nc.sbuf_tensor("fin_" + name, shape, dt))

        def bank(name, shape):
            return ctx.enter_context(nc.psum_tensor("fin_" + name, shape, F32))

        def sem(name):
            return ctx.enter_context(nc.semaphore("fin_" + name))

        FULL = N // (NB * P)
        REST = N - FULL * NB * P
        USED = FULL + 1
        UN = 2
        PN = USED % UN + 2 * UN
        sumT_ps = bank("sumT_ps", [P, 2, NB, P])
        conv_ps = bank("conv_ps", [P, 2, NB, D])
        sumT = tile("sumT", [P, 2, 2, NB, P])
        v = tile("v", [P, 2, NB, D])
        done = tile("done", [P, 2, NB, D])
        stats = tile("stats", [P, NB, 6])
        moments = tile("moments", [P, NB, 2])
        spread = tile("spread", [P, NB])
        rstd = tile("rstd", [P, NB])
        turned, turn_copied, aggregate_turn = sem("turned"), sem("turn_copied"), sem("aggregate_turn")
        conv_ready, v_ready, spread_ready, rstd_ready = sem("conv_ready"), sem("v_ready"), sem("spread_ready"), sem("rstd_ready")
        done_ready, chain = sem("done_ready"), sem("chain")
        stored = [sem(f"stored{b}") for b in range(2)]
        block = ctx.enter_context(nc.Block())
        resid = sb["xT"][:, :].rearrange("p (t f) -> p t f", f=D)

        @block.tensor
        def _(pe):
            def conv(n):
                pe.wait_ge(turn_copied, n + 1)
                at_least(pe, v_ready, n - 1)
                for t in range(NB):
                    nc.tensor.matmul(conv_ps[:, n % 2, t, :], sumT[:, n % 2, 0, t, :], sb["W_convA"][:, :], start=True, stop=False)
                    last = nc.tensor.matmul(conv_ps[:, n % 2, t, :], sumT[:, n % 2, 1, t, :], sb["W_convB"][:, :], start=False, stop=True)
                last.then_inc(conv_ready, 1)

            for n in range(USED):
                at_least(pe, turn_copied, n)
                for part in range(2):
                    for t in range(NB):
                        last = nc.tensor.transpose(sumT_ps[:, part, t, :], acc[:, n * NB + t, part * D:(part + 1) * D], sb["ident"][:, :])
                last.then_inc(turned, 1)
                if n:
                    conv(n - 1)
            conv(USED - 1)

        @block.scalar
        def _(act):
            def body(k, live):
                if not live(0):
                    return
                act.wait_ge(turned, k.uses())
                at_least(act, conv_ready, k.back(2).uses())
                nc.scalar.activation(sumT[:, k.slot(2), :, :, :], sumT_ps[:, :, :, :], ACT.Copy).then_inc(turn_copied, 1)
            steps(act, USED, PN, UN, 0, body)

        @block.gpsimd
        def _(pool):
            def body(k, live):
                if not live(0):
                    return
                pool.wait_ge(spread_ready, k.uses())
                nc.gpsimd.tensor_tensor(rstd[:, :], spread[:, :], sb["minus_half"][:, :], ALU.pow).then_inc(rstd_ready, 1)
            steps(pool, USED, PN, UN, 0, body)

        @block.vector
        def _(dve):
            def body(k, live):
                if not live(0):
                    return
                s = k.slot(2)
                dve.wait_ge(conv_ready, k.uses())
                at_least(dve, done_ready, k.back(1).uses())
                nc.vector.tensor_tensor(v[:, s, :, :], conv_ps[:, s, :, :], resid[:, bass.ds(k.index(NB), NB), :], ALU.add).then_inc(v_ready, 1)
                dve.wait_ge(v_ready, k.uses())
                for t in range(NB):
                    last = nc.vector.bn_stats(stats[:, t, :], v[:, s, t, :])
                last.then_inc(chain, 1)
                dve.wait_ge(chain, k.index(2, 1))
                dve.sem_inc(aggregate_turn, 1)
                for t in range(NB):
                    last = nc.vector.bn_aggr(moments[:, t, :], stats[:, t, :])
                last.then_inc(chain, 1)
                dve.wait_ge(chain, k.index(2, 2))
                nc.vector.tensor_scalar(spread[:, :], moments[:, :, 1], LN_EPS, None, ALU.add).then_inc(spread_ready, 1)
                dve.wait_ge(rstd_ready, k.uses())
                at_least(dve, stored[s], k.back(2).uses(2, 16))
                for t in range(NB):
                    last = nc.vector.tensor_scalar(done[:, s, t, :], v[:, s, t, :], moments[:, t, 0:1], rstd[:, t:t + 1], ALU.subtract, ALU.mult)
                last.then_inc(done_ready, 1)
            steps(dve, USED, PN, UN, 0, body)

        @block.sync
        def _(sp):
            def body(k, live):
                if not live(0):
                    return
                sp.wait_ge(done_ready, k.uses())
                sp.dma_start(out[bass.ds(k.index(NB * P), NB * P), :].rearrange("(t p) f -> p t f", p=P), done[:, k.slot(2), :, :]).then_inc(stored[k.slot(2)], 16)
            steps(sp, FULL, FULL % UN + UN, UN, 0, body)
            sp.wait_ge(done_ready, USED)
            pieces = 0
            for t in range(NB):
                n = min(P, REST - t * P)
                if n > 0:
                    lo = FULL * NB * P + t * P
                    sp.dma_start(out[lo:lo + n, :], done[0:n, FULL % 2, t, :]).then_inc(stored[FULL % 2], 16)
                    pieces += 1
            for b in range(2):
                whole = (FULL - b + 1) // 2 * 16
                sp.wait_ge(stored[b], whole + (pieces * 16 if b == FULL % 2 else 0))


def program(nc, q, out):
    with ExitStack() as ctx:
        def tile(name, shape, dt=F32):
            return ctx.enter_context(nc.sbuf_tensor(name, shape, dt))

        sb = {}
        for name, shape in (("W_lr", [P, 2 * D]), ("W_e", [P, D]), ("W1", [P, FF]), ("W2", [P, FC, D]), ("b1", [P, FC]), ("b_att", [P, D]),
                            ("b_lr", [P, 2 * D]), ("b2", [P, D]), ("g1", [P, D]), ("be1", [P, D]), ("g2", [P, D]), ("be2", [P, D]),
                            ("mlp1", [2 * RADIAL, 2 * HID]), ("mlp2", [2 * HID, 2 * HID]), ("Wp", [2 * HID, 2, D]), ("W_feat", [P, 2 * D]),
                            ("W_convA", [P, D]), ("W_convB", [P, D]), ("ident", [P, P]), ("less", [32 + H, H]), ("att_block", [P, H]),
                            ("iota", [P, P]), ("minus_half", [P, NB]), ("one", [P, 1]), ("minus_p", [P, 1]),
                            ("dst_pos", [P, T]), ("keep", [P, T]), ("pass_on", [P, T]),
                            ("xT", [P, N_PAD])):
            sb[name] = tile("c_" + name, shape)
        for name, n in (("tile_base", T), ("tile_pos", T), ("tile_block", T), ("narrow", 1)):
            sb[name] = tile("c_" + name, [1, n], I32)
        constants(nc, sb, q, out)
        project_nodes(nc, sb, q, out)
        with nc.sbuf_tensor("c_acc_attn", [P, BLOCKS, H, OX], F32) as acc:
            attention(nc, sb, q, out, acc)
            update_nodes(nc, sb, q, out, acc)
        with nc.sbuf_tensor("c_acc_conv", [P, BLOCKS, 2 * D], F32) as acc:
            convolution(nc, sb, q, out, acc)
            finish_nodes(nc, sb, q, out, acc)


def kernel(**inputs):
    import concourse.bacc as bacc
    from concourse.bass_utils import run_bass_kernel_spmd as run

    a = {k: np.asarray(v) for k, v in inputs.items()}

    def padded(x, n, value=0):
        return np.concatenate([x, np.full((n - x.shape[0],) + x.shape[1:], value, x.dtype)])

    dst = padded(a["dst"], E_PAD, N)
    x_pad = padded(a["x"], N_PAD)
    arrays = {k: np.ascontiguousarray(v) for k, v in a.items()
              if k.startswith("L") and k != "L0_gnn_b1"}
    arrays |= {
        "x_pad": x_pad,
        "xT": np.ascontiguousarray(x_pad.T),
        "b1_columns": np.ascontiguousarray(a["L0_gnn_b1"].reshape(FC, P).T),
        "src_tiles": np.ascontiguousarray(padded(a["src"], E_PAD).reshape(T, P).T),
        "dst_tiles": np.ascontiguousarray(dst.reshape(T, P).T),
        "dst_line": np.concatenate([np.full((1,), -1, dst.dtype), dst]),
        "attrT": np.ascontiguousarray(padded(a["edge_attr_128"], E_PAD).T),
        "radialT": np.ascontiguousarray(padded(a["edge_attr_8"], E_PAD).T),
        "edge4_tiles": np.ascontiguousarray(padded(a["edge_attr_4"], E_PAD).reshape(T, P, 4).transpose(1, 0, 2)).reshape(P, T * 4),
    }
    nc = bacc.Bacc("TRN2", target_bir_lowering=False, num_devices=1)
    q = {k: nc.dram_tensor("in_" + k, v.shape, mybir.dt.from_np(v.dtype), kind="ExternalInput").ap() for k, v in arrays.items()}
    for name, shape in (("xl", (N_PAD, D)), ("xr", (N_PAD, D)), ("feat", (N_PAD, D)), ("limit", (E_PAD + 1,)),
                        ("rel_group", (E_PAD,)), ("rel_tile", (E_PAD,)), ("ident_rows", (P, P))):
        q[name] = nc.dram_tensor(name, shape, F32).ap()
    out = nc.dram_tensor("out", (N, D), F32, kind="ExternalOutput").ap()
    program(nc, q, out)
    return run(nc, [{"in_" + k: v for k, v in arrays.items()}], core_ids=[0]).results[0]["out"]
```

```python
import numpy as np
from contextlib import ExitStack
import concourse.bass as bass
from concourse import mybir

F32 = mybir.dt.float32
BF16 = mybir.dt.bfloat16
I32 = mybir.dt.int32
ALU = mybir.AluOpType
ACT = mybir.ActivationFunctionType

P = 128
N, E, D, H = 6250, 206250, 128, 8
O = D // H
OX = O + 1
FF = 4 * D
FC = FF // P
MUL, RADIAL, HID = 32, 8, 64
V3 = 3 * MUL
TG = 4
GE = TG * P
G = -(-E // GE)
T = G * TG
E_PAD = G * GE
LINES = max(n for n in range(1, P + 1) if T % n == 0)
TL = T // LINES
NB = 4
BATCHES = -(-(N + P) // (NB * P))
N_PAD = BATCHES * NB * P
BLOCKS = BATCHES * NB + 1
PARTS = 3
NARROW = P // PARTS
U = 8
PEEL = G % U + U
BIG = 1e30
LN_EPS = 1e-5
NODE_ROWS = ("b_att", "b2", "g1", "be1", "g2", "be2")
MIX_C, MIX_S = float(np.cos(np.pi / 8)), float(np.sin(np.pi / 8))
SELF_SCALE = MIX_C / float(np.sqrt(MUL))
FEAT_SCALE = 1.0 / float(np.sqrt(MUL))
CONV_SCALE = MIX_S / float(np.sqrt(2 * MUL) * np.sqrt(32.0) * np.sqrt(2.0))
CONV_SCALE_B = CONV_SCALE / float(np.sqrt(3.0))


class Step:

    def __init__(self, at, i=0, stride=U):
        self.at, self.i, self.stride = at, i, stride

    def back(self, n):
        return Step(self.at - n, self.i, self.stride)

    def index(self, scale=1, plus=0):
        base = self.at * scale + plus
        return base if isinstance(self.i, int) else self.i * (self.stride * scale) + base

    def uses(self, n=1, by=1):
        base = (self.at // n + 1) * by
        return base if isinstance(self.i, int) else self.i * (self.stride // n * by) + base

    def slot(self, n):
        return self.at % n


def at_least(eng, sem, value):
    if not isinstance(value, int) or value > 0:
        eng.wait_ge(sem, value)


def steps(eng, total, peel, unroll, tail, body):
    for k in range(peel):
        body(Step(k, 0, unroll), lambda lag, k=k: 0 <= k - lag < total)
    with eng.Fori(0, (total - peel) // unroll) as i:
        for u in range(unroll):
            body(Step(peel + u, i, unroll), lambda lag: True)
    for k in range(total, total + tail):
        body(Step(k, 0, unroll), lambda lag, k=k: 0 <= k - lag < total)


def by_width(eng, narrow, run):
    flag = eng.value_load(narrow[0:1, 0:1], min_val=0, max_val=1)
    with eng.If(flag > 0):
        run(1)
    with eng.Else():
        run(TG)


def bc(ap, axis, n):
    ap = ap.unsqueeze(axis)
    shape = list(ap.shape)
    shape[axis] = n
    return ap.broadcast_to(shape)


def set_up(nc, sb, q, out):
    with ExitStack() as ctx:
        def tile(name, shape, dt=F32):
            return ctx.enter_context(nc.sbuf_tensor("set_" + name, shape, dt))

        def sem(name):
            return ctx.enter_context(nc.semaphore("set_" + name))

        X_CHUNK = 4
        rows = tile("rows", [P, 4, NB, 2 * D])
        parts = tile("parts", [P, 4, NB, PARTS, D], BF16)
        rest = tile("rest", [P, 2, NB, D])
        proj = ctx.enter_context(nc.psum_tensor("set_proj", [P, 4, NB, 2 * D], F32))
        x_loaded = [sem(f"x_loaded{c}") for c in range(-(-BATCHES // X_CHUNK))]
        weights_loaded, projected, rows_ready, rest_ready = sem("weights_loaded"), sem("projected"), sem("rows_ready"), sem("rest_ready")
        high_ready, mid_ready, parts_ready = sem("high_ready"), sem("mid_ready"), sem("parts_ready")
        xl_stored = [sem(f"xl_stored{b}") for b in range(4)]
        parts_stored = [sem(f"parts_stored{b}") for b in range(4)]
        UN = 4
        PN = BATCHES % UN + UN
        dst_tiles, base_all = tile("dst_tiles", [P, T], I32), tile("base_all", [P, T], I32)
        limit_sb, last_limit = tile("limit_sb", [LINES, TL * P]), tile("last_limit", [1, 1])
        lines, group_base = tile("lines", [LINES, 1 + TL * P], I32), tile("group_base", [LINES, TL], I32)
        rel_lines = tile("rel_lines", [LINES, 2, TL, P], BF16)
        tile_last, span, widest = tile("tile_last", [1, T], I32), tile("span", [1, G]), tile("widest", [1, 1])
        iota_i, p_i = tile("iota_i", [P, P], I32), tile("p_i", [P, 1], I32)
        att_col = tile("att_col", [P, 1])
        consts_loaded, later_loaded, masks, chain = sem("consts_loaded"), sem("later_loaded"), sem("masks"), sem("chain")
        limits_ready, limits_stored, rel_ready, rel_stored = sem("limits_ready"), sem("limits_stored"), sem("rel_ready"), sem("rel_stored")
        block = ctx.enter_context(nc.Block())

        def nodes(table, k):
            return q[table][bass.ds(k.index(NB * P), NB * P), :].rearrange("(t p) f -> p t f", p=P)

        def in_each(name):
            return q[name].rearrange("(a n) -> a n", a=1).partition_broadcast(P).rearrange("p a n -> p (a n)")

        loads = [(dst_tiles[:, :], q["dst_tiles"]),
                 (base_all[:, :], q["dst_tiles"][0:1, :].partition_broadcast(P).rearrange("p a n -> p (a n)")),
                 (lines[:, :], q["dst_lines"]),
                 (group_base[:, :], q["group_base"]),
                 (sb["tile_base"][:, :], q["dst_tiles"][0:1, :]),
                 (tile_last[:, :], q["dst_tiles"][P - 1:P, :]),
                 (att_col[:, :], q["L0_gnn_att"].rearrange("h o -> (h o)").rearrange("(p a) -> p a", a=1)),
                 (sb["window_row"][:, :], q["window_row"]),
                 (sb["W_e"][:, :], q["L0_gnn_W_e"])]
        later = [(sb["W1"][:, :], q["L0_gnn_W1"]),
                 (sb["W2"][:, :, :], q["L0_gnn_W2"].rearrange("(c p) n -> p c n", p=P)),
                 (sb["b1"][:, :], q["b1_columns"]),
                 (sb["norm_columns"][:, :], q["norm_columns"]),
                 (sb["node_rows"][:, :], in_each("node_rows")),
                 (sb["Wp"][:, :, :], q["Wp"].rearrange("p (a n) -> p a n", a=2))]
        later += [(sb[name][:, :], q[name]) for name in ("mlp1", "mlp2", "W_feat", "W_convA", "W_convB")]

        @block.sync
        def _(sp):
            sp.dma_start(sb["W_lr"][:, 0:D], q["L0_gnn_W_l"]).then_inc(weights_loaded, 16)
            sp.dma_start(sb["W_lr"][:, D:2 * D], q["L0_gnn_W_r"]).then_inc(weights_loaded, 16)
            for c, loaded in enumerate(x_loaded):
                cols = slice(c * X_CHUNK * NB * P, min((c + 1) * X_CHUNK * NB * P, N_PAD))
                sp.dma_start(sb["xT"][:, cols], q["xT"][:, cols]).then_inc(loaded, 16)
                if c == 0:
                    sp.dma_start(sb["b_lr"][:, 0:D], in_each("L0_gnn_b_l")).then_inc(weights_loaded, 16)
                    sp.dma_start(sb["b_lr"][:, D:2 * D], in_each("L0_gnn_b_r")).then_inc(weights_loaded, 16)
            for to, of in loads:
                sp.dma_start(to, of).then_inc(consts_loaded, 16)

            def body(k, live):
                if live(0):
                    sp.wait_ge(rows_ready, k.uses())
                    sp.dma_start(nodes("xl", k), rows[:, k.slot(4), :, 0:D]).then_inc(xl_stored[k.slot(4)], 16)
                if live(2):
                    g = k.back(2)
                    sp.wait_ge(parts_ready, g.uses())
                    sp.dma_start(nodes("xr_parts", g), parts[:, g.slot(4), :, :, :].rearrange("p t c f -> p t (c f)")).then_inc(parts_stored[g.slot(4)], 16)
            steps(sp, BATCHES, PN, UN, 2, body)
            for to, of in later:
                sp.dma_start(to, of).then_inc(later_loaded, 16)
            for nth, table in enumerate(("rel_group", "rel_tile")):
                sp.wait_ge(rel_ready, nth + 1)
                sp.dma_start(q[table].rearrange("(p t e) -> p t e", p=LINES, e=P), rel_lines[:, nth, :, :]).then_inc(rel_stored, 16)
            sp.wait_ge(limits_ready, 2)
            sp.dma_start(q["limit"][0:E_PAD].rearrange("(p n) -> p n", p=LINES), limit_sb[:, :]).then_inc(limits_stored, 16)
            sp.dma_start(q["limit"][E_PAD:E_PAD + 1].rearrange("(a n) -> a n", a=1), last_limit[:, :]).then_inc(limits_stored, 16)
            for b in range(4):
                sp.wait_ge(xl_stored[b], 16 * len(range(b, BATCHES, 4)))
                sp.wait_ge(parts_stored[b], 16 * len(range(b, BATCHES, 4)))
            sp.wait_ge(limits_stored, 32)
            sp.wait_ge(rel_stored, 32)

        @block.tensor
        def _(pe):
            pe.wait_ge(weights_loaded, 64)
            for n in range(BATCHES):
                if n % X_CHUNK == 0:
                    pe.wait_ge(x_loaded[n // X_CHUNK], 16)
                at_least(pe, rows_ready, n - 3)
                for t in range(NB):
                    last = nc.tensor.matmul(proj[:, n % 4, t, :], sb["xT"][:, (n * NB + t) * P:(n * NB + t + 1) * P], sb["W_lr"][:, :], start=True, stop=True)
                last.then_inc(projected, 1)

        @block.scalar
        def _(act):
            def body(k, live):
                if live(0):
                    act.wait_ge(rows_ready, k.uses())
                    at_least(act, parts_stored[k.slot(4)], k.back(4).uses(4, 16))
                    nc.scalar.activation(parts[:, k.slot(4), :, 0, :], rows[:, k.slot(4), :, D:2 * D], ACT.Copy).then_inc(high_ready, 1)
                if live(1):
                    g = k.back(1)
                    act.wait_ge(rest_ready, g.uses())
                    nc.scalar.activation(parts[:, g.slot(4), :, 1, :], rest[:, g.slot(2), :, :], ACT.Copy).then_inc(mid_ready, 1)
            steps(act, BATCHES, PN, UN, 2, body)

        @block.gpsimd
        def _(pool):
            pool.memset(sb["ident"][:, :], 0.0).then_inc(masks, 1)
            pool.memset(sb["att_block"][:, :], 1.0).then_inc(masks, 1)
            pool.iota(p_i[:, :], pattern=[[0, 1]], base=0, channel_multiplier=1).then_inc(masks, 1)
            pool.iota(iota_i[:, :], pattern=[[1, P]], base=0, channel_multiplier=0).then_inc(masks, 1)
            pool.wait_ge(masks, 4)
            pool.affine_select(out=sb["ident"][:, :], in_=sb["ident"][:, :], compare_op=ALU.not_equal, fill=1.0,
                               base=0, pattern=[[-1, P]], channel_multiplier=1).then_inc(masks, 1)
            pool.affine_select(out=sb["att_block"][:, :], in_=sb["att_block"][:, :], compare_op=ALU.is_ge, fill=0.0,
                               base=0, pattern=[[-O, H]], channel_multiplier=1).then_inc(masks, 1)
            pool.wait_ge(masks, 6)
            pool.affine_select(out=sb["att_block"][:, :], in_=sb["att_block"][:, :], compare_op=ALU.is_ge, fill=0.0,
                               base=O - 1, pattern=[[O, H]], channel_multiplier=-1).then_inc(masks, 1)

            def body(k, live):
                if live(1):
                    g = k.back(1)
                    pool.wait_ge(mid_ready, g.uses())
                    nc.gpsimd.tensor_tensor(parts[:, g.slot(4), :, 2, :], rest[:, g.slot(2), :, :], parts[:, g.slot(4), :, 1, :], ALU.subtract).then_inc(parts_ready, 1)
            steps(pool, BATCHES, PN, UN, 1, body)

        @block.vector
        def _(dve):
            dve.memset(last_limit[:, :], -BIG).then_inc(limits_ready, 1)
            dve.memset(sb["minus_half"][:, :], -0.5)
            dve.memset(sb["one"][:, :], 1.0)
            dve.wait_ge(masks, 7)
            dve.tensor_copy(sb["iota"][:, :], iota_i[:, :])
            dve.tensor_copy(sb["row"][:, :], p_i[:, :]).then_inc(chain, 1)

            def body(k, live):
                if live(0):
                    s = k.slot(4)
                    dve.wait_ge(projected, k.uses())
                    at_least(dve, xl_stored[s], k.back(4).uses(4, 16))
                    at_least(dve, rest_ready, k.back(4).uses())
                    nc.vector.tensor_tensor(rows[:, s, :, :], proj[:, s, :, :], bc(sb["b_lr"][:, :], 1, NB), ALU.add).then_inc(rows_ready, 1)
                if live(1):
                    g = k.back(1)
                    dve.wait_ge(high_ready, g.uses())
                    at_least(dve, parts_ready, g.back(2).uses())
                    nc.vector.tensor_tensor(rest[:, g.slot(2), :, :], rows[:, g.slot(4), :, D:2 * D], parts[:, g.slot(4), :, 0, :], ALU.subtract).then_inc(rest_ready, 1)
            dve.wait_ge(weights_loaded, 64)
            steps(dve, BATCHES, PN, UN, 1, body)

            dve.wait_ge(consts_loaded, 16 * len(loads))
            ends = lines[:, 1:].rearrange("p (t e) -> p t e", e=P)
            dve.tensor_tensor(rel_lines[:, 0, :, :], ends, bc(group_base[:, :], 2, P), ALU.subtract).then_inc(rel_ready, 1)
            dve.tensor_tensor(rel_lines[:, 1, :, :], ends, ends[:, :, 0:1].broadcast_to([LINES, TL, P]), ALU.subtract).then_inc(rel_ready, 1)
            dve.tensor_tensor(limit_sb[:, :], lines[:, 1:], lines[:, 0:TL * P], ALU.is_equal).then_inc(chain, 1)
            dve.tensor_scalar(dst_tiles[:, :], dst_tiles[:, :], P - 1, None, ALU.bitwise_and)
            dve.tensor_scalar(base_all[:, :], base_all[:, :], P - 1, None, ALU.bitwise_and).then_inc(chain, 1)
            dve.wait_ge(chain, 2)
            dve.tensor_scalar(limit_sb[:, :], limit_sb[:, :], 2 * BIG, -BIG, ALU.mult, ALU.add).then_inc(limits_ready, 1)
            dve.tensor_scalar(sb["tile_block"][:, :], sb["tile_base"][:, :], P.bit_length() - 1, None, ALU.arith_shift_right)
            dve.wait_ge(chain, 3)
            dve.tensor_copy(sb["dst_pos"][:, :], dst_tiles[:, :])
            dve.tensor_scalar(sb["minus_pos"][:, :], dst_tiles[:, :], -1.0, None, ALU.mult)
            dve.tensor_copy(sb["first_pos"][:, :], base_all[0:H, :])
            dve.tensor_scalar(sb["keep"][:, :], base_all[:, :], sb["row"][:, :], None, ALU.is_le)
            dve.tensor_scalar(sb["pass_on"][:, :], base_all[:, :], sb["row"][:, :], None, ALU.is_gt)
            firsts = sb["tile_base"][:, :].rearrange("a (g t) -> a g t", t=TG)[:, :, 0]
            lasts = tile_last[:, :].rearrange("a (g t) -> a g t", t=TG)[:, :, TG - 1]
            dve.tensor_tensor(span[:, :], lasts, firsts, ALU.subtract).then_inc(chain, 1)
            dve.wait_ge(chain, 4)
            dve.reduce_max(widest[:, :], span[:, :], mybir.AxisListType.X).then_inc(chain, 1)
            dve.wait_ge(chain, 5)
            dve.tensor_scalar(sb["narrow"][:, :], widest[:, :], float(NARROW), None, ALU.is_lt)
            dve.tensor_scalar(sb["att_block"][:, :], sb["att_block"][:, :], att_col[:, :], None, ALU.mult)
            dve.wait_ge(later_loaded, 16 * len(later))
            dve.tensor_scalar(sb["W_convA"][:, :], sb["W_convA"][:, :], CONV_SCALE, None, ALU.mult)
            dve.tensor_scalar(sb["W_convB"][0:3 * MUL, :], sb["W_convB"][0:3 * MUL, :], CONV_SCALE, None, ALU.mult)
            dve.tensor_scalar(sb["W_convB"][3 * MUL:P, :], sb["W_convB"][3 * MUL:P, :], CONV_SCALE_B, None, ALU.mult)


def attention(nc, sb, q, out, acc):
    with ExitStack() as ctx:
        def tile(name, shape, dt=F32):
            return ctx.enter_context(nc.sbuf_tensor("attn_" + name, shape, dt))

        def bank(name, shape):
            return ctx.enter_context(nc.psum_tensor("attn_" + name, shape, F32))

        def sem(name):
            return ctx.enter_context(nc.semaphore("attn_" + name))

        NX = 12
        NI = 6
        ND = 4
        NF = 4
        HX = H * OX
        LOGITS, DROPS = 32, 64
        SX = DROPS + H
        idx = [tile(f"idx{b}", [P, TG], I32) for b in range(NI)]
        xl_rows = tile("xl_rows", [P, NX, TG, D])
        attrT = tile("attrT", [P, ND, GE])
        xr_win = tile("xr_win", [P, ND, TG, PARTS, D], BF16)
        rel = tile("rel", [P, ND, GE], BF16)
        limit = tile("limit", [H, ND, GE + 1])
        onehot = tile("onehot", [P, 2, TG, P])
        far = tile("far", [P, TG, P])
        onehotT = tile("onehotT", [P, 2, GE], BF16)
        fifth = tile("fifth", [P, 2, GE])
        leaky = tile("leaky", [P, 2, GE])
        stack = tile("stack", [SX, 2, GE])
        prefix = tile("prefix", [H, 2, GE])
        drop = tile("drop", [H, 2, 1])
        factor = tile("factor", [P, NF, H])
        peaks = tile("peaks", [P, TG, H])
        shift = tile("shift", [P, 2, TG, H])
        msg = tile("msg", [P, 2, TG, H, OX])
        pre_ps = bank("pre_ps", [P, 2, GE])
        logit_ps = bank("logit_ps", [H, 2, GE])
        stackT_ps = bank("stackT_ps", [P, TG, P])
        sums_ps = bank("sums_ps", [P, 2, GE])

        idx_loaded = [sem(f"idx_loaded{b}") for b in range(NI)]
        attr_xr_loaded = [sem(f"attr_xr_loaded{b}") for b in range(ND)]
        rel_loaded = [sem(f"rel_loaded{b}") for b in range(ND)]
        limit_loaded = [sem(f"limit_loaded{b}") for b in range(ND)]
        rows_gathered = [sem(f"rows_gathered{b}") for b in range(NX)]
        pool_turn, zeroed = sem("pool_turn"), sem("zeroed")
        onehot_ready, onehotT_ready = sem("onehot_ready"), sem("onehotT_ready")
        pre_ready, fifth_ready, leaky_ready = sem("pre_ready"), sem("fifth_ready"), sem("leaky_ready")
        logit_ready, logit_copied = sem("logit_ready"), sem("logit_copied")
        prefix_ready, peak_ready, drop_made, drop_ready = sem("prefix_ready"), sem("peak_ready"), sem("drop_made"), sem("drop_ready")
        turned, turn_copied, shift_ready = sem("turned"), sem("turn_copied"), sem("shift_ready")
        far_ready, exp_ready, msg_ready = sem("far_ready"), sem("exp_ready"), sem("msg_ready")
        sums_ready, acc_steps = sem("sums_ready"), sem("acc_steps")
        TAIL = 7
        U = NX
        PEEL = G % U + U
        block = ctx.enter_context(nc.Block())

        @block.sync
        def _(sp):
            def run(wins):
                rows = NARROW * PARTS if wins == 1 else P
                rel_line = q["rel_group"] if wins == 1 else q["rel_tile"]

                def body(k, live):
                    if live(0):
                        b = k.slot(NI)
                        at_least(sp, rows_gathered[k.back(NI).slot(NX)], k.back(NI).uses(NX, 16 * TG))
                        sp.dma_start(idx[b][:, :], q["src_tiles"][:, bass.ds(k.index(TG), TG)]).then_inc(idx_loaded[b], 16)
                    if live(4):
                        early(k.back(4))
                    if live(6):
                        late(k.back(6))

                def early(k):
                    b = k.slot(ND)
                    at_least(sp, pre_ready, k.back(ND).uses())
                    sp.dma_start(rel[0:rows, b, :], rel_line[bass.ds(k.index(GE), GE)].rearrange("(a n) -> a n", a=1)
                                 .partition_broadcast(rows).rearrange("p a n -> p (a n)")).then_inc(rel_loaded[b], 16)
                    sp.dma_start(attrT[:, b, :], q["attrT"][:, bass.ds(k.index(GE), GE)]).then_inc(attr_xr_loaded[b], 16)
                    for w in range(wins):
                        base = sp.value_load(sb["tile_base"][0:1, bass.ds(k.index(TG, w), 1)], min_val=0, max_val=N)
                        if wins == 1:
                            sp.dma_start(xr_win[0:rows, b, 0, 0, :], q["xr_parts"][bass.ds(base, NARROW), :].rearrange("n (c f) -> (n c) f", c=PARTS)).then_inc(attr_xr_loaded[b], 16)
                        else:
                            sp.dma_start(xr_win[:, b, w, :, :], q["xr_parts"][bass.ds(base, rows), :].rearrange("n (c f) -> n c f", c=PARTS)).then_inc(attr_xr_loaded[b], 16)

                def late(k):
                    b = k.slot(ND)
                    at_least(sp, drop_ready, k.back(ND).uses())
                    sp.dma_start(limit[:, b, :], q["limit"][bass.ds(k.index(GE), GE + 1)].rearrange("(a n) -> a n", a=1)
                                 .partition_broadcast(H).rearrange("p a n -> p (a n)")).then_inc(limit_loaded[b], 16)
                steps(sp, G, PEEL, U, 6, body)
            by_width(sp, sb["narrow"], run)

        @block.gpsimd
        def _(pool):
            def body(k, live):
                if not live(0):
                    return
                b, i = k.slot(NX), k.slot(NI)
                pool.wait_ge(idx_loaded[i], k.uses(NI, 16))
                pool.sem_inc(pool_turn, 1)
                if not isinstance(k.i, int) or k.at >= NX:
                    pool.wait_ge(msg_ready, k.back(NX).uses())
                    pool.sem_inc(pool_turn, 1)
                for t in range(TG):
                    pool.indirect_dma_start(xl_rows[:, b, t, :], None, q["xl"][:, :],
                                            bass.IndirectOffsetOnAxis(ap=idx[i][:, t:t + 1], axis=0)
                                            ).then_inc(rows_gathered[b], 16)
            steps(pool, G, PEEL, U, 0, body)

        @block.tensor
        def _(pe):
            ident = sb["ident"]

            def run(wins):
                def body(k, live):
                    if live(3):
                        g = k.back(3)
                        pe.wait_ge(leaky_ready, g.uses())
                        at_least(pe, prefix_ready, g.back(2).uses())
                        nc.tensor.matmul(logit_ps[:, g.slot(2), :], sb["att_block"][:, :], leaky[:, g.slot(2), :], start=True, stop=True).then_inc(logit_ready, 1)
                    if live(1):
                        g = k.back(1)
                        b = g.slot(ND)
                        pe.wait_ge(attr_xr_loaded[b], g.uses(ND, 16 * (1 + wins)))
                        at_least(pe, leaky_ready, g.back(2).uses())
                        nc.tensor.matmul(pre_ps[:, g.slot(2), :], sb["W_e"][:, :], attrT[:, b, :], start=True, stop=False)
                        pe.wait_ge(onehotT_ready, g.uses())
                        if wins == 1:
                            rows = NARROW * PARTS
                            nc.tensor.matmul(pre_ps[:, g.slot(2), :], xr_win[0:rows, b, 0, 0, :], onehotT[0:rows, g.slot(2), :], start=False, stop=False)
                        else:
                            for t in range(TG):
                                cols = slice(t * P, (t + 1) * P)
                                for c in range(PARTS):
                                    nc.tensor.matmul(pre_ps[:, g.slot(2), cols], xr_win[:, b, t, c, :], onehotT[:, g.slot(2), cols], start=False, stop=False)
                        pe.wait_ge(rows_gathered[g.slot(NX)], g.uses(NX, 16 * TG))
                        for t in range(TG):
                            last = nc.tensor.matmul(pre_ps[:, g.slot(2), t * P:(t + 1) * P], xl_rows[:, g.slot(NX), t, :], ident[:, :],
                                                    is_transpose=True, start=False, stop=t == TG - 1)
                        last.then_inc(pre_ready, 1)
                    if live(6):
                        g = k.back(6)
                        pe.wait_ge(msg_ready, g.uses())
                        pe.wait_ge(onehot_ready, g.uses())
                        at_least(pe, acc_steps, g.back(2 if wins == 1 else 1).uses(1, 1 + 2 * wins))
                        for t in range(TG):
                            to = sums_ps[:, g.slot(2), 0:HX] if wins == 1 else sums_ps[:, t // 2, t % 2 * 256:t % 2 * 256 + HX]
                            last = nc.tensor.matmul(to, onehot[:, g.slot(2), t, :], msg[:, g.slot(2), t, :, :].rearrange("p h o -> p (h o)"),
                                                    start=wins > 1 or t == 0, stop=wins > 1 or t == TG - 1)
                        last.then_inc(sums_ready, 1)
                    if live(4):
                        g = k.back(4)
                        pe.wait_ge(drop_ready, g.uses())
                        at_least(pe, shift_ready, g.back(1).uses())
                        for t in range(TG):
                            last = nc.tensor.transpose(stackT_ps[:, t, 0:SX], stack[:, g.slot(2), t * P:(t + 1) * P], ident[0:SX, 0:SX])
                        last.then_inc(turned, 1)
                steps(pe, G, PEEL, U, TAIL, body)
            by_width(pe, sb["narrow"], run)

        @block.scalar
        def _(act):
            def run(wins):
                def body(k, live):
                    if live(3):
                        g = k.back(3)
                        act.wait_ge(logit_ready, g.uses())
                        at_least(act, turned, g.back(2).uses())
                        nc.scalar.activation(stack[LOGITS:LOGITS + H, g.slot(2), :], logit_ps[:, g.slot(2), :], ACT.Copy).then_inc(logit_copied, 1)
                    if live(5):
                        g = k.back(5)
                        at_least(act, onehot_ready, g.back(1).uses())
                        for t in range(TG):
                            nc.scalar.activation(far[:, t, :], sb["iota"][:, :], ACT.Abs, bias=sb["minus_pos"][:, bass.ds(g.index(TG, t), 1)]).then_inc(far_ready, 1)
                        act.wait_ge(far_ready, g.uses(1, TG))
                        at_least(act, sums_ready, g.back(2).uses())
                        nc.scalar.activation(onehot[:, g.slot(2), :, :], far[:, :, :], ACT.Relu, bias=sb["one"][:, :], scale=-1.0).then_inc(onehot_ready, 1)
                    if live(1):
                        g = k.back(1)
                        act.wait_ge(pre_ready, g.uses())
                        at_least(act, leaky_ready, g.back(2).uses())
                        nc.scalar.activation(fifth[:, g.slot(2), :], pre_ps[:, g.slot(2), :], ACT.Copy, scale=0.2).then_inc(fifth_ready, 1)
                    if live(4):
                        g = k.back(4)
                        act.wait_ge(turned, g.uses())
                        at_least(act, shift_ready, g.back(1).uses())
                        nc.scalar.activation(peaks[:, :, :], stackT_ps[:, :, 0:H], ACT.Copy).then_inc(turn_copied, 1)
                        at_least(act, acc_steps, g.back(NF).uses(1, 1 + 2 * wins))
                        nc.scalar.activation(factor[:, g.slot(NF), :], stackT_ps[:, 0, DROPS:SX], ACT.Exp).then_inc(turn_copied, 1)
                    if live(4):
                        g = k.back(4)
                        act.wait_ge(shift_ready, g.uses())
                        at_least(act, sums_ready, g.back(2).uses())
                        nc.scalar.activation(msg[:, g.slot(2), :, :, O], shift[:, g.slot(2), :, :], ACT.Exp).then_inc(exp_ready, 1)
                steps(act, G, PEEL, U, TAIL, body)
            by_width(act, sb["narrow"], run)

        @block.vector
        def _(dve):
            dve.memset(acc[:, :, :, :], 0.0).then_inc(zeroed, 1)
            dve.memset(stack[:, :, :], 0.0).then_inc(zeroed, 1)
            dve.memset(prefix[:, 1, :], -BIG).then_inc(zeroed, 1)
            dve.wait_ge(zeroed, 3)

            def run(wins):
                step_count = 1 + 2 * wins
                rows, row = (NARROW * PARTS, sb["window_row"]) if wins == 1 else (P, sb["row"])

                def body(k, live):
                    if live(0):
                        dve.wait_ge(rel_loaded[k.slot(ND)], k.uses(ND, 16))
                        at_least(dve, pre_ready, k.back(2).uses())
                        nc.vector.tensor_scalar(onehotT[0:rows, k.slot(2), :], rel[0:rows, k.slot(ND), :], row[0:rows, :], None, ALU.is_equal).then_inc(onehotT_ready, 1)

                    g, n = k.back(4), k.back(7)
                    b, s, before = g.slot(ND), g.slot(2), g.back(1).slot(2)
                    first = n.index(step_count)

                    def add(w, part):
                        to = acc[:, bass.ds(block_of[w] + part, 1), :, :].rearrange("p b h o -> p (b h o)")
                        sums = sums_ps[:, n.slot(2), 0:HX] if wins == 1 else sums_ps[:, w // 2, w % 2 * 256:w % 2 * 256 + HX]
                        if part == 0:
                            dve.wait_ge(acc_steps, first + (1 + 2 * w))
                        nc.vector.scalar_tensor_tensor(out=to, in0=sums, scalar=sb["pass_on" if part else "keep"][:, bass.ds(n.index(TG, w), 1)], in1=to,
                                                       op0=ALU.mult, op1=ALU.add).then_inc(acc_steps, 1)

                    if live(4):
                        dve.wait_ge(limit_loaded[b], g.uses(ND, 16))
                        dve.wait_ge(logit_copied, g.uses())
                        at_least(dve, drop_made, g.back(1).uses())
                        nc.vector.tensor_tensor_scan(prefix[:, s, :], limit[:, b, 0:GE], logit_ps[:, g.slot(2), :],
                                                     prefix[:, before, GE - 1:GE], ALU.min, ALU.max).then_inc(prefix_ready, 1)
                    if live(7):
                        block_of = [dve.value_load(sb["tile_block"][0:1, bass.ds(n.index(TG, w), 1)], min_val=0, max_val=BLOCKS - 2) for w in range(wins)]
                        dve.wait_ge(turn_copied, n.uses(1, 2))
                        at_least(dve, acc_steps, first)
                        old = acc[:, bass.ds(block_of[0], 1), :, :].rearrange("p b h o -> p (b h) o")
                        nc.vector.tensor_tensor(old, old, bc(factor[:, n.slot(NF), :], 2, OX), ALU.mult).then_inc(acc_steps, 1)
                    if live(4):
                        dve.wait_ge(prefix_ready, g.uses())
                        at_least(dve, turned, g.back(2).uses())
                        nc.vector.tensor_tensor_scan(stack[0:H, s, ::-1], limit[:, b, GE:0:-1], prefix[:, s, ::-1],
                                                     -BIG, ALU.min, ALU.max).then_inc(peak_ready, 1)
                    if live(7):
                        dve.wait_ge(sums_ready, n.uses())
                        add(0, 0)
                    if live(4):
                        dve.wait_ge(peak_ready, g.uses())
                        nc.vector.tensor_scalar(drop[:, s, :], prefix[:, before, GE - 1:GE], stack[0:H, s, 0:1], 0.0,
                                                ALU.subtract, ALU.min).then_inc(drop_made, 1)
                    if live(7):
                        add(0, 1)
                        for w in range(1, wins):
                            add(w, 0)
                            add(w, 1)
                    if live(4):
                        dve.wait_ge(drop_made, g.uses())
                        nc.vector.tensor_scalar(stack[DROPS:SX, s, 0:P], sb["iota"][0:H, :], sb["first_pos"][:, bass.ds(g.index(TG), 1)], drop[:, s, :],
                                                ALU.is_equal, ALU.mult).then_inc(drop_ready, 1)
                    if live(5):
                        m_of = k.back(5)
                        dve.wait_ge(exp_ready, m_of.uses())
                        m = msg[:, m_of.slot(2), :, :, :].rearrange("p t h o -> p (t h) o")
                        nc.vector.tensor_tensor(m[:, :, 0:O], xl_rows[:, m_of.slot(NX), :, :].rearrange("p t (h o) -> p (t h) o", o=O),
                                                m[:, :, O:OX].broadcast_to([P, TG * H, O]), ALU.mult).then_inc(msg_ready, 1)
                    if live(1):
                        z = k.back(1)
                        dve.wait_ge(fifth_ready, z.uses())
                        at_least(dve, logit_ready, z.back(2).uses())
                        nc.vector.tensor_tensor(leaky[:, z.slot(2), :], pre_ps[:, z.slot(2), :], fifth[:, z.slot(2), :], ALU.max).then_inc(leaky_ready, 1)
                    if live(4):
                        dve.wait_ge(turn_copied, g.uses(1, 2))
                        at_least(dve, exp_ready, g.back(2).uses())
                        nc.vector.tensor_tensor(shift[:, g.slot(2), :, :], stackT_ps[:, :, LOGITS:LOGITS + H], peaks[:, :, :],
                                                ALU.subtract).then_inc(shift_ready, 1)
                steps(dve, G, PEEL, U, TAIL, body)
            by_width(dve, sb["narrow"], run)


def update_nodes(nc, sb, q, out, acc):
    with ExitStack() as ctx:
        def tile(name, shape, dt=F32):
            return ctx.enter_context(nc.sbuf_tensor("upd_" + name, shape, dt))

        def bank(name, shape):
            return ctx.enter_context(nc.psum_tensor("upd_" + name, shape, F32))

        def sem(name):
            return ctx.enter_context(nc.semaphore("upd_" + name))

        BN = NB * P
        x_rows = tile("x_rows", [P, 4, NB, D])
        x_bias = tile("x_bias", [P, 2, NB, D])
        h_bias = tile("h_bias", [P, 2, NB, D])
        shift = tile("shift", [P, D])
        y = tile("y", [P, NB, D])
        h = tile("h", [P, 2, NB, D])
        hT = tile("hT", [P, BN])
        hidden = tile("hidden", [P, FC, BN])
        v = tile("v", [P, 2, NB, D])
        x2 = tile("x2", [P, 2, NB, D])
        x2T = tile("x2T", [P, BN])
        feat = tile("feat", [P, 2, NB, D])
        den = tile("den", [P, 2, BATCHES * NB, H])
        hT_ps = bank("hT_ps", [P, BN])
        x2T_ps = bank("x2T_ps", [P, BN])
        hidden_ps = bank("hidden_ps", [P, 2, BN])
        ffn_ps = bank("ffn_ps", [P, NB, D])
        table_ps = bank("table_ps", [P, NB, 2 * D])
        x_loaded = [sem(f"x_loaded{b}") for b in range(4)]
        feat_stored = [sem(f"feat_stored{b}") for b in range(2)]
        x_bias_ready, x_be2_ready, h_bias_ready, h_ready = sem("x_bias_ready"), sem("x_be2_ready"), sem("h_bias_ready"), sem("h_ready")
        h_turned, hT_ready, x2_turned, x2T_ready = sem("h_turned"), sem("hT_ready"), sem("x2_turned"), sem("x2T_ready")
        hidden_ready, gelu_ready, ffn_ready, x2_ready = sem("hidden_ready"), sem("gelu_ready"), sem("ffn_ready"), sem("x2_ready")
        table_ready, feat_ready, self_ready = sem("table_ready"), sem("feat_ready"), sem("self_ready")
        resid = sb["xT"][:, :].rearrange("p (t f) -> p t f", f=D)
        h_links, v_links, den_links, h_scaled, shift_ready = sem("h_links"), sem("v_links"), sem("den_links"), sem("h_scaled"), sem("shift_ready")
        H_LINKS, V_LINKS = 4, 8

        def node_row(name):
            return sb["node_rows"][:, NODE_ROWS.index(name) * D:(NODE_ROWS.index(name) + 1) * D]

        V_SUMMED, V_X_ADDED = 1, 6
        aggregate_turn = sem("aggregate_turn")

        class Norm:

            def __init__(self, name):
                self.stats, self.moments = tile(name + "_stats", [P, NB, 6]), tile(name + "_moments", [P, NB, 2])
                self.spread, self.rstd = tile(name + "_spread", [P, NB]), tile(name + "_rstd", [P, NB])
                self.spread_ready, self.rstd_ready = sem(name + "_spread_ready"), sem(name + "_rstd_ready")

        norm_h, norm_v, norm_x2 = Norm("norm_h"), Norm("norm_v"), Norm("norm_x2")
        LAGS = 5
        UN = 4
        PN = BATCHES % UN + UN
        assert PN >= LAGS
        block = ctx.enter_context(nc.Block())

        def nodes(table, k):
            return q[table][bass.ds(k.index(BN), BN), :].rearrange("(t p) f -> p t f", p=P)

        @block.sync
        def _(sp):
            def body(k, live):
                if live(0):
                    at_least(sp, v_links, k.back(4).index(V_LINKS, V_X_ADDED))
                    sp.dma_start(x_rows[:, k.slot(4), :, :], nodes("x_pad", k)).then_inc(x_loaded[k.slot(4)], 16)
                if live(5):
                    g = k.back(5)
                    sp.wait_ge(feat_ready, g.uses())
                    sp.dma_start(nodes("feat", g), feat[:, g.slot(2), :, :]).then_inc(feat_stored[g.slot(2)], 16)
            steps(sp, BATCHES, PN, UN, LAGS, body)
            for b in range(2):
                sp.wait_ge(feat_stored[b], Step(BATCHES - 2 + (BATCHES - b) % 2).uses(2, 16))

        @block.gpsimd
        def _(pool):
            nc.gpsimd.tensor_tensor(shift[:, :], node_row("be1"), node_row("b2"), ALU.add).then_inc(shift_ready, 1)
            pool.wait_ge(shift_ready, 1)

            def invert(norm, g):
                pool.wait_ge(norm.spread_ready, g.uses())
                nc.gpsimd.tensor_tensor(norm.rstd[:, :], norm.spread[:, :], sb["minus_half"][:, :], ALU.pow).then_inc(norm.rstd_ready, 1)

            def body(k, live):
                if live(3):
                    invert(norm_v, k.back(3))
                if live(1):
                    invert(norm_h, k.back(1))
                if live(1):
                    g = k.back(1)
                    pool.wait_ge(h_ready, g.uses())
                    at_least(pool, v_links, g.back(2).index(V_LINKS, V_SUMMED))
                    to = h_bias[:, g.slot(2), :, :]
                    nc.gpsimd.tensor_tensor(to, h[:, g.slot(2), :, :], bc(node_row("g1"), 1, NB), ALU.mult).then_inc(h_scaled, 1)
                    pool.wait_ge(h_scaled, g.uses())
                    nc.gpsimd.tensor_tensor(to, to, bc(shift[:, :], 1, NB), ALU.add).then_inc(h_bias_ready, 1)
                if live(0):
                    rows = x_rows[:, k.slot(4), :, :]
                    pool.wait_ge(x_loaded[k.slot(4)], k.uses(4, 16))
                    at_least(pool, h_ready, k.back(2).uses())
                    nc.gpsimd.tensor_tensor(x_bias[:, k.slot(2), :, :], rows, bc(node_row("b_att"), 1, NB), ALU.add).then_inc(x_bias_ready, 1)
                    pool.wait_ge(x_bias_ready, k.uses())
                    nc.gpsimd.tensor_tensor(rows, rows, bc(node_row("be2"), 1, NB), ALU.add).then_inc(x_be2_ready, 1)
                if live(3):
                    invert(norm_x2, k.back(3))
            steps(pool, BATCHES, PN, UN, LAGS, body)

        @block.tensor
        def _(pe):
            ident = sb["ident"]

            def body(k, live):
                g, z = k.back(1), k.back(3)
                if live(1):
                    pe.wait_ge(hT_ready, g.uses())
                    for c in range(FC):
                        at_least(pe, gelu_ready, g.index(FC, c - 1))
                        nc.tensor.matmul(hidden_ps[:, c % 2, :], sb["W1"][:, c * P:(c + 1) * P], hT[:, :], start=True, stop=True).then_inc(hidden_ready, 1)
                if live(3):
                    pe.wait_ge(x2_ready, z.uses())
                    at_least(pe, x2T_ready, z.back(1).uses())
                    for t in range(NB):
                        last = nc.tensor.transpose(x2T_ps[:, t * P:(t + 1) * P], x2[:, z.slot(2), t, :], ident[:, :])
                    last.then_inc(x2_turned, 1)
                if live(1):
                    pe.wait_ge(gelu_ready, g.uses(1, FC))
                    at_least(pe, v_links, g.back(1).index(V_LINKS, V_SUMMED))
                    for t in range(NB):
                        for c in range(FC):
                            last = nc.tensor.matmul(ffn_ps[:, t, :], hidden[:, c, t * P:(t + 1) * P], sb["W2"][:, c, :], start=c == 0, stop=c == FC - 1)
                    last.then_inc(ffn_ready, 1)
                if live(0):
                    pe.wait_ge(h_ready, k.uses())
                    at_least(pe, hT_ready, k.back(1).uses())
                    for t in range(NB):
                        last = nc.tensor.transpose(hT_ps[:, t * P:(t + 1) * P], h[:, k.slot(2), t, :], ident[:, :])
                    last.then_inc(h_turned, 1)
                if live(3):
                    pe.wait_ge(x2T_ready, z.uses())
                    at_least(pe, self_ready, z.back(1).uses())
                    for t in range(NB):
                        last = nc.tensor.matmul(table_ps[:, t, :], x2T[:, t * P:(t + 1) * P], sb["W_feat"][:, :], start=True, stop=True)
                    last.then_inc(table_ready, 1)
            steps(pe, BATCHES, PN, UN, LAGS, body)

        @block.scalar
        def _(act):
            def body(k, live):
                if live(1):
                    g = k.back(1)
                    at_least(act, ffn_ready, g.back(1).uses())
                    for c in range(FC):
                        act.wait_ge(hidden_ready, g.index(FC, c + 1))
                        nc.scalar.activation(hidden[:, c, :], hidden_ps[:, c % 2, :], ACT.Gelu, bias=sb["b1"][:, c:c + 1]).then_inc(gelu_ready, 1)
                if live(3):
                    g = k.back(3)
                    act.wait_ge(x2_turned, g.uses())
                    at_least(act, table_ready, g.back(1).uses())
                    nc.scalar.activation(x2T[:, :], x2T_ps[:, :], ACT.Copy).then_inc(x2T_ready, 1)
                if live(0):
                    act.wait_ge(h_turned, k.uses())
                    at_least(act, hidden_ready, k.index(FC))
                    nc.scalar.activation(hT[:, :], hT_ps[:, :], ACT.Identity, scale=sb["norm_columns"][:, 0:1], bias=sb["norm_columns"][:, 1:2]).then_inc(hT_ready, 1)
                if live(3):
                    g = k.back(3)
                    act.wait_ge(table_ready, g.uses())
                    at_least(act, feat_stored[g.slot(2)], g.back(2).uses(2, 16))
                    nc.scalar.activation(feat[:, g.slot(2), :, :], table_ps[:, :, 0:D], ACT.Copy, scale=FEAT_SCALE).then_inc(feat_ready, 1)
            steps(act, BATCHES, PN, UN, LAGS, body)

        @block.vector
        def _(dve):
            class Chain:

                def __init__(self, links, start):
                    self.links, self.start, self.made = links, start, 0

                def link(self, ins):
                    ins.then_inc(self.links, 1)
                    self.made += 1

                def wait(self):
                    at_least(dve, self.links, self.start + self.made if self.made else self.start)

            def measure(chain, norm, of):
                chain.wait()
                for t in range(NB):
                    last = nc.vector.bn_stats(norm.stats[:, t, :], of[:, t, :])
                chain.link(last)

            def aggregate(chain, norm):
                chain.wait()
                dve.sem_inc(aggregate_turn, 1)
                for t in range(NB):
                    last = nc.vector.bn_aggr(norm.moments[:, t, :], norm.stats[:, t, :])
                chain.link(last)

            def spread(chain, norm):
                chain.wait()
                nc.vector.tensor_scalar(norm.spread[:, :], norm.moments[:, :, 1], LN_EPS, None, ALU.add).then_inc(norm.spread_ready, 1)

            def normalise(norm, to, of, g):
                dve.wait_ge(norm.rstd_ready, g.uses())
                for t in range(NB):
                    last = nc.vector.tensor_scalar(to[:, t, :], of[:, t, :], norm.moments[:, t, 0:1], norm.rstd[:, t:t + 1], ALU.subtract, ALU.mult)
                return last

            nc.vector.tensor_scalar(den[:, 0, :, :], acc[:, 0:BATCHES * NB, :, O], 1e-16, None, ALU.add).then_inc(den_links, 1)
            dve.wait_ge(den_links, 1)
            nc.vector.reciprocal(den[:, 1, :, :], den[:, 0, :, :]).then_inc(den_links, 1)
            dve.wait_ge(den_links, 2)

            def body(k, live):
                o, z = k.back(2), k.back(3)
                hs, vs = Chain(h_links, k.index(H_LINKS)), Chain(v_links, o.index(V_LINKS))
                h_k, v_o = h[:, k.slot(2), :, :], v[:, o.slot(2), :, :]
                if live(0):
                    here = acc[:, bass.ds(k.index(NB), NB), :, :].rearrange("p t h o -> p (t h) o")[:, :, 0:O]
                    hs.wait()
                    at_least(dve, h_ready, k.back(1).uses())
                    hs.link(nc.vector.tensor_tensor(y[:, :, :].rearrange("p t (h o) -> p (t h) o", o=O), here,
                                                    bc(den[:, 1, bass.ds(k.index(NB), NB), :].rearrange("p t h -> p (t h)"), 2, O), ALU.mult))
                if live(2):
                    dve.wait_ge(ffn_ready, o.uses())
                    dve.wait_ge(h_bias_ready, o.uses())
                    at_least(dve, x2_ready, o.back(2).uses())
                    vs.wait()
                    vs.link(nc.vector.tensor_tensor(v_o, ffn_ps[:, :, :], h_bias[:, o.slot(2), :, :], ALU.add))
                if live(0):
                    dve.wait_ge(x_bias_ready, k.uses())
                    hs.wait()
                    hs.link(nc.vector.tensor_tensor(y[:, :, :], y[:, :, :], x_bias[:, k.slot(2), :, :], ALU.add))
                if live(2):
                    measure(vs, norm_v, v_o)
                if live(0):
                    measure(hs, norm_h, y)
                if live(2):
                    aggregate(vs, norm_v)
                if live(0):
                    aggregate(hs, norm_h)
                if live(2):
                    spread(vs, norm_v)
                if live(0):
                    spread(hs, norm_h)
                if live(3):
                    at_least(dve, self_ready, z.back(2).uses())
                    normalise(norm_x2, x2[:, z.slot(2), :, :], v[:, z.slot(2), :, :], z).then_inc(x2_ready, 1)
                if live(2):
                    vs.link(normalise(norm_v, v_o, v_o, o))
                if live(0):
                    at_least(dve, h_turned, k.back(2).uses())
                    at_least(dve, h_bias_ready, k.back(2).uses())
                    normalise(norm_h, h_k, y, k).then_inc(h_ready, 1)
                if live(2):
                    vs.wait()
                    vs.link(nc.vector.tensor_tensor(v_o, v_o, bc(node_row("g2"), 1, NB), ALU.mult))
                if live(2):
                    dve.wait_ge(x_be2_ready, o.uses())
                    vs.wait()
                    vs.link(nc.vector.tensor_tensor(v_o, v_o, x_rows[:, o.slot(4), :, :], ALU.add))
                if live(2):
                    measure(vs, norm_x2, v_o)
                if live(4):
                    g = k.back(4)
                    dve.wait_ge(feat_ready, g.uses())
                    nc.vector.scalar_tensor_tensor(out=resid[:, bass.ds(g.index(NB), NB), :], in0=table_ps[:, :, D:2 * D], scalar=SELF_SCALE,
                                                   in1=x2[:, g.slot(2), :, :], op0=ALU.mult, op1=ALU.add).then_inc(self_ready, 1)
                if live(2):
                    at_least(dve, x2_ready, o.back(1).uses())
                    aggregate(vs, norm_x2)
                    spread(vs, norm_x2)
            steps(dve, BATCHES, PN, UN, LAGS, body)


def convolution(nc, sb, q, out, acc):
    with ExitStack() as ctx:
        def tile(name, shape, dt=F32):
            return ctx.enter_context(nc.sbuf_tensor("conv_" + name, shape, dt))

        def bank(name, shape):
            return ctx.enter_context(nc.psum_tensor("conv_" + name, shape, F32))

        def sem(name):
            return ctx.enter_context(nc.semaphore("conv_" + name))

        NX = 8
        ND = 4
        HE = GE // 2
        DX = 2 * D
        idx = [tile(f"idx{b}", [P, TG], I32) for b in range(ND)]
        rows = tile("rows", [P, NX, TG, D])
        radial = tile("radial", [2 * RADIAL, ND, HE])
        edge4 = tile("edge4", [P, T, 4])
        onehot = tile("onehot", [P, 2, TG, P])
        hid1 = tile("hid1", [2 * HID, 2, HE])
        hid2 = tile("hid2", [2 * HID, 2, HE])
        scaled = tile("scaled", [P, 2, TG, 2 * MUL])
        dots = tile("dots", [P, TG, 3, MUL])
        dot = tile("dot", [P, 2, TG, MUL])
        scal = tile("scal", [P, TG, MUL])
        vals = tile("vals", [P, 2, TG, DX])
        hid1_ps = bank("hid1_ps", [2 * HID, GE])
        hid2_ps = bank("hid2_ps", [2 * HID, GE])
        w_ps = bank("w_ps", [P, 2, TG, D])
        sums_ps = bank("sums_ps", [P, 2, GE])
        idx_loaded = [sem(f"idx_loaded{b}") for b in range(ND)]
        radial_loaded = [sem(f"radial_loaded{b}") for b in range(ND)]
        rows_gathered = [sem(f"rows_gathered{b}") for b in range(NX)]
        pool_turn, edge4_loaded, zeroed = sem("pool_turn"), sem("edge4_loaded"), sem("zeroed")
        onehot_ready, hid1_ready, gelu1_ready, hid2_ready, gelu2_ready = sem("onehot_ready"), sem("hid1_ready"), sem("gelu1_ready"), sem("hid2_ready"), sem("gelu2_ready")
        w_ready, scaled_ready, products, vals_ready = sem("w_ready"), sem("scaled_ready"), sem("products"), sem("vals_ready")
        sums_ready, acc_steps = sem("sums_ready"), sem("acc_steps")
        TAIL = 5
        PRODUCTS = 5
        block = ctx.enter_context(nc.Block())

        @block.sync
        def _(sp):
            sp.dma_start(edge4[:, :, :], q["edge4_tiles"].rearrange("p (t c) -> p t c", c=4)).then_inc(edge4_loaded, 16)

            def body(k, live):
                if not live(0):
                    return
                b = k.slot(ND)
                at_least(sp, rows_gathered[k.back(ND).slot(NX)], k.back(ND).uses(NX, 16 * TG))
                sp.dma_start(idx[b][:, :], q["src_tiles"][:, bass.ds(k.index(TG), TG)]).then_inc(idx_loaded[b], 16)
                at_least(sp, hid1_ready, k.back(ND).uses())
                for half in range(2):
                    sp.dma_start(radial[half * RADIAL:(half + 1) * RADIAL, b, :],
                                 q["radialT"][:, bass.ds(k.index(GE, half * HE), HE)]).then_inc(radial_loaded[b], 16)
            steps(sp, G, PEEL, U, 0, body)

        @block.gpsimd
        def _(pool):
            def body(k, live):
                if not live(0):
                    return
                b = k.slot(ND)
                pool.wait_ge(idx_loaded[b], k.uses(ND, 16))
                pool.sem_inc(pool_turn, 1)
                if not isinstance(k.i, int) or k.at >= NX:
                    pool.wait_ge(vals_ready, k.back(NX).uses())
                    pool.sem_inc(pool_turn, 1)
                for t in range(TG):
                    pool.indirect_dma_start(rows[:, k.slot(NX), t, :], None, q["feat"][:, :],
                                            bass.IndirectOffsetOnAxis(ap=idx[b][:, t:t + 1], axis=0)
                                            ).then_inc(rows_gathered[k.slot(NX)], 16)
            steps(pool, G, PEEL, U, 0, body)

        @block.tensor
        def _(pe):
            def run(wins):
                def body(k, live):
                    if live(4):
                        g = k.back(4)
                        pe.wait_ge(vals_ready, g.uses())
                        pe.wait_ge(onehot_ready, g.uses())
                        at_least(pe, acc_steps, g.back(2 if wins == 1 else 1).uses(1, 2 * wins))
                        for t in range(TG):
                            to = sums_ps[:, g.slot(2), 0:DX] if wins == 1 else sums_ps[:, t // 2, t % 2 * DX:(t % 2 + 1) * DX]
                            last = nc.tensor.matmul(to, onehot[:, g.slot(2), t, :], vals[:, g.slot(2), t, :], start=wins > 1 or t == 0, stop=wins > 1 or t == TG - 1)
                        last.then_inc(sums_ready, 1)
                    if live(2):
                        g = k.back(2)
                        pe.wait_ge(gelu2_ready, g.uses())
                        at_least(pe, vals_ready, g.back(2).uses())
                        for c in range(2):
                            last = nc.tensor.matmul(w_ps[:, g.slot(2), c:TG:2, :], hid2[:, g.slot(2), c * P:(c + 1) * P], sb["Wp"][:, :, :], start=True, stop=True)
                        last.then_inc(w_ready, 1)
                    if live(1):
                        g = k.back(1)
                        pe.wait_ge(gelu1_ready, g.uses())
                        at_least(pe, gelu2_ready, g.back(1).uses())
                        nc.tensor.matmul(hid2_ps[:, 0:HE], sb["mlp2"][:, :], hid1[:, g.slot(2), :], start=True, stop=True).then_inc(hid2_ready, 1)
                    if live(0):
                        pe.wait_ge(radial_loaded[k.slot(ND)], k.uses(ND, 32))
                        at_least(pe, gelu1_ready, k.back(1).uses())
                        nc.tensor.matmul(hid1_ps[:, 0:HE], sb["mlp1"][:, :], radial[:, k.slot(ND), :], start=True, stop=True).then_inc(hid1_ready, 1)
                steps(pe, G, PEEL, U, TAIL, body)
            by_width(pe, sb["narrow"], run)

        @block.scalar
        def _(act):
            act.wait_ge(edge4_loaded, 16)

            def body(k, live):
                if live(2):
                    g = k.back(2)
                    act.wait_ge(w_ready, g.uses())
                    at_least(act, vals_ready, g.back(2).uses())
                    for t in range(TG):
                        nc.scalar.activation(scaled[:, g.slot(2), t, :], w_ps[:, g.slot(2), t, 0:2 * MUL], ACT.Copy,
                                             scale=edge4[:, bass.ds(g.index(TG, t), 1), 0:1].rearrange("p t c -> p (t c)")).then_inc(scaled_ready, 1)
                if live(1):
                    g = k.back(1)
                    act.wait_ge(hid2_ready, g.uses())
                    at_least(act, w_ready, g.back(2).uses())
                    nc.scalar.activation(hid2[:, g.slot(2), :], hid2_ps[:, 0:HE], ACT.Gelu_apprx_tanh, scale=1.0 / float(np.sqrt(HID))).then_inc(gelu2_ready, 1)
                if live(0):
                    act.wait_ge(hid1_ready, k.uses())
                    at_least(act, hid2_ready, k.back(2).uses())
                    nc.scalar.activation(hid1[:, k.slot(2), :], hid1_ps[:, 0:HE], ACT.Gelu_apprx_tanh, scale=1.0 / float(np.sqrt(RADIAL))).then_inc(gelu1_ready, 1)
            steps(act, G, PEEL, U, TAIL, body)

        @block.vector
        def _(dve):
            dve.memset(acc[:, :, :], 0.0).then_inc(zeroed, 1)
            dve.wait_ge(zeroed, 1)
            dve.wait_ge(edge4_loaded, 16)

            def run(wins):
                def body(k, live):
                    if live(3):
                        g = k.back(3)
                        at_least(dve, sums_ready, g.back(2).uses())
                        nc.vector.tensor_tensor(onehot[:, g.slot(2), :, :], bc(sb["iota"][:, :], 1, TG),
                                                bc(sb["dst_pos"][:, bass.ds(g.index(TG), TG)], 2, P), ALU.is_equal).then_inc(onehot_ready, 1)
                    if live(5):
                        g = k.back(5)
                        first = g.index(2 * wins)
                        for w in range(wins):
                            at = dve.value_load(sb["tile_block"][0:1, bass.ds(g.index(TG, w), 1)], min_val=0, max_val=BLOCKS - 2)
                            here, beyond = acc[:, bass.ds(at, 1), :].rearrange("p b f -> p (b f)"), acc[:, bass.ds(at + 1, 1), :].rearrange("p b f -> p (b f)")
                            sums = sums_ps[:, g.slot(2), 0:DX] if wins == 1 else sums_ps[:, w // 2, w % 2 * DX:(w % 2 + 1) * DX]
                            tile_at = bass.ds(g.index(TG, w), 1)
                            if w == 0:
                                dve.wait_ge(sums_ready, g.uses())
                            at_least(dve, acc_steps, first + 2 * w if w else first)
                            nc.vector.scalar_tensor_tensor(out=here, in0=sums, scalar=sb["keep"][:, tile_at], in1=here,
                                                           op0=ALU.mult, op1=ALU.add).then_inc(acc_steps, 1)
                            nc.vector.scalar_tensor_tensor(out=beyond, in0=sums, scalar=sb["pass_on"][:, tile_at], in1=beyond,
                                                           op0=ALU.mult, op1=ALU.add).then_inc(acc_steps, 1)
                    if live(3):
                        g = k.back(3)
                        s = g.slot(2)
                        r = rows[:, g.slot(NX), :, :]
                        e0 = r[:, :, 0:MUL]
                        e1 = r[:, :, MUL:D].rearrange("p t (c w) -> p t c w", c=3)
                        a1 = bc(edge4[:, bass.ds(g.index(TG), TG), 1:4], 3, MUL)
                        to, w = vals[:, s, :, :], w_ps[:, s, :, :]
                        at_least(dve, vals_ready, g.back(1).uses())
                        dve.wait_ge(rows_gathered[g.slot(NX)], g.uses(NX, 16 * TG))
                        nc.vector.tensor_tensor(dots[:, :, :, :], e1, a1, ALU.mult).then_inc(products, 1)
                        dve.wait_ge(scaled_ready, g.uses(1, TG))
                        nc.vector.tensor_tensor(scal[:, :, :], w[:, :, 2 * MUL:3 * MUL], e0, ALU.mult).then_inc(products, 1)
                        dve.wait_ge(products, g.index(PRODUCTS, 1))
                        nc.vector.tensor_tensor(dot[:, 0, :, :], dots[:, :, 0, :], dots[:, :, 1, :], ALU.add).then_inc(products, 1)
                        nc.vector.tensor_tensor(to[:, :, 0:MUL], scaled[:, s, :, 0:MUL], e0, ALU.mult)
                        dve.wait_ge(products, g.index(PRODUCTS, 3))
                        nc.vector.tensor_tensor(dot[:, 1, :, :], dot[:, 0, :, :], dots[:, :, 2, :], ALU.add).then_inc(products, 1)
                        nc.vector.tensor_tensor(to[:, :, MUL:D].rearrange("p t (c w) -> p t c w", c=3), e1, bc(scaled[:, s, :, MUL:2 * MUL], 2, 3), ALU.mult)
                        nc.vector.tensor_tensor(to[:, :, D:D + V3].rearrange("p t (c w) -> p t c w", c=3), bc(scal[:, :, :], 2, 3), a1, ALU.mult).then_inc(products, 1)
                        dve.wait_ge(products, g.index(PRODUCTS, 4))
                        nc.vector.tensor_tensor(to[:, :, D + V3:DX], dot[:, 1, :, :], w[:, :, 3 * MUL:4 * MUL], ALU.mult).then_inc(vals_ready, 1)
                steps(dve, G, PEEL, U, TAIL, body)
            by_width(dve, sb["narrow"], run)


def finish_nodes(nc, sb, q, out, acc):
    with ExitStack() as ctx:
        def tile(name, shape, dt=F32):
            return ctx.enter_context(nc.sbuf_tensor("fin_" + name, shape, dt))

        def bank(name, shape):
            return ctx.enter_context(nc.psum_tensor("fin_" + name, shape, F32))

        def sem(name):
            return ctx.enter_context(nc.semaphore("fin_" + name))

        FULL = N // (NB * P)
        REST = N - FULL * NB * P
        USED = FULL + 1
        UN = 2
        PN = USED % UN + 2 * UN
        sumT_ps = bank("sumT_ps", [P, 2, NB, P])
        conv_ps = bank("conv_ps", [P, 2, NB, D])
        sumT = tile("sumT", [P, 2, 2, NB, P])
        v = tile("v", [P, 2, NB, D])
        done = tile("done", [P, 2, NB, D])
        stats = tile("stats", [P, NB, 6])
        moments = tile("moments", [P, NB, 2])
        spread = tile("spread", [P, NB])
        rstd = tile("rstd", [P, NB])
        turned, turn_copied, aggregate_turn = sem("turned"), sem("turn_copied"), sem("aggregate_turn")
        conv_ready, v_ready, spread_ready, rstd_ready = sem("conv_ready"), sem("v_ready"), sem("spread_ready"), sem("rstd_ready")
        done_ready, chain = sem("done_ready"), sem("chain")
        stored = [sem(f"stored{b}") for b in range(2)]
        block = ctx.enter_context(nc.Block())
        resid = sb["xT"][:, :].rearrange("p (t f) -> p t f", f=D)

        @block.tensor
        def _(pe):
            def conv(n):
                pe.wait_ge(turn_copied, n + 1)
                at_least(pe, v_ready, n - 1)
                for t in range(NB):
                    nc.tensor.matmul(conv_ps[:, n % 2, t, :], sumT[:, n % 2, 0, t, :], sb["W_convA"][:, :], start=True, stop=False)
                    last = nc.tensor.matmul(conv_ps[:, n % 2, t, :], sumT[:, n % 2, 1, t, :], sb["W_convB"][:, :], start=False, stop=True)
                last.then_inc(conv_ready, 1)

            for n in range(USED):
                at_least(pe, turn_copied, n)
                for part in range(2):
                    for t in range(NB):
                        last = nc.tensor.transpose(sumT_ps[:, part, t, :], acc[:, n * NB + t, part * D:(part + 1) * D], sb["ident"][:, :])
                last.then_inc(turned, 1)
                if n:
                    conv(n - 1)
            conv(USED - 1)

        @block.scalar
        def _(act):
            def body(k, live):
                if not live(0):
                    return
                act.wait_ge(turned, k.uses())
                at_least(act, conv_ready, k.back(2).uses())
                nc.scalar.activation(sumT[:, k.slot(2), :, :, :], sumT_ps[:, :, :, :], ACT.Copy).then_inc(turn_copied, 1)
            steps(act, USED, PN, UN, 0, body)

        @block.gpsimd
        def _(pool):
            def body(k, live):
                if not live(0):
                    return
                pool.wait_ge(spread_ready, k.uses())
                nc.gpsimd.tensor_tensor(rstd[:, :], spread[:, :], sb["minus_half"][:, :], ALU.pow).then_inc(rstd_ready, 1)
            steps(pool, USED, PN, UN, 0, body)

        @block.vector
        def _(dve):
            def body(k, live):
                if live(0):
                    s = k.slot(2)
                    dve.wait_ge(conv_ready, k.uses())
                    at_least(dve, done_ready, k.back(2).uses())
                    nc.vector.tensor_tensor(v[:, s, :, :], conv_ps[:, s, :, :], resid[:, bass.ds(k.index(NB), NB), :], ALU.add).then_inc(v_ready, 1)
                    at_least(dve, chain, k.index(2))
                    dve.wait_ge(v_ready, k.uses())
                    for t in range(NB):
                        last = nc.vector.bn_stats(stats[:, t, :], v[:, s, t, :])
                    last.then_inc(chain, 1)
                if live(1):
                    g = k.back(1)
                    s = g.slot(2)
                    dve.wait_ge(rstd_ready, g.uses())
                    at_least(dve, stored[s], g.back(2).uses(2, 16))
                    for t in range(NB):
                        last = nc.vector.tensor_scalar(done[:, s, t, :], v[:, s, t, :], moments[:, t, 0:1], rstd[:, t:t + 1], ALU.subtract, ALU.mult)
                    last.then_inc(done_ready, 1)
                if live(0):
                    at_least(dve, done_ready, k.back(1).uses())
                    dve.wait_ge(chain, k.index(2, 1))
                    dve.sem_inc(aggregate_turn, 1)
                    for t in range(NB):
                        last = nc.vector.bn_aggr(moments[:, t, :], stats[:, t, :])
                    last.then_inc(chain, 1)
                    dve.wait_ge(chain, k.index(2, 2))
                    nc.vector.tensor_scalar(spread[:, :], moments[:, :, 1], LN_EPS, None, ALU.add).then_inc(spread_ready, 1)
            steps(dve, USED, PN, UN, 1, body)

        @block.sync
        def _(sp):
            def body(k, live):
                if not live(0):
                    return
                sp.wait_ge(done_ready, k.uses())
                sp.dma_start(out[bass.ds(k.index(NB * P), NB * P), :].rearrange("(t p) f -> p t f", p=P), done[:, k.slot(2), :, :]).then_inc(stored[k.slot(2)], 16)
            steps(sp, FULL, FULL % UN + UN, UN, 0, body)
            sp.wait_ge(done_ready, USED)
            pieces = 0
            for t in range(NB):
                n = min(P, REST - t * P)
                if n > 0:
                    lo = FULL * NB * P + t * P
                    sp.dma_start(out[lo:lo + n, :], done[0:n, FULL % 2, t, :]).then_inc(stored[FULL % 2], 16)
                    pieces += 1
            for b in range(2):
                whole = (FULL - b + 1) // 2 * 16
                sp.wait_ge(stored[b], whole + (pieces * 16 if b == FULL % 2 else 0))


def program(nc, q, out):
    with ExitStack() as ctx:
        def tile(name, shape, dt=F32):
            return ctx.enter_context(nc.sbuf_tensor(name, shape, dt))

        sb = {}
        for name, shape in (("W_lr", [P, 2 * D]), ("W_e", [P, D]), ("W1", [P, FF]), ("W2", [P, FC, D]), ("b1", [P, FC]), ("norm_columns", [P, 2]),
                            ("b_lr", [P, 2 * D]), ("node_rows", [P, len(NODE_ROWS) * D]),
                            ("mlp1", [2 * RADIAL, 2 * HID]), ("mlp2", [2 * HID, 2 * HID]), ("Wp", [2 * HID, 2, D]), ("W_feat", [P, 2 * D]),
                            ("W_convA", [P, D]), ("W_convB", [P, D]), ("ident", [P, P]), ("att_block", [P, H]),
                            ("iota", [P, P]), ("minus_half", [P, NB]), ("one", [P, 1]), ("row", [P, 1]), ("window_row", [P, 1]),
                            ("dst_pos", [P, T]), ("minus_pos", [P, T]), ("first_pos", [H, T]), ("keep", [P, T]), ("pass_on", [P, T]),
                            ("xT", [P, N_PAD])):
            sb[name] = tile("c_" + name, shape)
        for name, n in (("tile_base", T), ("tile_block", T), ("narrow", 1)):
            sb[name] = tile("c_" + name, [1, n], I32)
        set_up(nc, sb, q, out)
        with nc.sbuf_tensor("c_acc_attn", [P, BLOCKS, H, OX], F32) as acc:
            attention(nc, sb, q, out, acc)
            update_nodes(nc, sb, q, out, acc)
        with nc.sbuf_tensor("c_acc_conv", [P, BLOCKS, 2 * D], F32) as acc:
            convolution(nc, sb, q, out, acc)
            finish_nodes(nc, sb, q, out, acc)


def conv_weights(w):
    out = {name: np.zeros(shape, np.float32) for name, shape in (
        ("mlp1", (2 * RADIAL, 2 * HID)), ("mlp2", (2 * HID, 2 * HID)), ("Wp", (2 * HID, 2 * D)),
        ("W_feat", (P, 2 * D)), ("W_convA", (P, D)), ("W_convB", (P, D)))}
    for half in range(2):
        hid = slice(half * HID, (half + 1) * HID)
        out["mlp1"][half * RADIAL:(half + 1) * RADIAL, hid] = w["W_mlp1"]
        out["mlp2"][hid, hid] = w["W_mlp2"]
        out["Wp"][hid, half * D:(half + 1) * D] = np.concatenate([w["Wp_" + path] for path in ("00", "10", "01", "11")], axis=1)
    out["W_feat"][0:MUL, 0:MUL] = w["W1_0e"][:, 0:MUL]
    out["W_feat"][0:MUL, D:D + MUL] = w["W1_0e"][:, MUL:2 * MUL]
    out["W_convA"][0:MUL, 0:MUL] = w["W2_0e"][0:MUL, :]
    out["W_convB"][3 * MUL:4 * MUL, 0:MUL] = w["W2_0e"][MUL:2 * MUL, :]
    for c in range(3):
        lo = MUL * (c + 1)
        out["W_feat"][MUL + c:D:3, lo:lo + MUL] = w["W1_1o"][:, 0:MUL]
        out["W_feat"][MUL + c:D:3, D + MUL + c:2 * D:3] = w["W1_1o"][:, MUL:2 * MUL]
        out["W_convA"][lo:lo + MUL, MUL + c:D:3] = w["W2_1o"][MUL:2 * MUL, :]
        out["W_convB"][MUL * c:MUL * (c + 1), MUL + c:D:3] = w["W2_1o"][0:MUL, :]
    return out


def kernel(**inputs):
    import concourse.bacc as bacc
    from concourse.bass_utils import run_bass_kernel_spmd as run

    a = {k: np.asarray(v) for k, v in inputs.items()}

    def padded(x, n, value=0):
        return np.concatenate([x, np.full((n - x.shape[0],) + x.shape[1:], value, x.dtype)])

    dst = padded(a["dst"], E_PAD, N)
    x_pad = padded(a["x"], N_PAD)
    arrays = {k: np.ascontiguousarray(v) for k, v in a.items()
              if k.startswith("L0") and k[len("L0_gnn_"):] not in NODE_ROWS + ("b1",)}
    arrays |= {
        "x_pad": x_pad,
        "xT": np.ascontiguousarray(x_pad.T),
        "b1_columns": np.ascontiguousarray(a["L0_gnn_b1"].reshape(FC, P).T),
        "norm_columns": np.stack([a["L0_gnn_g1"], a["L0_gnn_be1"]], axis=1),
        "src_tiles": np.ascontiguousarray(padded(a["src"], E_PAD).reshape(T, P).T),
        "dst_tiles": np.ascontiguousarray(dst.reshape(T, P).T),
        "dst_lines": np.stack([np.concatenate([dst[p * TL * P - 1:p * TL * P] if p else np.full((1,), -1, dst.dtype), dst[p * TL * P:(p + 1) * TL * P]])
                               for p in range(LINES)]),
        "attrT": np.ascontiguousarray(padded(a["edge_attr_128"], E_PAD).T),
        "radialT": np.ascontiguousarray(padded(a["edge_attr_8"], E_PAD).T),
        "group_base": np.repeat(dst[::GE], TG).reshape(LINES, TL),
        "node_rows": np.concatenate([a["L0_gnn_" + name] for name in NODE_ROWS]),
        "window_row": np.arange(P, dtype=np.float32)[:, None] // PARTS,
        "edge4_tiles": np.ascontiguousarray(padded(a["edge_attr_4"], E_PAD).reshape(T, P, 4).transpose(1, 0, 2)).reshape(P, T * 4),
    }
    arrays |= conv_weights({k[len("L1_gnn_"):]: v for k, v in a.items() if k.startswith("L1")})
    nc = bacc.Bacc("TRN2", target_bir_lowering=False, num_devices=1)
    q = {k: nc.dram_tensor("in_" + k, v.shape, mybir.dt.from_np(v.dtype), kind="ExternalInput").ap() for k, v in arrays.items()}
    for name, shape in (("xl", (N_PAD, D)), ("feat", (N_PAD, D)), ("limit", (E_PAD + 1,))):
        q[name] = nc.dram_tensor(name, shape, F32).ap()
    for name, shape in (("xr_parts", (N_PAD, PARTS * D)), ("rel_group", (E_PAD,)), ("rel_tile", (E_PAD,))):
        q[name] = nc.dram_tensor(name, shape, BF16).ap()
    out = nc.dram_tensor("out", (N, D), F32, kind="ExternalOutput").ap()
    program(nc, q, out)
    return run(nc, [{"in_" + k: v for k, v in arrays.items()}], core_ids=[0]).results[0]["out"]
```
